# Optimizing a Trainium2 kernel written in Bass

```python
import numpy as np
import jax
import jax.numpy as jnp

def _softmax(x, axis=-1):
    return jax.nn.softmax(x, axis=axis)

def _gelu(x):
    return jax.nn.gelu(x, approximate=True)

def _silu(x):
    return jax.nn.silu(x)

def _sigmoid(x):
    return jax.nn.sigmoid(x)

def _layernorm(x, axis=-1, eps=1e-05):
    m = jnp.mean(x, axis=axis, keepdims=True)
    v = jnp.var(x, axis=axis, keepdims=True)
    return (x - m) / jnp.sqrt(v + eps)

def _scatter_add(tgt, idx, src, axis=0):
    return tgt.at[idx].add(src)

def _segment_sum(src, seg, n):
    return jax.ops.segment_sum(src, seg, n)
kernel_name = 'mk_pixart_resid_d4_seqx_r8_c9d1ff'

def setup_inputs(seed: int=0):
    np.random.seed(seed)
    _w = jnp.asarray

    def _rec_inputs():
        import jax
        import jax.numpy as jnp
        _rk = jax.random.key(seed)
        x = -0.0002928 + 1 * jax.random.normal(jax.random.fold_in(_rk, 1), (2, 512, 128), jnp.float32)
        _lenS = 512 - jax.random.randint(jax.random.fold_in(_rk, 7), (2,), 0, max(1, 512 // 4) + 1, jnp.int32)
        _lenS2 = 77 - jax.random.randint(jax.random.fold_in(_rk, 8), (2,), 0, max(1, 77 // 4) + 1, jnp.int32)
        _ctx_1024P = jax.random.normal(jax.random.fold_in(_rk, 11), (2, 16, 128), jnp.float32)
        _ctx_1024c = jax.random.dirichlet(jax.random.fold_in(_rk, 511), 0.3 * jnp.ones((16,), jnp.float32), (2, 77))
        _ctx_1024t = jnp.einsum('bsk,bkd->bsd', _ctx_1024c, _ctx_1024P)
        _ctx_1024t = _ctx_1024t * jax.lax.rsqrt(jnp.mean(jnp.square(_ctx_1024t)) + 1e-12) * 0.953939
        ctx_1024 = -1.52775e-05 + 0.999936 * (_ctx_1024t + 0.3 * jax.random.normal(jax.random.fold_in(_rk, 611), (2, 77, 128), jnp.float32))
        cond_1024 = -0.00779384 + 0.997222 * jax.random.normal(jax.random.fold_in(_rk, 12), (2, 128), jnp.float32)
        return (x, ctx_1024, cond_1024)
    x, ctx_1024, cond_1024 = _rec_inputs()

    def _L0_xcond_setup():
        import jax, jax.numpy as jnp
        import numpy as np
        B, T, S, H, E = (128, 32, 32, 128, 128)
        key = jax.random.key(seed)
        ks = jax.random.split(key, 8)
        sc = lambda n: 1.0 / np.sqrt(n)
        return dict(dec_seq=jax.random.normal(ks[0], (B, T, E), jnp.float32), enc_hiddens=jax.random.normal(ks[1], (B, S, H), jnp.float32), last_hidden=jax.random.normal(ks[2], (B, H), jnp.float32), W_att=jax.random.normal(ks[3], (2 * H, H), jnp.float32) * sc(2 * H), V_att=jax.random.normal(ks[4], (H, 1), jnp.float32) * sc(H), Wi=jax.random.normal(ks[5], (E + H, 3 * H), jnp.float32) * sc(E + H), Uh=jax.random.normal(ks[6], (H, 3 * H), jnp.float32) * sc(H), b=jnp.zeros((3 * H,), jnp.float32))
    _L0_xcond_all = _L0_xcond_setup()
    _L0_xcond_in = {k: v for k, v in _L0_xcond_all.items() if k in ('W_att', 'V_att', 'Wi', 'Uh', 'b')}
    del _L0_xcond_all

    def _L0_ffn_setup():
        import jax, jax.numpy as jnp
        import numpy as np
        NUM_EXPERTS = 8
        HIDDEN = 128
        FFN = 512
        BATCH = 2
        SEQ = 256
        key = jax.random.key(seed)
        k_x, k_g, k_u, k_d = jax.random.split(key, 4)
        scale_in = 1.0 / np.sqrt(HIDDEN)
        scale_mid = 1.0 / np.sqrt(FFN)
        return {'hidden_states': jax.random.normal(k_x, (BATCH, SEQ, HIDDEN), dtype=jnp.float32), 'Wg': jax.random.normal(k_g, (NUM_EXPERTS, HIDDEN, FFN), dtype=jnp.float32) * scale_in, 'Wu': jax.random.normal(k_u, (NUM_EXPERTS, HIDDEN, FFN), dtype=jnp.float32) * scale_in, 'Wd': jax.random.normal(k_d, (NUM_EXPERTS, FFN, HIDDEN), dtype=jnp.float32) * scale_mid}
    _L0_ffn_all = _L0_ffn_setup()
    _L0_ffn_in = {k: v for k, v in _L0_ffn_all.items() if k in ('Wg', 'Wu', 'Wd')}
    del _L0_ffn_all

    def _L1_xcond_setup():
        import jax, jax.numpy as jnp
        import numpy as np
        import math
        B, S, CTX, D, H, DH = (2, 256, 32, 128, 16, 64)
        INNER = H * DH
        DFF = 4 * D

        def layernorm(x, eps=1e-05):
            m = jnp.mean(x, axis=-1, keepdims=True)
            v = jnp.var(x, axis=-1, keepdims=True)
            return (x - m) * jax.lax.rsqrt(v + eps)

        def adaln(x, t, w, b):
            emb = t @ w + b
            scale, shift = jnp.split(emb, 2, axis=-1)
            return layernorm(x) * (1.0 + scale) + shift

        def mha(xq, ctx, wq, wk, wv, wo, bo):
            b, sq, _ = xq.shape
            sk = ctx.shape[1]
            q = (xq @ wq).reshape(b, sq, H, DH).transpose(0, 2, 1, 3)
            k = (ctx @ wk).reshape(b, sk, H, DH).transpose(0, 2, 1, 3)
            v = (ctx @ wv).reshape(b, sk, H, DH).transpose(0, 2, 1, 3)
            scores = jnp.einsum('bhqd,bhkd->bhqk', q, k) / math.sqrt(DH)
            attn = jax.nn.softmax(scores, axis=-1)
            out = jnp.einsum('bhqk,bhkd->bhqd', attn, v)
            out = out.transpose(0, 2, 1, 3).reshape(b, sq, INNER)
            return out @ wo + bo

        def glu_ff(x, w1, b1, w2, b2):
            u = x @ w1 + b1
            a, gate = jnp.split(u, 2, axis=-1)
            return a * jax.nn.gelu(gate, approximate=False) @ w2 + b2
        key = jax.random.key(seed)
        ks = jax.random.split(key, 24)
        s = 1.0 / math.sqrt(D)

        def n(k, shape, scale=1.0):
            return jax.random.normal(k, shape, dtype=jnp.float32) * scale
        return {'x': n(ks[0], (B, S, D)), 't': n(ks[1], (B, 1, D)), 'context': n(ks[2], (B, CTX, D)), 'attn1_wq': n(ks[3], (D, INNER), s), 'attn1_wk': n(ks[4], (D, INNER), s), 'attn1_wv': n(ks[5], (D, INNER), s), 'attn1_wo': n(ks[6], (INNER, D), s), 'attn1_bo': n(ks[7], (D,), 0.01), 'attn2_wq': n(ks[8], (D, INNER), s), 'attn2_wk': n(ks[9], (D, INNER), s), 'attn2_wv': n(ks[10], (D, INNER), s), 'attn2_wo': n(ks[11], (INNER, D), s), 'attn2_bo': n(ks[12], (D,), 0.01), 'ff_w1': n(ks[13], (D, 2 * DFF), s), 'ff_b1': n(ks[14], (2 * DFF,), 0.01), 'ff_w2': n(ks[15], (DFF, D), 1.0 / math.sqrt(DFF)), 'ff_b2': n(ks[16], (D,), 0.01), 'norm1_w': n(ks[17], (D, 2 * D), s), 'norm1_b': n(ks[18], (2 * D,), 0.01), 'norm2_w': n(ks[19], (D, 2 * D), s), 'norm2_b': n(ks[20], (2 * D,), 0.01), 'norm3_w': n(ks[21], (D, 2 * D), s), 'norm3_b': n(ks[22], (2 * D,), 0.01)}
    _L1_xcond_all = _L1_xcond_setup()
    _L1_xcond_in = {k: v for k, v in _L1_xcond_all.items() if k in ('attn1_wq', 'attn1_wk', 'attn1_wv', 'attn1_wo', 'attn1_bo', 'attn2_wq', 'attn2_wk', 'attn2_wv', 'attn2_wo', 'attn2_bo', 'ff_w1', 'ff_b1', 'ff_w2', 'ff_b2', 'norm1_w', 'norm1_b', 'norm2_w', 'norm2_b', 'norm3_w', 'norm3_b')}
    del _L1_xcond_all

    def _L1_ffn_setup():
        import jax, jax.numpy as jnp
        import numpy as np
        D_MODEL = 128
        EXPANSION = 4
        D_HIDDEN = D_MODEL * EXPANSION
        NUM_STAGES = int(np.log2(D_HIDDEN))

        def butterfly(y, weights, dim):
            lead = y.shape[:-1]
            for stage in range(weights.shape[0]):
                s = 2 ** stage
                nb = dim // (2 * s)
                yr = y.reshape(*lead, nb, 2, s)
                a = yr[..., 0, :]
                b = yr[..., 1, :]
                w = weights[stage].reshape(nb, s, 2, 2)
                na = w[..., 0, 0] * a + w[..., 0, 1] * b
                nb2 = w[..., 1, 0] * a + w[..., 1, 1] * b
                y = jnp.stack([na, nb2], axis=-2).reshape(*lead, dim)
            return y
        key = jax.random.key(seed)
        ks = jax.random.split(key, 6)
        B, S = (4, 256)
        x = jax.random.normal(ks[0], (B, S, D_MODEL), jnp.float32)
        W_exp = jax.random.normal(ks[1], (D_MODEL, D_HIDDEN), jnp.float32) * 0.02
        b_exp = jnp.zeros((D_HIDDEN,), jnp.float32)
        up_weights = jax.random.normal(ks[2], (NUM_STAGES, D_HIDDEN // 2, 2, 2), jnp.float32) * 0.02
        up_bias = jnp.zeros((D_HIDDEN,), jnp.float32)
        down_weights = jax.random.normal(ks[3], (NUM_STAGES, D_HIDDEN // 2, 2, 2), jnp.float32) * 0.02
        W_con = jax.random.normal(ks[4], (D_HIDDEN, D_MODEL), jnp.float32) * 0.02
        b_con = jnp.zeros((D_MODEL,), jnp.float32)
        down_bias = jnp.zeros((D_MODEL,), jnp.float32)
        return dict(x=x, W_exp=W_exp, b_exp=b_exp, up_weights=up_weights, up_bias=up_bias, down_weights=down_weights, W_con=W_con, b_con=b_con, down_bias=down_bias)
    _L1_ffn_all = _L1_ffn_setup()
    _L1_ffn_in = {k: v for k, v in _L1_ffn_all.items() if k in ('W_exp', 'b_exp', 'up_weights', 'up_bias', 'down_weights', 'W_con', 'b_con', 'down_bias')}
    del _L1_ffn_all

    def _L2_xcond_setup():
        import jax, jax.numpy as jnp
        import numpy as np
        B, N, K, D, T = (16, 512, 16, 128, 3)
        EPS_ATTN = 1e-08
        LN_EPS = 1e-05

        def _ln(x, g, b):
            mu = jnp.mean(x, axis=-1, keepdims=True)
            var = jnp.mean(jnp.square(x - mu), axis=-1, keepdims=True)
            return (x - mu) * jax.lax.rsqrt(var + LN_EPS) * g + b
        key = jax.random.key(seed)
        ks = jax.random.split(key, 16)
        w = lambda k, i, o: jax.random.normal(k, (i, o), jnp.float32) * 0.02
        inp = {'x_cls': jax.random.normal(ks[0], (B, D), jnp.float32), 'x': jax.random.normal(ks[1], (B, N, D), jnp.float32), 'noise': jax.random.normal(ks[2], (B, K, D), jnp.float32), 'q_mu': jax.random.normal(ks[3], (1, 1, D), jnp.float32), 'q_logsig': jax.random.normal(ks[4], (1, 1, D), jnp.float32) * 0.02, 'lnkv_g': jnp.ones((D,), jnp.float32), 'lnkv_b': jnp.zeros((D,), jnp.float32), 'lnq_g': jnp.ones((D,), jnp.float32), 'lnq_b': jnp.zeros((D,), jnp.float32), 'lnm_g': jnp.ones((D,), jnp.float32), 'lnm_b': jnp.zeros((D,), jnp.float32), 'lnp_g': jnp.ones((D,), jnp.float32), 'lnp_b': jnp.zeros((D,), jnp.float32), 'wk': w(ks[5], D, D), 'bk': jnp.zeros((D,), jnp.float32), 'wv': w(ks[6], D, D), 'bv': jnp.zeros((D,), jnp.float32), 'wq': w(ks[7], D, D), 'bq': jnp.zeros((D,), jnp.float32), 'wu': w(ks[8], D, D), 'bu': jnp.zeros((D,), jnp.float32), 'w1': w(ks[9], D, D), 'b1': jnp.zeros((D,), jnp.float32), 'w2': w(ks[10], D, D), 'b2': jnp.zeros((D,), jnp.float32)}
        return inp
    _L2_xcond_all = _L2_xcond_setup()
    _L2_xcond_in = {k: v for k, v in _L2_xcond_all.items() if k in ('q_mu', 'q_logsig', 'lnkv_g', 'lnkv_b', 'lnq_g', 'lnq_b', 'lnm_g', 'lnm_b', 'lnp_g', 'lnp_b', 'wk', 'bk', 'wv', 'bv', 'wq', 'bq', 'wu', 'bu', 'w1', 'b1', 'w2', 'b2')}
    del _L2_xcond_all

    def _L2_ffn_setup():
        import jax, jax.numpy as jnp
        import numpy as np
        B, T, D = (4, 512, 128)
        E = 8
        TOP_K = 2
        FFN = 384
        HALF = FFN // 2

        def _kaiming_uniform(key, shape, fan_in):
            bound = 1.0 / np.sqrt(fan_in)
            return jax.random.uniform(key, shape, jnp.float32, -bound, bound)
        key = jax.random.key(seed)
        ks = jax.random.split(key, 7)
        x = jax.random.normal(ks[0], (B, T, D), jnp.float32)
        gate_w = _kaiming_uniform(ks[1], (E, D), D) * 0.01
        w_up = _kaiming_uniform(ks[2], (E, FFN, D), D)
        w_down = _kaiming_uniform(ks[3], (E, D, HALF), HALF)
        sg_gate = _kaiming_uniform(ks[4], (HALF, D), D)
        sg_up = _kaiming_uniform(ks[5], (HALF, D), D)
        sg_down = _kaiming_uniform(ks[6], (D, HALF), HALF)
        return {'x': x, 'gate_w': gate_w, 'w_up': w_up, 'w_down': w_down, 'sg_gate': sg_gate, 'sg_up': sg_up, 'sg_down': sg_down}
    _L2_ffn_all = _L2_ffn_setup()
    _L2_ffn_in = {k: v for k, v in _L2_ffn_all.items() if k in ('gate_w', 'w_up', 'w_down', 'sg_gate', 'sg_up', 'sg_down')}
    del _L2_ffn_all

    def _L3_xcond_setup():
        import jax, jax.numpy as jnp
        import numpy as np
        DIM = 128
        DIM_HEAD = 64
        HEADS = 16
        INNER = DIM_HEAD * HEADS
        B, N1, N2 = (8, 512, 32)
        EPS = 1e-05

        def layer_norm(x, w, b):
            mu = jnp.mean(x, axis=-1, keepdims=True)
            var = jnp.var(x, axis=-1, keepdims=True)
            return (x - mu) * jax.lax.rsqrt(var + EPS) * w + b
        key = jax.random.key(seed)
        ks = jax.random.split(key, 10)
        return {'x': jax.random.normal(ks[0], (B, N1, DIM), jnp.float32), 'latents': jax.random.normal(ks[1], (B, N2, DIM), jnp.float32), 'shift': jax.random.normal(ks[2], (B, DIM), jnp.float32), 'scale': jax.random.normal(ks[3], (B, DIM), jnp.float32), 'ln1_w': jnp.ones((DIM,), jnp.float32), 'ln1_b': jnp.zeros((DIM,), jnp.float32), 'ln2_w': jnp.ones((DIM,), jnp.float32), 'ln2_b': jnp.zeros((DIM,), jnp.float32), 'Wq': jax.random.normal(ks[4], (INNER, DIM), jnp.float32) * 0.02, 'Wkv': jax.random.normal(ks[5], (2 * INNER, DIM), jnp.float32) * 0.02, 'Wo': jax.random.normal(ks[6], (DIM, INNER), jnp.float32) * 0.02}
    _L3_xcond_all = _L3_xcond_setup()
    _L3_xcond_in = {k: v for k, v in _L3_xcond_all.items() if k in ('ln1_w', 'ln1_b', 'ln2_w', 'ln2_b', 'Wq', 'Wkv', 'Wo')}
    del _L3_xcond_all

    def _L3_ffn_setup():
        import jax, jax.numpy as jnp
        import numpy as np
        N_EXPERTS = 16
        TOP_K = int(N_EXPERTS * 0.2)
        EPS = 1e-12
        key = jax.random.key(seed)
        ks = jax.random.split(key, 6)
        B, T, D, H, E = (4, 128, 128, 256, N_EXPERTS)
        x = jax.random.normal(ks[0], (B, T, D), dtype=jnp.float32)
        gate = jax.random.normal(ks[1], (D, E), dtype=jnp.float32)
        W1 = jax.random.normal(ks[2], (E, D, H), dtype=jnp.float32) * (1.0 / np.sqrt(D))
        b1 = jax.random.normal(ks[3], (E, H), dtype=jnp.float32) * 0.02
        W2 = jax.random.normal(ks[4], (E, H, D), dtype=jnp.float32) * (1.0 / np.sqrt(H))
        b2 = jax.random.normal(ks[5], (E, D), dtype=jnp.float32) * 0.02
        return {'x': x, 'gate': gate, 'W1': W1, 'b1': b1, 'W2': W2, 'b2': b2}
    _L3_ffn_all = _L3_ffn_setup()
    _L3_ffn_in = {k: v for k, v in _L3_ffn_all.items() if k in ('gate', 'W1', 'b1', 'W2', 'b2')}
    del _L3_ffn_all
    return {'x': x, 'ctx_1024': ctx_1024, 'cond_1024': cond_1024, 'L0_xcond_W_att': _L0_xcond_in['W_att'], 'L0_xcond_V_att': _L0_xcond_in['V_att'], 'L0_xcond_Wi': _L0_xcond_in['Wi'], 'L0_xcond_Uh': _L0_xcond_in['Uh'], 'L0_xcond_b': _L0_xcond_in['b'], 'L0_ffn_Wg': _L0_ffn_in['Wg'], 'L0_ffn_Wu': _L0_ffn_in['Wu'], 'L0_ffn_Wd': _L0_ffn_in['Wd'], 'L1_xcond_attn1_wq': _L1_xcond_in['attn1_wq'], 'L1_xcond_attn1_wk': _L1_xcond_in['attn1_wk'], 'L1_xcond_attn1_wv': _L1_xcond_in['attn1_wv'], 'L1_xcond_attn1_wo': _L1_xcond_in['attn1_wo'], 'L1_xcond_attn1_bo': _L1_xcond_in['attn1_bo'], 'L1_xcond_attn2_wq': _L1_xcond_in['attn2_wq'], 'L1_xcond_attn2_wk': _L1_xcond_in['attn2_wk'], 'L1_xcond_attn2_wv': _L1_xcond_in['attn2_wv'], 'L1_xcond_attn2_wo': _L1_xcond_in['attn2_wo'], 'L1_xcond_attn2_bo': _L1_xcond_in['attn2_bo'], 'L1_xcond_ff_w1': _L1_xcond_in['ff_w1'], 'L1_xcond_ff_b1': _L1_xcond_in['ff_b1'], 'L1_xcond_ff_w2': _L1_xcond_in['ff_w2'], 'L1_xcond_ff_b2': _L1_xcond_in['ff_b2'], 'L1_xcond_norm1_w': _L1_xcond_in['norm1_w'], 'L1_xcond_norm1_b': _L1_xcond_in['norm1_b'], 'L1_xcond_norm2_w': _L1_xcond_in['norm2_w'], 'L1_xcond_norm2_b': _L1_xcond_in['norm2_b'], 'L1_xcond_norm3_w': _L1_xcond_in['norm3_w'], 'L1_xcond_norm3_b': _L1_xcond_in['norm3_b'], 'L1_ffn_W_exp': _L1_ffn_in['W_exp'], 'L1_ffn_b_exp': _L1_ffn_in['b_exp'], 'L1_ffn_up_weights': _L1_ffn_in['up_weights'], 'L1_ffn_up_bias': _L1_ffn_in['up_bias'], 'L1_ffn_down_weights': _L1_ffn_in['down_weights'], 'L1_ffn_W_con': _L1_ffn_in['W_con'], 'L1_ffn_b_con': _L1_ffn_in['b_con'], 'L1_ffn_down_bias': _L1_ffn_in['down_bias'], 'L2_xcond_q_mu': _L2_xcond_in['q_mu'], 'L2_xcond_q_logsig': _L2_xcond_in['q_logsig'], 'L2_xcond_lnkv_g': _L2_xcond_in['lnkv_g'], 'L2_xcond_lnkv_b': _L2_xcond_in['lnkv_b'], 'L2_xcond_lnq_g': _L2_xcond_in['lnq_g'], 'L2_xcond_lnq_b': _L2_xcond_in['lnq_b'], 'L2_xcond_lnm_g': _L2_xcond_in['lnm_g'], 'L2_xcond_lnm_b': _L2_xcond_in['lnm_b'], 'L2_xcond_lnp_g': _L2_xcond_in['lnp_g'], 'L2_xcond_lnp_b': _L2_xcond_in['lnp_b'], 'L2_xcond_wk': _L2_xcond_in['wk'], 'L2_xcond_bk': _L2_xcond_in['bk'], 'L2_xcond_wv': _L2_xcond_in['wv'], 'L2_xcond_bv': _L2_xcond_in['bv'], 'L2_xcond_wq': _L2_xcond_in['wq'], 'L2_xcond_bq': _L2_xcond_in['bq'], 'L2_xcond_wu': _L2_xcond_in['wu'], 'L2_xcond_bu': _L2_xcond_in['bu'], 'L2_xcond_w1': _L2_xcond_in['w1'], 'L2_xcond_b1': _L2_xcond_in['b1'], 'L2_xcond_w2': _L2_xcond_in['w2'], 'L2_xcond_b2': _L2_xcond_in['b2'], 'L2_ffn_gate_w': _L2_ffn_in['gate_w'], 'L2_ffn_w_up': _L2_ffn_in['w_up'], 'L2_ffn_w_down': _L2_ffn_in['w_down'], 'L2_ffn_sg_gate': _L2_ffn_in['sg_gate'], 'L2_ffn_sg_up': _L2_ffn_in['sg_up'], 'L2_ffn_sg_down': _L2_ffn_in['sg_down'], 'L3_xcond_ln1_w': _L3_xcond_in['ln1_w'], 'L3_xcond_ln1_b': _L3_xcond_in['ln1_b'], 'L3_xcond_ln2_w': _L3_xcond_in['ln2_w'], 'L3_xcond_ln2_b': _L3_xcond_in['ln2_b'], 'L3_xcond_Wq': _L3_xcond_in['Wq'], 'L3_xcond_Wkv': _L3_xcond_in['Wkv'], 'L3_xcond_Wo': _L3_xcond_in['Wo'], 'L3_ffn_gate': _L3_ffn_in['gate'], 'L3_ffn_W1': _L3_ffn_in['W1'], 'L3_ffn_b1': _L3_ffn_in['b1'], 'L3_ffn_W2': _L3_ffn_in['W2'], 'L3_ffn_b2': _L3_ffn_in['b2']}

def reference(x, ctx_1024, cond_1024, L0_xcond_W_att, L0_xcond_V_att, L0_xcond_Wi, L0_xcond_Uh, L0_xcond_b, L0_ffn_Wg, L0_ffn_Wu, L0_ffn_Wd, L1_xcond_attn1_wq, L1_xcond_attn1_wk, L1_xcond_attn1_wv, L1_xcond_attn1_wo, L1_xcond_attn1_bo, L1_xcond_attn2_wq, L1_xcond_attn2_wk, L1_xcond_attn2_wv, L1_xcond_attn2_wo, L1_xcond_attn2_bo, L1_xcond_ff_w1, L1_xcond_ff_b1, L1_xcond_ff_w2, L1_xcond_ff_b2, L1_xcond_norm1_w, L1_xcond_norm1_b, L1_xcond_norm2_w, L1_xcond_norm2_b, L1_xcond_norm3_w, L1_xcond_norm3_b, L1_ffn_W_exp, L1_ffn_b_exp, L1_ffn_up_weights, L1_ffn_up_bias, L1_ffn_down_weights, L1_ffn_W_con, L1_ffn_b_con, L1_ffn_down_bias, L2_xcond_q_mu, L2_xcond_q_logsig, L2_xcond_lnkv_g, L2_xcond_lnkv_b, L2_xcond_lnq_g, L2_xcond_lnq_b, L2_xcond_lnm_g, L2_xcond_lnm_b, L2_xcond_lnp_g, L2_xcond_lnp_b, L2_xcond_wk, L2_xcond_bk, L2_xcond_wv, L2_xcond_bv, L2_xcond_wq, L2_xcond_bq, L2_xcond_wu, L2_xcond_bu, L2_xcond_w1, L2_xcond_b1, L2_xcond_w2, L2_xcond_b2, L2_ffn_gate_w, L2_ffn_w_up, L2_ffn_w_down, L2_ffn_sg_gate, L2_ffn_sg_up, L2_ffn_sg_down, L3_xcond_ln1_w, L3_xcond_ln1_b, L3_xcond_ln2_w, L3_xcond_ln2_b, L3_xcond_Wq, L3_xcond_Wkv, L3_xcond_Wo, L3_ffn_gate, L3_ffn_W1, L3_ffn_b1, L3_ffn_W2, L3_ffn_b2):
    import jax
    import jax.numpy as jnp

    def _L0_xcond_ref(dec_seq, enc_hiddens, last_hidden, W_att, V_att, Wi, Uh, b):
        import jax, jax.numpy as jnp
        import numpy as np
        B, T, S, H, E = (128, 32, 32, 128, 128)
        Bn, Sn, Hn = enc_hiddens.shape

        def step(h, x_t):
            hid = jnp.broadcast_to(h[:, None, :], (Bn, Sn, Hn))
            combined = jnp.concatenate([hid, enc_hiddens], axis=2)
            score = jnp.tanh(jnp.einsum('bsk,kh->bsh', combined, W_att))
            score = jnp.einsum('bsh,h->bs', score, V_att[:, 0])
            attn = jax.nn.softmax(score, axis=-1)
            context = jnp.einsum('bs,bsh->bh', attn, enc_hiddens)
            inp = jnp.concatenate([x_t, context], axis=1)
            gz, gr, gh = jnp.split(inp @ Wi + b, 3, axis=1)
            rz, rr, rh = jnp.split(h @ Uh, 3, axis=1)
            z = jax.nn.sigmoid(gz + rz)
            r = jax.nn.sigmoid(gr + rr)
            hh = jnp.tanh(gh + r * rh)
            h_new = z * h + (1.0 - z) * hh
            return (h_new, h_new)
        _, outs = jax.lax.scan(step, last_hidden, jnp.swapaxes(dec_seq, 0, 1))
        return jnp.swapaxes(outs, 0, 1)

    def _L0_ffn_ref(hidden_states, Wg, Wu, Wd):
        import jax, jax.numpy as jnp
        import numpy as np
        NUM_EXPERTS = 8
        HIDDEN = 128
        FFN = 512
        BATCH = 2
        SEQ = 256
        B, S, H = hidden_states.shape
        x = hidden_states.reshape(-1, H)

        def expert_step(acc, w):
            wg, wu, wd = w
            h = jax.nn.silu(x @ wg) * (x @ wu)
            return (acc + h @ wd, None)
        acc, _ = jax.lax.scan(expert_step, jnp.zeros_like(x), (Wg, Wu, Wd))
        return acc.reshape(B, S, H)

    def _L1_xcond_ref(x, t, context, attn1_wq, attn1_wk, attn1_wv, attn1_wo, attn1_bo, attn2_wq, attn2_wk, attn2_wv, attn2_wo, attn2_bo, ff_w1, ff_b1, ff_w2, ff_b2, norm1_w, norm1_b, norm2_w, norm2_b, norm3_w, norm3_b):
        import jax, jax.numpy as jnp
        import numpy as np
        import math
        B, S, CTX, D, H, DH = (2, 256, 32, 128, 16, 64)
        INNER = H * DH
        DFF = 4 * D

        def layernorm(x, eps=1e-05):
            m = jnp.mean(x, axis=-1, keepdims=True)
            v = jnp.var(x, axis=-1, keepdims=True)
            return (x - m) * jax.lax.rsqrt(v + eps)

        def adaln(x, t, w, b):
            emb = t @ w + b
            scale, shift = jnp.split(emb, 2, axis=-1)
            return layernorm(x) * (1.0 + scale) + shift

        def mha(xq, ctx, wq, wk, wv, wo, bo):
            b, sq, _ = xq.shape
            sk = ctx.shape[1]
            q = (xq @ wq).reshape(b, sq, H, DH).transpose(0, 2, 1, 3)
            k = (ctx @ wk).reshape(b, sk, H, DH).transpose(0, 2, 1, 3)
            v = (ctx @ wv).reshape(b, sk, H, DH).transpose(0, 2, 1, 3)
            scores = jnp.einsum('bhqd,bhkd->bhqk', q, k) / math.sqrt(DH)
            attn = jax.nn.softmax(scores, axis=-1)
            out = jnp.einsum('bhqk,bhkd->bhqd', attn, v)
            out = out.transpose(0, 2, 1, 3).reshape(b, sq, INNER)
            return out @ wo + bo

        def glu_ff(x, w1, b1, w2, b2):
            u = x @ w1 + b1
            a, gate = jnp.split(u, 2, axis=-1)
            return a * jax.nn.gelu(gate, approximate=False) @ w2 + b2
        h1 = adaln(x, t, norm1_w, norm1_b)
        x = mha(h1, h1, attn1_wq, attn1_wk, attn1_wv, attn1_wo, attn1_bo) + x
        h2 = adaln(x, t, norm2_w, norm2_b)
        x = mha(h2, context, attn2_wq, attn2_wk, attn2_wv, attn2_wo, attn2_bo) + x
        h3 = adaln(x, t, norm3_w, norm3_b)
        x = glu_ff(h3, ff_w1, ff_b1, ff_w2, ff_b2) + x
        return x

    def _L1_ffn_ref(x, W_exp, b_exp, up_weights, up_bias, down_weights, W_con, b_con, down_bias):
        import jax, jax.numpy as jnp
        import numpy as np
        D_MODEL = 128
        EXPANSION = 4
        D_HIDDEN = D_MODEL * EXPANSION
        NUM_STAGES = int(np.log2(D_HIDDEN))

        def butterfly(y, weights, dim):
            lead = y.shape[:-1]
            for stage in range(weights.shape[0]):
                s = 2 ** stage
                nb = dim // (2 * s)
                yr = y.reshape(*lead, nb, 2, s)
                a = yr[..., 0, :]
                b = yr[..., 1, :]
                w = weights[stage].reshape(nb, s, 2, 2)
                na = w[..., 0, 0] * a + w[..., 0, 1] * b
                nb2 = w[..., 1, 0] * a + w[..., 1, 1] * b
                y = jnp.stack([na, nb2], axis=-2).reshape(*lead, dim)
            return y
        h = jnp.einsum('bsd,dh->bsh', x, W_exp) + b_exp
        h = butterfly(h, up_weights, D_HIDDEN)
        h = jax.nn.gelu(h + up_bias, approximate=False)
        h = butterfly(h, down_weights, D_HIDDEN)
        y = jnp.einsum('bsh,hd->bsd', h, W_con) + b_con
        return y + down_bias

    def _L2_xcond_ref(x_cls, x, noise, q_mu, q_logsig, lnkv_g, lnkv_b, lnq_g, lnq_b, lnm_g, lnm_b, lnp_g, lnp_b, wk, bk, wv, bv, wq, bq, wu, bu, w1, b1, w2, b2):
        import jax, jax.numpy as jnp
        import numpy as np
        B, N, K, D, T = (16, 512, 16, 128, 3)
        EPS_ATTN = 1e-08
        LN_EPS = 1e-05

        def _ln(x, g, b):
            mu = jnp.mean(x, axis=-1, keepdims=True)
            var = jnp.mean(jnp.square(x - mu), axis=-1, keepdims=True)
            return (x - mu) * jax.lax.rsqrt(var + LN_EPS) * g + b
        scale = D ** (-0.5)
        x_in = _ln(x, lnkv_g, lnkv_b)
        k = x_in @ wk + bk
        v = x_in @ wv + bv
        slots = q_mu + jnp.exp(q_logsig) * noise
        for _ in range(T):
            prev = slots
            q = _ln(slots, lnq_g, lnq_b) @ wq + bq
            logits = jnp.einsum('bnd,bkd->bnk', k, q) / scale
            attn = jax.nn.softmax(logits, axis=-1) + EPS_ATTN
            attn = attn / jnp.sum(attn, axis=1, keepdims=True)
            upd = jnp.einsum('bnk,bnd->bkd', attn, v)
            slots = upd @ wu + bu + prev
            h = _ln(slots, lnm_g, lnm_b) @ w1 + b1
            slots = jax.nn.gelu(h, approximate=False) @ w2 + b2 + slots
            slots = _ln(slots + x_cls[:, None, :], lnp_g, lnp_b)
        return slots

    def _L2_ffn_ref(x, gate_w, w_up, w_down, sg_gate, sg_up, sg_down):
        import jax, jax.numpy as jnp
        import numpy as np
        B, T, D = (4, 512, 128)
        E = 8
        TOP_K = 2
        FFN = 384
        HALF = FFN // 2

        def _kaiming_uniform(key, shape, fan_in):
            bound = 1.0 / np.sqrt(fan_in)
            return jax.random.uniform(key, shape, jnp.float32, -bound, bound)
        b, t, d = x.shape
        xf = x.reshape(b * t, d)
        N = xf.shape[0]
        logits = xf @ gate_w.T
        topk_logits, topk_idx = jax.lax.top_k(logits, TOP_K)
        topk_w = jax.nn.softmax(topk_logits.astype(jnp.float32), axis=-1).astype(x.dtype)
        comb = jnp.zeros((N, E), x.dtype).at[jnp.arange(N)[:, None], topk_idx].add(topk_w)
        wg = w_up[:, :HALF, :]
        wu = w_up[:, HALF:, :]
        out = jnp.zeros_like(xf)
        for e in range(E):
            g = xf @ wg[e].T
            u = xf @ wu[e].T
            y = jax.nn.silu(g) * u @ w_down[e].T
            out = out + comb[:, e:e + 1] * y
        shared = jax.nn.silu(xf @ sg_gate.T) * (xf @ sg_up.T) @ sg_down.T
        return (shared + out).reshape(b, t, d)

    def _L3_xcond_ref(x, latents, shift, scale, ln1_w, ln1_b, ln2_w, ln2_b, Wq, Wkv, Wo):
        import jax, jax.numpy as jnp
        import numpy as np
        DIM = 128
        DIM_HEAD = 64
        HEADS = 16
        INNER = DIM_HEAD * HEADS
        B, N1, N2 = (8, 512, 32)
        EPS = 1e-05

        def layer_norm(x, w, b):
            mu = jnp.mean(x, axis=-1, keepdims=True)
            var = jnp.var(x, axis=-1, keepdims=True)
            return (x - mu) * jax.lax.rsqrt(var + EPS) * w + b
        x = layer_norm(x, ln1_w, ln1_b)
        lat = layer_norm(latents, ln2_w, ln2_b)
        lat = lat * (1.0 + scale[:, None, :]) + shift[:, None, :]
        b, n2, _ = lat.shape
        q = jnp.einsum('bld,ed->ble', lat, Wq)
        kv_in = jnp.concatenate((x, lat), axis=-2)
        kv = jnp.einsum('bld,ed->ble', kv_in, Wkv)
        k, v = jnp.split(kv, 2, axis=-1)

        def to_heads(t):
            bsz, L, _ = t.shape
            return t.reshape(bsz, L, HEADS, DIM_HEAD).transpose(0, 2, 1, 3)
        q, k, v = (to_heads(q), to_heads(k), to_heads(v))
        attn_scale = 1.0 / np.sqrt(np.sqrt(DIM_HEAD)).astype(np.float32)
        logits = jnp.einsum('bhqd,bhkd->bhqk', q * attn_scale, k * attn_scale)
        w = jax.nn.softmax(logits.astype(jnp.float32), axis=-1).astype(logits.dtype)
        out = jnp.einsum('bhqk,bhkd->bhqd', w, v)
        out = out.transpose(0, 2, 1, 3).reshape(b, n2, INNER)
        return jnp.einsum('ble,de->bld', out, Wo)

    def _L3_ffn_ref(x, gate, W1, b1, W2, b2):
        import jax, jax.numpy as jnp
        import numpy as np
        N_EXPERTS = 16
        TOP_K = int(N_EXPERTS * 0.2)
        EPS = 1e-12
        raw_gate = jax.nn.softmax(jnp.einsum('btd,de->bte', x, gate), axis=-1)
        _, topk_idx = jax.lax.top_k(raw_gate, TOP_K)
        mask = jax.nn.one_hot(topk_idx, raw_gate.shape[-1], dtype=raw_gate.dtype).sum(axis=2)
        gate_topk = mask * raw_gate
        gate_topk = gate_topk / jnp.maximum(jnp.sum(jnp.abs(gate_topk), axis=-1, keepdims=True), EPS)
        hidden = jax.nn.relu(jnp.einsum('btd,edh->bteh', x, W1) + b1)
        expert_out = jnp.einsum('bteh,ehd->bted', hidden, W2) + b2
        return jnp.einsum('bte,bted->btd', gate_topk, expert_out)
    x = x + _L0_xcond_ref(_layernorm(x, axis=-1), ctx_1024, cond_1024, L0_xcond_W_att, L0_xcond_V_att, L0_xcond_Wi, L0_xcond_Uh, L0_xcond_b)
    x = x + _L0_ffn_ref(_layernorm(x, axis=-1), L0_ffn_Wg, L0_ffn_Wu, L0_ffn_Wd)
    x = x + _L1_xcond_ref(_layernorm(x, axis=-1), cond_1024[:, None, :], ctx_1024, L1_xcond_attn1_wq, L1_xcond_attn1_wk, L1_xcond_attn1_wv, L1_xcond_attn1_wo, L1_xcond_attn1_bo, L1_xcond_attn2_wq, L1_xcond_attn2_wk, L1_xcond_attn2_wv, L1_xcond_attn2_wo, L1_xcond_attn2_bo, L1_xcond_ff_w1, L1_xcond_ff_b1, L1_xcond_ff_w2, L1_xcond_ff_b2, L1_xcond_norm1_w, L1_xcond_norm1_b, L1_xcond_norm2_w, L1_xcond_norm2_b, L1_xcond_norm3_w, L1_xcond_norm3_b)
    x = x + _L1_ffn_ref(_layernorm(x, axis=-1), L1_ffn_W_exp, L1_ffn_b_exp, L1_ffn_up_weights, L1_ffn_up_bias, L1_ffn_down_weights, L1_ffn_W_con, L1_ffn_b_con, L1_ffn_down_bias)
    x = x + _L2_xcond_ref(cond_1024, ctx_1024, _layernorm(x, axis=-1), L2_xcond_q_mu, L2_xcond_q_logsig, L2_xcond_lnkv_g, L2_xcond_lnkv_b, L2_xcond_lnq_g, L2_xcond_lnq_b, L2_xcond_lnm_g, L2_xcond_lnm_b, L2_xcond_lnp_g, L2_xcond_lnp_b, L2_xcond_wk, L2_xcond_bk, L2_xcond_wv, L2_xcond_bv, L2_xcond_wq, L2_xcond_bq, L2_xcond_wu, L2_xcond_bu, L2_xcond_w1, L2_xcond_b1, L2_xcond_w2, L2_xcond_b2)
    x = x + _L2_ffn_ref(_layernorm(x, axis=-1), L2_ffn_gate_w, L2_ffn_w_up, L2_ffn_w_down, L2_ffn_sg_gate, L2_ffn_sg_up, L2_ffn_sg_down)
    x = x + _L3_xcond_ref(ctx_1024, _layernorm(x, axis=-1), cond_1024, cond_1024, L3_xcond_ln1_w, L3_xcond_ln1_b, L3_xcond_ln2_w, L3_xcond_ln2_b, L3_xcond_Wq, L3_xcond_Wkv, L3_xcond_Wo)
    x = x + _L3_ffn_ref(_layernorm(x, axis=-1), L3_ffn_gate, L3_ffn_W1, L3_ffn_b1, L3_ffn_W2, L3_ffn_b2)
    return x

_drawn_inputs = setup_inputs


def setup_inputs(seed=0):
    import zlib

    import numpy as np

    out = dict(_drawn_inputs(seed))
    spreads = {'L0_xcond_b': (0.0, 0.1),
     'L1_ffn_b_exp': (0.0, 0.1),
     'L1_ffn_up_bias': (0.0, 0.1),
     'L1_ffn_b_con': (0.0, 0.447),
     'L1_ffn_down_bias': (0.0, 0.481),
     'L2_xcond_lnkv_g': (1.0, 0.6),
     'L2_xcond_lnkv_b': (0.0, 0.8),
     'L2_xcond_lnq_g': (1.0, 0.6),
     'L2_xcond_lnq_b': (0.0, 2.0),
     'L2_xcond_lnm_g': (1.0, 0.6),
     'L2_xcond_lnm_b': (0.0, 0.8),
     'L2_xcond_lnp_g': (1.0, 0.2),
     'L2_xcond_lnp_b': (0.0, 0.1),
     'L2_xcond_bk': (0.0, 0.8),
     'L2_xcond_bv': (0.0, 0.8),
     'L2_xcond_bq': (0.0, 2.0),
     'L2_xcond_bu': (0.0, 0.384),
     'L2_xcond_b1': (0.0, 0.8),
     'L2_xcond_b2': (0.0, 0.412),
     'L3_xcond_ln1_w': (1.0, 0.6),
     'L3_xcond_ln1_b': (0.0, 2.0),
     'L3_xcond_ln2_w': (1.0, 0.6),
     'L3_xcond_ln2_b': (0.0, 2.0)}
    factors = {'L1_xcond_attn1_bo': 8.0,
     'L1_xcond_attn2_bo': 8.0,
     'L1_xcond_ff_b1': 8.0,
     'L1_xcond_ff_b2': 8.0,
     'L1_xcond_norm1_b': 5.503,
     'L1_xcond_norm2_b': 8.0,
     'L1_xcond_norm3_b': 8.0,
     'L2_xcond_q_logsig': 8.0,
     'L2_xcond_wk': 8.0,
     'L2_xcond_wv': 8.0,
     'L2_xcond_wq': 8.0,
     'L2_xcond_wu': 6.949,
     'L2_xcond_w1': 8.0,
     'L2_xcond_w2': 8.0,
     'L2_ffn_gate_w': 4.849,
     'L2_ffn_w_up': 4.17,
     'L2_ffn_w_down': 4.148,
     'L2_ffn_sg_gate': 3.114,
     'L2_ffn_sg_up': 2.834,
     'L2_ffn_sg_down': 2.712,
     'L3_xcond_Wq': 30.872,
     'L3_ffn_b1': 39.911,
     'L3_ffn_b2': 26.501}
    for name, (base, spread) in spreads.items():
        noise = np.random.default_rng([zlib.crc32(name.encode()), seed]).standard_normal(out[name].shape)
        drawn = base * np.exp(spread * noise) if base else spread * noise
        out[name] = jnp.asarray(drawn.astype(out[name].dtype))
    for name, factor in factors.items():
        out[name] = (out[name] * factor).astype(out[name].dtype)
    return out
```

```python
from contextlib import ExitStack

import concourse.bass as bass
import numpy as np
from concourse import mybir

P = 128
B, T, D = 2, 512, 128
NT = B * T // P
TB = T // P
S = 77
HEADS, DH = 16, 64
HP = HEADS // 2
F32 = mybir.dt.float32
BF16 = mybir.dt.bfloat16
ALU = mybir.AluOpType
ACT = mybir.ActivationFunctionType
AX = mybir.AxisListType


class Count:

    def __init__(self, sem):
        self.sem, self.at = sem, 0


class Core:

    def __init__(self, nc, ctx, w):
        self.nc, self.ctx, self.w = nc, ctx, w
        self.counts = {}
        self.pair = [ctx.enter_context(nc.psum_tensor(f"pair{i}", [P, 1024], F32)) for i in range(4)]
        self.bank = [self.pair[i // 2][:, (i % 2) * 512:(i % 2) * 512 + 512] for i in range(8)]
        self.n = 0

    def count(self, name):
        if name not in self.counts:
            self.counts[name] = Count(self.ctx.enter_context(self.nc.semaphore(name)))
        return self.counts[name]

    def sb(self, ctx, name, shape, dt=F32):
        self.n += 1
        return ctx.enter_context(self.nc.sbuf_tensor(f"{name}_{self.n}", shape, dt))


def layernorm(k, src, rows, n, dst=None, dst_T=None, affine=None, group=TB, add_row=None):
    nc = k.nc
    stats_c, sd_c, xn_c, turned_c, out_c = (k.count(x) for x in ("ln_stats", "ln_deviation", "ln_normal", "ln_turned", "ln_out"))
    groups = n // group
    with ExitStack() as ctx:
        stats = k.sb(ctx, "ln_stats", [P, n, 6])
        mv = k.sb(ctx, "ln_mv", [P, n, 2])
        sd = k.sb(ctx, "ln_sd", [P, n])
        rstd = k.sb(ctx, "ln_rstd", [P, n])
        xn = dst if dst is not None else k.sb(ctx, "ln_xn", [P, n, D])
        with nc.Block() as block:
            @block.vector
            def _(dve):
                for j in range(n):
                    nc.vector.bn_stats(stats[0:rows, j, :], src[0:rows, j, :]).then_inc(stats_c.sem, 1)
                for j in range(n):
                    dve.wait_ge(stats_c.sem, stats_c.at + j + 1)
                    nc.vector.bn_aggr(mv[0:rows, j, :], stats[0:rows, j, :]).then_inc(stats_c.sem, 1)
                dve.wait_ge(sd_c.sem, sd_c.at + 1)
                nc.vector.reciprocal(rstd[0:rows, :], sd[0:rows, :]).then_inc(stats_c.sem, 1)
                dve.wait_ge(stats_c.sem, stats_c.at + 2 * n + 1)
                for j in range(n):
                    nc.vector.tensor_scalar(xn[0:rows, j, :], src[0:rows, j, :], mv[0:rows, j, 0:1], rstd[0:rows, j:j + 1],
                                            ALU.subtract, ALU.mult).then_inc(xn_c.sem, 1)
                if dst_T is not None:
                    for g in range(1, groups, 2):
                        dve.wait_ge(turned_c.sem, turned_c.at + g + 1)
                        out = dst_T(g)
                        ps = k.bank[g][:, 0:group * rows]
                        if affine is None:
                            nc.vector.tensor_copy(out, ps).then_inc(out_c.sem, 1)
                        else:
                            nc.vector.tensor_scalar(out, ps, affine[g][0], affine[g][1], ALU.mult, ALU.add).then_inc(out_c.sem, 1)

            @block.scalar
            def _(act):
                act.wait_ge(stats_c.sem, stats_c.at + 2 * n)
                nc.scalar.activation(sd[0:rows, :], mv[0:rows, :, 1], ACT.Sqrt, bias=k.eps[0:rows, 0:1]).then_inc(sd_c.sem, 1)
                if dst_T is not None:
                    for g in range(0, groups, 2):
                        act.wait_ge(turned_c.sem, turned_c.at + g + 1)
                        out = dst_T(g)
                        ps = k.bank[g][:, 0:group * rows]
                        if affine is None:
                            nc.scalar.activation(out, ps, ACT.Copy).then_inc(out_c.sem, 1)
                        else:
                            nc.scalar.activation(out, ps, ACT.Identity, scale=affine[g][0], bias=affine[g][1]).then_inc(out_c.sem, 1)

            if dst_T is not None:
                @block.tensor
                def _(pe):
                    for j in range(n):
                        pe.wait_ge(xn_c.sem, xn_c.at + j + 1)
                        c = j % group
                        last = nc.tensor.transpose(k.bank[j // group][:, c * rows:(c + 1) * rows], xn[0:rows, j, :],
                                                   k.ident[0:rows, 0:rows])
                        if c == group - 1:
                            last.then_inc(turned_c.sem, 1)
    stats_c.at += 2 * n + 1
    sd_c.at += 1
    xn_c.at += n
    if dst_T is not None:
        turned_c.at += groups
        out_c.at += groups


def turn_and_add(k, src_T, dst, psum=True, bias=None, first=None, dst2=None):
    nc = k.nc
    flat_c, turned_c, out_c = (k.count(x) for x in ("add_flat", "add_turned", "add_out"))
    with ExitStack() as ctx:
        flat = k.sb(ctx, "add_flat", [P, B, T])
        with nc.Block() as block:
            @block.scalar
            def _(act):
                for b in range(B):
                    if bias is None:
                        nc.scalar.activation(flat[:, b, :], src_T[b], ACT.Copy).then_inc(flat_c.sem, 1)
                    else:
                        nc.scalar.activation(flat[:, b, :], src_T[b], ACT.Identity, bias=bias).then_inc(flat_c.sem, 1)

            @block.tensor
            def _(pe):
                for b in range(B):
                    pe.wait_ge(flat_c.sem, flat_c.at + b + 1)
                    for c in range(TB):
                        last = nc.tensor.transpose(k.bank[b][:, c * P:(c + 1) * P], flat[:, b, c * P:(c + 1) * P], k.ident[:])
                    last.then_inc(turned_c.sem, 1)

            @block.vector
            def _(dve):
                for b in range(B):
                    dve.wait_ge(turned_c.sem, turned_c.at + b + 1)
                    ps = k.bank[b].rearrange("p (c d) -> p c d", c=TB)
                    old = (dst if first is None else first)[:, b * TB:(b + 1) * TB, :]
                    nc.vector.tensor_tensor(dst[:, b * TB:(b + 1) * TB, :], old, ps, ALU.add).then_inc(out_c.sem, 1)
                    if dst2 is not None:
                        dve.wait_ge(out_c.sem, out_c.at + b + 1)
                        nc.vector.tensor_tensor(dst2[:, b * TB:(b + 1) * TB, :], dst2[:, b * TB:(b + 1) * TB, :],
                                                dst[:, b * TB:(b + 1) * TB, :], ALU.add)
    flat_c.at += B
    turned_c.at += B
    out_c.at += B


def mlp(k, x_T, experts, widths, gate, up, down, func, gate_bias=None, up_bias=None, comb=None, last=None, last_rhs=None,
        aside=None):
    nc = k.nc
    F = sum(widths)
    nf = len(widths)
    per = 2 if experts > 1 else 1
    U = nf * B
    units = [(s, f, b) for s in range(per) for f in range(nf) for b in range(B)]
    nU = len(units)
    loads = (2 + (up is not None) + (comb is not None)) * 16
    names = ("mlp_gate", "mlp_up", "mlp_act", "mlp_mul", "mlp_hidden", "mlp_down", "mlp_opened")
    gate_c, up_c, act_c, mul_c, hid_c, down_c, open_c = (k.count(x) for x in names)
    if comb is None:
        hid_c = act_c if up is None else mul_c
    load_c = [k.count(f"mlp_loads{s}") for s in range(2)]
    acc = k.bank[4:6]
    rounds = experts // per
    with ExitStack() as ctx:
        G = F + (nf if gate_bias == "columns" else 0)
        wg = k.sb(ctx, "mlp_wg", [P, per, G])
        wu = k.sb(ctx, "mlp_wu", [P, per, F]) if up is not None else None
        wd = k.sb(ctx, "mlp_wd", [P, per, nf, D])
        cb = k.sb(ctx, "mlp_cb", [P, per, B, T]) if comb is not None else None
        a_s = k.sb(ctx, "mlp_act", [P, 2, T])
        m_s = k.sb(ctx, "mlp_mul", [P, 2, T]) if (up is not None and comb is not None) else None
        h_s = k.sb(ctx, "mlp_hidden", [P, 3, T])
        hid_buf = h_s if (up is not None or comb is not None) else None

        def load(q, e, s):
            q.dma_start(wg[:, s, :], gate[e]).then_inc(load_c[s].sem, 16)
            if up is not None:
                q.dma_start(wu[:, s, :], up[e]).then_inc(load_c[s].sem, 16)
            if comb is not None:
                q.dma_start(cb[:, s, :, :].rearrange("p b t -> p (b t)"), comb[e:e + 1, :].to_broadcast([P, B * T]) if isinstance(e, int)
                            else comb[bass.ds(e, 1), :].to_broadcast([P, B * T])).then_inc(load_c[s].sem, 16)
            q.dma_start(wd[:, s, :, :], down[e].rearrange("f p d -> p f d")).then_inc(load_c[s].sem, 16)

        def rounds_of(eng, body):
            if rounds == 1:
                body(0)
            else:
                with eng.Fori(0, rounds) as r:
                    body(r)

        with nc.Block() as block:
            if aside is not None:
                aside(k, block, ctx)

            @block.sync
            def _(sp):
                for s in range(per):
                    load(sp, s, s)
                if rounds > 1:
                    with sp.Fori(0, rounds - 1) as r:
                        for s in range(per):
                            sp.wait_ge(down_c.sem, down_c.at + r * nU + (s + 1) * U)
                            load(sp, (r + 1) * per + s, s)

            @block.tensor
            def _(pe):
                for b in range(B):
                    nc.tensor.matmul(acc[b], k.zeros[0:1, 0:P], k.ones[0:1, :], start=True, stop=False, skip_group_check=True)

                def down_product(r, q):
                    s, f, b = units[q]
                    m = widths[f]
                    pe.wait_ge(hid_c.sem, hid_c.at + r * nU + q + 1)
                    nc.tensor.matmul(acc[b], wd[0:m, s, f, :], h_s[0:m, q % 3, :], start=False, stop=False,
                                     skip_group_check=True).then_inc(down_c.sem, 1)

                def body(r):
                    for q, (s, f, b) in enumerate(units):
                        m, f0 = widths[f], sum(widths[:f])
                        if q % U == 0:
                            pe.wait_ge(load_c[s].sem, load_c[s].at + (r + 1) * loads)
                        if q >= 2:
                            pe.wait_ge(act_c.sem, act_c.at + r * nU + q - 1)
                        nc.tensor.matmul(k.bank[q % 2][0:m, :], wg[:, s, f0:f0 + m], x_T[:, b * T:(b + 1) * T], start=True,
                                         stop=True).then_inc(gate_c.sem, 1)
                        if up is not None:
                            if q >= 2:
                                pe.wait_ge(mul_c.sem, mul_c.at + r * nU + q - 1)
                            nc.tensor.matmul(k.bank[2 + q % 2][0:m, :], wu[:, s, f0:f0 + m], x_T[:, b * T:(b + 1) * T],
                                             start=True, stop=True).then_inc(up_c.sem, 1)
                        if q >= 2:
                            down_product(r, q - 2)
                    for q in range(max(nU - 2, 0), nU):
                        down_product(r, q)

                rounds_of(pe, body)
                for b in range(B):
                    nc.tensor.matmul(acc[b], last, last_rhs[b], start=False, stop=True, skip_group_check=True)

            @block.scalar
            def _(act):
                def body(r):
                    for q, (s, f, b) in enumerate(units):
                        m = widths[f]
                        act.wait_ge(gate_c.sem, gate_c.at + r * nU + q + 1)
                        if hid_buf is None:
                            if q >= 3:
                                act.wait_ge(down_c.sem, down_c.at + r * nU + q - 2)
                            out = h_s[0:m, q % 3, :]
                        else:
                            if q >= 2:
                                act.wait_ge(mul_c.sem if up is not None else hid_c.sem,
                                            (mul_c.at if up is not None else hid_c.at) + r * nU + q - 1)
                            out = a_s[0:m, q % 2, :]
                        if gate_bias == "columns":
                            bias = wg[:, s, F + f:F + f + 1]
                        else:
                            bias = gate_bias(f) if gate_bias is not None else 0.0
                        nc.scalar.activation(out, k.bank[q % 2][0:m, :], func, bias=bias).then_inc(act_c.sem, 1)

                rounds_of(act, body)

            if up is not None:
                @block.vector
                def _(dve):
                    def body(r):
                        for q, (s, f, b) in enumerate(units):
                            m = widths[f]
                            dve.wait_ge(act_c.sem, act_c.at + r * nU + q + 1)
                            dve.wait_ge(up_c.sem, up_c.at + r * nU + q + 1)
                            if comb is None:
                                if q >= 3:
                                    dve.wait_ge(down_c.sem, down_c.at + r * nU + q - 2)
                                out = h_s[0:m, q % 3, :]
                            else:
                                if q >= 2:
                                    dve.wait_ge(hid_c.sem, hid_c.at + r * nU + q - 1)
                                out = m_s[0:m, q % 2, :]
                            if up_bias is None:
                                i = nc.vector.tensor_tensor(out, k.bank[2 + q % 2][0:m, :], a_s[0:m, q % 2, :], ALU.mult)
                            else:
                                i = nc.vector.scalar_tensor_tensor(out=out, in0=k.bank[2 + q % 2][0:m, :], scalar=up_bias(f),
                                                                   in1=a_s[0:m, q % 2, :], op0=ALU.add, op1=ALU.mult)
                            i.then_inc(mul_c.sem, 1)

                    rounds_of(dve, body)

            if comb is not None:
                @block.gpsimd
                def _(pool):
                    def body(r):
                        for q, (s, f, b) in enumerate(units):
                            m = widths[f]
                            if q % U == 0:
                                pool.wait_ge(load_c[s].sem, load_c[s].at + (r + 1) * loads)
                            src = m_s if up is not None else a_s
                            c = mul_c if up is not None else act_c
                            pool.wait_ge(c.sem, c.at + r * nU + q + 1)
                            if q >= 3:
                                pool.wait_ge(down_c.sem, down_c.at + r * nU + q - 2)
                            nc.gpsimd.tensor_tensor(h_s[0:m, q % 3, :], src[0:m, q % 2, :], cb[0:m, s, b, :],
                                                    ALU.mult).then_inc(hid_c.sem, 1)

                    rounds_of(pool, body)
    n = rounds * nU
    for c in (gate_c, act_c, down_c):
        c.at += n
    if comb is not None:
        hid_c.at += n
    if up is not None:
        up_c.at += n
        mul_c.at += n
    for s in range(per):
        load_c[s].at += rounds * loads


def attention(k, q_T, kv_T, nk, wq, wk, wv, wo, bias):
    nc = k.nc
    tiles = [(i * P, min(P, nk - i * P)) for i in range((nk + P - 1) // P)]
    KT = len(tiles)
    parts = [(0, min(nk, 512))] + ([(512, nk - 512)] if nk > 512 else [])
    items = [(b, a, j) for b in range(B) for a in range(2) for j in range(TB)]
    nI = len(items)
    nG = nI // TB
    names = ("att_v_psum", "att_v_dve", "att_v_act", "att_ones", "att_v_pair", "att_q_psum", "att_q", "att_k_psum", "att_k", "att_score", "att_max",
             "att_prob", "att_turned", "att_turned_copy", "att_sum", "att_recip", "att_heads", "att_wo_used", "att_wv_load",
             "att_wqk_load", "att_wo_load")
    (vps_c, vd_c, va_c, ones_c, vpair_c, qps_c, q_c, kps_c, k_c, score_c, max_c, prob_c, turned_c, copy_c, sum_c, rec_c, heads_c, wo_used_c,
     wv_load_c, wqk_load_c, wo_load_c) = (k.count(x) for x in names)
    acc = k.bank[6:8]
    with ExitStack() as ctx:
        wq_s = k.sb(ctx, "att_wq", [P, P])
        wk_s = k.sb(ctx, "att_wk", [P, P])
        wo_s = k.sb(ctx, "att_wo", [P, P])
        wv_s = k.sb(ctx, "att_wv", [P, HEADS * DH])
        v_all = k.sb(ctx, "att_v", [P, B, KT, HEADS, DH])
        v_pair = k.sb(ctx, "att_v_pair", [P, B, KT, 4 * DH])
        qh = k.sb(ctx, "att_q", [P, 2, B, T])
        kh = k.sb(ctx, "att_k", [P, B, nk])
        prob = k.sb(ctx, "att_prob", [P, 2, nk])
        prob_T = k.sb(ctx, "att_prob_T", [P, 2, KT, T])
        recip = k.sb(ctx, "att_recip", [P, 2, T])
        heads_T = k.sb(ctx, "att_heads_T", [P, B, T])
        negmax = k.sb(ctx, "att_negmax", [P, 2])

        def rows(a):
            return slice(DH * a, DH * a + DH)

        def fifth(i):
            return k.pair[i % 2][0:tiles[4][1], 512 + P:512 + 2 * P]

        v_jobs = [(b, t, c) for b in range(B) for t in range(KT) for c in range(2)]
        nV = len(v_jobs) // 2

        def pairs_of(eng, body):
            with eng.Fori(0, HP - 1) as r:
                body(r, False)
            body(HP - 1, True)

        def values_of(n):
            b, t, c = v_jobs[n]
            return v_all[0:tiles[t][1], b, t, 8 * c:8 * c + 8, :].rearrange("p h d -> p (h d)"), k.bank[n % 4][0:tiles[t][1], :]

        full = sum(tn == P for _, tn in tiles)
        spans = ([(P, 0, full)] if full else []) + ([(tiles[full][1], full, KT)] if full < KT else [])
        nS = 2 * len(spans)

        with nc.Block() as block:
            @block.sync
            def _(sp):
                sp.dma_start(wv_s[:], wv).then_inc(wv_load_c.sem, 16)
                sp.dma_start(wq_s[:], wq[0]).then_inc(wqk_load_c.sem, 16)
                sp.dma_start(wk_s[:], wk[0]).then_inc(wqk_load_c.sem, 16)
                sp.dma_start(wo_s[:], wo[0]).then_inc(wo_load_c.sem, 16)
                with sp.Fori(0, HP - 1) as r:
                    sp.wait_ge(kps_c.sem, kps_c.at + r * B + B)
                    sp.dma_start(wq_s[:], wq[r + 1]).then_inc(wqk_load_c.sem, 16)
                    sp.dma_start(wk_s[:], wk[r + 1]).then_inc(wqk_load_c.sem, 16)
                    sp.wait_ge(wo_used_c.sem, wo_used_c.at + r + 1)
                    sp.dma_start(wo_s[:], wo[r + 1]).then_inc(wo_load_c.sem, 16)

            @block.gpsimd
            def _(pool):
                nc.gpsimd.memset(qh[:], 0.0).then_inc(ones_c.sem, 1)
                nc.gpsimd.memset(v_pair[:, :, :, DH:3 * DH], 1.0).then_inc(ones_c.sem, 1)
                pool.wait_ge(vd_c.sem, vd_c.at + nV)
                pool.wait_ge(va_c.sem, va_c.at + nV)

                def values(r):
                    for m, t0, t1 in spans:
                        for a in range(2):
                            nc.gpsimd.tensor_copy(v_pair[0:m, :, t0:t1, 3 * a * DH:(3 * a + 1) * DH],
                                                  v_all[0:m, :, t0:t1, 2 * r + a, :]).then_inc(vpair_c.sem, 1)

                values(0)
                with pool.Fori(0, HP - 1) as r:
                    pool.wait_ge(sum_c.sem, sum_c.at + r * nG + nG)
                    values(r + 1)

            @block.tensor
            def _(pe):
                mm = nc.tensor.matmul
                pe.wait_ge(wv_load_c.sem, wv_load_c.at + 16)
                for n, (b, t, c) in enumerate(v_jobs):
                    t0, tn = tiles[t]
                    if n >= 4:
                        side = va_c if n % 2 else vd_c
                        pe.wait_ge(side.sem, side.at + n // 2 - 1)
                    mm(k.bank[n % 4][0:tn, :], kv_T[:, b, t0:t0 + tn], wv_s[:, c * 512:(c + 1) * 512], start=True,
                       stop=True).then_inc(vps_c.sem, 1)
                for b in range(B):
                    mm(acc[b], bias, k.ones[0:1, :], start=True, stop=False, skip_group_check=True)
                pe.wait_ge(vd_c.sem, vd_c.at + nV)
                pe.wait_ge(va_c.sem, va_c.at + nV)
                pe.wait_ge(ones_c.sem, ones_c.at + 2)

                def project_pair(r):
                    pe.wait_ge(wqk_load_c.sem, wqk_load_c.at + r * 32 + 32)
                    for b in range(B):
                        mm(k.bank[2 * b], wq_s[:], q_T[:, b, :], start=True, stop=True).then_inc(qps_c.sem, 1)
                    for b in range(B):
                        pe.wait_ge(q_c.sem, q_c.at + r * B + b + 1)
                        for s0, sn in parts:
                            last = mm(k.pair[b][:, s0:s0 + sn], wk_s[:], kv_T[:, b, s0:s0 + sn], start=True, stop=True)
                        last.then_inc(kps_c.sem, 1)

                def scores(r, i):
                    b, a, j = items[i]
                    if i < 2:
                        pe.wait_ge(k_c.sem, k_c.at + r * B + B)
                    else:
                        pe.wait_ge(prob_c.sem, prob_c.at + r * nI + i - 1)
                        if KT == 5:
                            pe.wait_ge(copy_c.sem, copy_c.at + r * nI + i - 1)
                    for s0, sn in parts:
                        last = mm(k.pair[i % 2][:, s0:s0 + sn], qh[:, a, b, j * P:(j + 1) * P], kh[:, b, s0:s0 + sn],
                                  start=True, stop=True)
                    last.then_inc(score_c.sem, 1)

                def turn(r, i):
                    if i >= 1:
                        pe.wait_ge(copy_c.sem, copy_c.at + r * nI + i)
                    pe.wait_ge(prob_c.sem, prob_c.at + r * nI + i + 1)
                    for t, (t0, tn) in enumerate(tiles):
                        out = k.bank[4][0:tn, t * P:(t + 1) * P] if t < 4 else fifth(i)
                        last = nc.tensor.transpose(out, prob[:, i % 2, t0:t0 + tn], k.ident[:])
                    last.then_inc(turned_c.sem, 1)

                def weigh(r, g, ts):
                    b, a = g // 2, g % 2
                    if 0 in ts:
                        pe.wait_ge(copy_c.sem, copy_c.at + r * nI + (g + 1) * TB)
                        if g == 0:
                            pe.wait_ge(vpair_c.sem, vpair_c.at + r * nS + nS)
                        else:
                            pe.wait_ge(heads_c.sem, heads_c.at + r * nG + g)
                    for t in ts:
                        tn = tiles[t][1]
                        last = mm(k.bank[5], v_pair[0:tn, b, t, a * 2 * DH:(a + 1) * 2 * DH], prob_T[0:tn, g % 2, t, :],
                                  start=(t == 0), stop=(t == KT - 1))
                    if KT - 1 in ts:
                        last.then_inc(sum_c.sem, 1)

                def body(r, last_pair):
                    for i in range(1, nI + 1):
                        if 2 <= i < nI:
                            scores(r, i)
                        turn(r, i - 1)
                        g, step = (i - 5) // TB, (i - 5) % TB
                        if i >= 5 and step < 3:
                            ts = [t for t in range(KT) if min(t // 2, 2) == step]
                            if ts:
                                weigh(r, g, ts)
                    if not last_pair:
                        if KT == 5:
                            pe.wait_ge(copy_c.sem, copy_c.at + r * nI + nI)
                        project_pair(r + 1)
                    weigh(r, nG - 1, list(range(KT)))
                    if not last_pair:
                        scores(r + 1, 0)
                        scores(r + 1, 1)
                    pe.wait_ge(wo_load_c.sem, wo_load_c.at + r * 16 + 16)
                    pe.wait_ge(heads_c.sem, heads_c.at + r * nG + nG)
                    for b in range(B):
                        last = mm(acc[b], wo_s[:], heads_T[:, b, :], start=False, stop=False, skip_group_check=True)
                    last.then_inc(wo_used_c.sem, 1)

                project_pair(0)
                scores(0, 0)
                scores(0, 1)
                pairs_of(pe, body)
                for b in range(B):
                    mm(acc[b], k.zeros[0:1, 0:P], k.ones[0:1, :], start=False, stop=True, skip_group_check=True)

            @block.scalar
            def _(act):
                for n in range(1, 2 * nV, 2):
                    act.wait_ge(vps_c.sem, vps_c.at + n + 1)
                    nc.scalar.activation(*values_of(n), ACT.Copy).then_inc(va_c.sem, 1)
                act.wait_ge(ones_c.sem, ones_c.at + 1)

                def queries(r):
                    for b in range(B):
                        act.wait_ge(qps_c.sem, qps_c.at + r * B + b + 1)
                        for a in range(2):
                            last = nc.scalar.activation(qh[rows(a), a, b, :], k.bank[2 * b][rows(a), :], ACT.Copy, scale=DH ** -0.5)
                        last.then_inc(q_c.sem, 1)

                def body(r, last_pair):
                    for i in range(nI):
                        if i >= 2:
                            act.wait_ge(turned_c.sem, turned_c.at + r * nI + i - 1)
                        act.wait_ge(max_c.sem, max_c.at + r * nI + i + 1)
                        nc.scalar.activation(prob[:, i % 2, :], k.pair[i % 2][:, 0:nk], ACT.Exp,
                                             bias=negmax[:, i % 2:i % 2 + 1]).then_inc(prob_c.sem, 1)
                    if not last_pair:
                        queries(r + 1)

                queries(0)
                pairs_of(act, body)

            @block.vector
            def _(dve):
                v = nc.vector
                for n in range(0, 2 * nV, 2):
                    dve.wait_ge(vps_c.sem, vps_c.at + n + 1)
                    v.tensor_copy(*values_of(n)).then_inc(vd_c.sem, 1)

                def keys(r):
                    for b in range(B):
                        dve.wait_ge(kps_c.sem, kps_c.at + r * B + b + 1)
                        v.tensor_copy(kh[:, b, :], k.pair[b][:, 0:nk]).then_inc(k_c.sem, 1)

                def maximum(r, i):
                    dve.wait_ge(score_c.sem, score_c.at + r * nI + i + 1)
                    v.tensor_reduce(negmax[:, i % 2:i % 2 + 1], k.pair[i % 2][:, 0:nk], AX.X, ALU.max, negate=True).then_inc(max_c.sem, 1)

                def copy(r, i):
                    g, j = i // TB, i % TB
                    if g >= 2:
                        dve.wait_ge(sum_c.sem, sum_c.at + r * nG + g - 1)
                    dve.wait_ge(turned_c.sem, turned_c.at + r * nI + i + 1)
                    if full:
                        last = v.tensor_copy(prob_T[:, g % 2, 0:full, j * P:(j + 1) * P],
                                             k.bank[4][:, 0:full * P].rearrange("p (t q) -> p t q", q=P))
                    if full < KT:
                        tn = tiles[full][1]
                        ps = k.bank[4][0:tn, 0:P] if full == 0 else fifth(i)
                        last = v.tensor_copy(prob_T[0:tn, g % 2, full, j * P:(j + 1) * P], ps)
                    last.then_inc(copy_c.sem, 1)

                def divide(r, g):
                    b, a = g // 2, g % 2
                    dve.wait_ge(sum_c.sem, sum_c.at + r * nG + g + 1)
                    v.reciprocal(recip[rows(a), g % 2, :], k.bank[5][rows(1 - a), :]).then_inc(rec_c.sem, 1)
                    dve.wait_ge(rec_c.sem, rec_c.at + r * nG + g + 1)
                    v.tensor_tensor(heads_T[rows(a), b, :], k.bank[5][rows(a), :], recip[rows(a), g % 2, :], ALU.mult).then_inc(heads_c.sem, 1)

                def body(r, last_pair):
                    for i in range(nI + 1):
                        if i < nI:
                            maximum(r, i)
                        if i >= 1:
                            copy(r, i - 1)
                        if i >= 8 and i % TB == 0:
                            divide(r, i // TB - 2)
                    if not last_pair:
                        keys(r + 1)
                    divide(r, nG - 1)

                keys(0)
                pairs_of(dve, body)
    for c, n in ((vps_c, 2 * nV), (vd_c, nV), (va_c, nV), (ones_c, 2), (vpair_c, HP * nS), (qps_c, HP * B), (q_c, HP * B), (kps_c, HP * B), (k_c, HP * B),
                 (sum_c, HP * nG), (rec_c, HP * nG), (heads_c, HP * nG), (wo_used_c, HP), (wv_load_c, 16), (wqk_load_c, 32 * HP),
                 (wo_load_c, 16 * HP)):
        c.at += n
    for c in (score_c, max_c, prob_c, turned_c, copy_c):
        c.at += HP * nI


UNROLL = 16
HALF = UNROLL // 2
PRODUCTS = ((0, 2), (2, 0), (1, 1), (0, 1), (1, 0), (0, 0))
PARTS = 5


def chain(k, name):
    c = k.count(name)

    def link(eng, ins):
        ins.then_inc(c.sem, 1)
        c.at += 1
        eng.wait_ge(c.sem, c.at)
    return link


def recurrence(k):
    nc, w = k.nc, k.w
    with ExitStack() as ctx:
        def sb(name, shape, dt=F32):
            return k.sb(ctx, name, shape, dt)

        def sem(name):
            return k.count(name).sem

        def sems(name):
            return [sem(f"{name}{b}") for b in range(B)]

        xT = sb("gru_xT", [P, B, T])
        xg = sb("gru_xg", [P, T, 3, B])
        w_att = sb("gru_w_att", [P, 2, D])
        v_col = sb("gru_v", [P, 1])
        v_b = sb("gru_v_b", [P, P])
        wi = sb("gru_wi", [P, 2, 3, D])
        uh = sb("gru_uh", [P, 3, D])
        b_col = sb("gru_b", [P, 3])
        ep = sb("gru_ep", [P, B, S])
        uh_part = sb("gru_uh_parts", [P, 3, 3, D], BF16)
        uh_rest = sb("gru_uh_rest", [P, 3, D])
        ident_b = sb("gru_ident", [P, P], BF16)
        ep_part = sb("gru_ep_parts", [P, 3, B, S], BF16)
        ep_rest = sb("gru_ep_rest", [P, B, S])
        h_part = sb("gru_h_parts", [P, 3, B], BF16)
        h_rest = sb("gru_h_rest", [P, B])
        h_half = sb("gru_h_half", [P, B])
        tanh_s = sb("gru_tanh", [P, B, S])
        exp_s = sb("gru_exp", [P, B, S])
        junk = sb("gru_products", [P, 3, B, S])
        negmax = sb("gru_negmax", [P, B])
        esum = sb("gru_esum", [P, B])
        raw = sb("gru_raw", [P, 3, B])
        pre = sb("gru_pre", [P, 3, B])
        gate = sb("gru_gate", [P, 3, B])
        tzr = sb("gru_tzr", [P, 2, B])
        erec = sb("gru_erec", [P, B])
        cand = sb("gru_candidate", [P, B])
        ring = sb("gru_ring", [P, UNROLL, B])
        omz = sb("gru_1mz", [P, B])
        zh = sb("gru_zh", [P, B])
        hh = sb("gru_hh", [P, B])
        hT, ctxT, condT, ident, bank = k.hT, k.ctxT, k.condT, k.ident, k.bank

        HW_ps = [bank[4 * b][:, 0:S] for b in range(B)]
        S_ps = [bank[4 * b + 1][:, 0:S] for b in range(B)]
        U_ps = bank[2][:, 0:6].rearrange("p (g b) -> p g b", g=3)
        EW_ps = bank[3][:, 0:3 * B * S].rearrange("p (k b s) -> p k b s", k=3, b=B)

        s_ld, s_prep, s_h = sem("gru_loads"), sem("gru_prepared"), sems("gru_h")
        s_xgp, s_xg, s_epp, s_ep = sem("gru_xg_psum"), sem("gru_xg"), sem("gru_ep_psum"), sem("gru_ep")

        def state_of(u):
            return ring[:, u % UNROLL, :]

        layernorm(k, k.x_tok, P, NT, dst_T=lambda g: xT[:, g, :])

        with nc.Block() as block:
            @block.sync
            def _(sp):
                for dst, src in ((w_att[:], w["l0_w_att"]), (v_col[:], w["l0_v"]), (wi[:], w["l0_wi"]), (uh[:], w["l0_uh"]),
                                 (b_col[:], w["l0_b"])):
                    sp.dma_start(dst, src).then_inc(s_ld, 16)

            @block.vector
            def _(dve):
                dve.wait_ge(s_ld, 16 * 5)
                nc.vector.tensor_scalar(uh[:, 2, :], uh[:, 2, :], 0.5, None, ALU.mult).then_inc(s_prep, 1)
                nc.vector.tensor_scalar(v_b[:], k.ones[:, 0:P], v_col[:, 0:1], None, ALU.mult).then_inc(s_prep, 1)
                for b in range(B):
                    nc.vector.tensor_copy(state_of(-1)[:, b:b + 1], condT[:, b:b + 1]).then_inc(s_h[b], 1)
                dve.wait_ge(s_prep, 1)
                nc.vector.tensor_copy(uh_part[:, 0], uh[:]).then_inc(s_prep, 1)
                dve.wait_ge(s_prep, 3)
                nc.vector.tensor_tensor(uh_rest[:], uh[:], uh_part[:, 0], ALU.subtract).then_inc(s_prep, 1)
                dve.wait_ge(s_prep, 4)
                nc.vector.tensor_copy(uh_part[:, 1], uh_rest[:]).then_inc(s_prep, 1)
                dve.wait_ge(s_prep, 5)
                nc.vector.tensor_tensor(uh_part[:, 2], uh_rest[:], uh_part[:, 1], ALU.subtract).then_inc(s_prep, 1)
                nc.vector.tensor_copy(ident_b[:], ident[:])
                dve.wait_ge(s_epp, 1)
                nc.vector.tensor_copy(ep[:].rearrange("p b s -> p (b s)"), bank[0][:, 0:B * S]).then_inc(s_ep, 1)
                dve.wait_ge(s_ep, 1)
                nc.vector.tensor_copy(ep_part[:, 0], ep[:]).then_inc(s_ep, 1)
                dve.wait_ge(s_ep, 2)
                nc.vector.tensor_tensor(ep_rest[:], ep[:], ep_part[:, 0], ALU.subtract).then_inc(s_ep, 1)
                dve.wait_ge(s_ep, 3)
                nc.vector.tensor_copy(ep_part[:, 1], ep_rest[:]).then_inc(s_ep, 1)
                dve.wait_ge(s_ep, 4)
                nc.vector.tensor_tensor(ep_part[:, 2], ep_rest[:], ep_part[:, 1], ALU.subtract).then_inc(s_ep, 1)

            @block.scalar
            def _(act):
                for g in range(3):
                    for b in range(B):
                        act.wait_ge(s_xgp, g * B + b + 1)
                        nc.scalar.activation(xg[:, :, g, b], bank[2 + g * B + b], ACT.Identity, bias=b_col[:, g:g + 1]).then_inc(s_xg, 1)

            @block.tensor
            def _(pe):
                pe.wait_ge(s_ld, 16 * 5)
                for g in range(3):
                    for b in range(B):
                        nc.tensor.matmul(bank[2 + g * B + b], wi[:, 0, g, :], xT[:, b, :], start=True, stop=True).then_inc(s_xgp, 1)
                nc.tensor.matmul(bank[0][:, 0:B * S], w_att[:, 1, :], ctxT[:], start=True, stop=True).then_inc(s_epp, 1)
                pe.wait_ge(s_xg, 3 * B)
                for g in range(3):
                    nc.tensor.matmul(EW_ps[:, g, :, :], wi[:, 1, g, :], ctxT[:], start=True, stop=True)

        s_hw, s_tanh, s_score, s_max, s_exp = (sems("gru_" + x) for x in ("hw", "tanh", "score", "max", "exp"))
        s_raw, s_gate, s_tzr, s_zh, s_hh = (sems("gru_" + x) for x in ("raw", "gate", "tzr", "zh", "hh"))
        s_uh, s_part, s_pre, s_cand, s_kept = (sem("gru_" + x) for x in ("uh", "parts", "pre", "candidate", "kept"))

        with nc.Block() as block:
            @block.tensor
            def _(pe):
                mm = nc.tensor.matmul

                def step(t, u):
                    h = state_of(u - 1)
                    for b in range(B):
                        pe.wait_ge(s_h[b], t + 1)
                        mm(HW_ps[b], w_att[:, 0, :], h[:, b:b + 1].to_broadcast([P, S]), start=False, stop=True,
                           skip_group_check=True).then_inc(s_hw[b], 1)
                    for b in range(B):
                        pe.wait_ge(s_tanh[b], t + 1)
                        mm(S_ps[b], v_b[:], tanh_s[:, b, :], start=True, stop=True).then_inc(s_score[b], 1)
                    pe.wait_ge(s_part, PARTS * (t + 1))
                    for g in range(3):
                        for n, (i, j) in enumerate(PRODUCTS):
                            last = mm(U_ps[:, g, :], uh_part[:, i, g, :], h_part[:, j, :], start=(n == 0), stop=(n == len(PRODUCTS) - 1))
                    last.then_inc(s_uh, 1)
                    attended_context()

                def attended_context():
                    for b in range(B):
                        for j in range(3):
                            mm(HW_ps[b], ident_b[:], ep_part[:, j, b, :], start=(j == 0), stop=False, skip_group_check=True)

                attended_context()
                with pe.Fori(0, T // UNROLL) as i:
                    for u in range(UNROLL):
                        step(i * UNROLL + u, u)
                for b in range(B):
                    mm(HW_ps[b], k.zeros[:, 0:P], k.zeros[:, 0:S], start=False, stop=True, skip_group_check=True)

            @block.scalar
            def _(act):
                av = nc.scalar.activation

                def step(t, u):
                    for b in range(B):
                        act.wait_ge(s_hw[b], t + 1)
                        av(tanh_s[:, b, :], HW_ps[b], ACT.Tanh).then_inc(s_tanh[b], 1)
                    for b in range(B):
                        act.wait_ge(s_max[b], t + 1)
                        av(exp_s[:, b, :], S_ps[b], ACT.Exp, bias=negmax[:, b:b + 1], accum_out=esum[:, b:b + 1]).then_inc(s_exp[b], 1)
                    act.wait_ge(s_pre, t + 1)
                    av(cand[:], U_ps[:, 2, :], ACT.Copy).then_inc(s_cand, 1)
                    for b in range(B):
                        act.wait_ge(s_gate[b], t + 1)
                        av(tzr[:, :, b], gate[:, 0:2, b], ACT.Tanh, scale=0.5).then_inc(s_tzr[b], 1)
                        act.wait_ge(s_cand, t + 1)
                        act.wait_ge(s_tzr[b], t + 1)
                        av(hh[:, b:b + 1], tzr[:, 1, b:b + 1], ACT.Tanh, scale=cand[:, b:b + 1], bias=gate[:, 2, b:b + 1]).then_inc(s_hh[b], 1)

                with act.Fori(0, T // UNROLL) as i:
                    for u in range(UNROLL):
                        step(i * UNROLL + u, u)

            @block.gpsimd
            def _(pool):
                with pool.Fori(0, T // UNROLL) as i:
                    for u in range(UNROLL):
                        if (u + 1) % HALF == 0:
                            pool.wait_ge(s_h[0], i * UNROLL + u + 2)
                            pool.wait_ge(s_h[1], i * UNROLL + u + 2)
                            nc.gpsimd.tensor_copy(hT[:, bass.ds(i * UNROLL + (u + 1 - HALF), HALF), :],
                                                  ring[:, u + 1 - HALF:u + 1, :]).then_inc(s_kept, 1)

            @block.vector
            def _(dve):
                v = nc.vector

                def weigh(t, b, gates):
                    for g in gates:
                        last = v.tensor_tensor_reduce(junk[:, g, b, :], exp_s[:, b, :], EW_ps[:, g, b, :], 1.0, 0.0,
                                                      ALU.mult, ALU.add, raw[:, g, b:b + 1])
                    return last

                def gates_in(t, b):
                    dve.wait_ge(s_raw[b], 2 * t + 2)
                    v.scalar_tensor_tensor(out=gate[:, :, b], in0=raw[:, :, b], scalar=erec[:, b:b + 1], in1=pre[:, :, b],
                                           op0=ALU.mult, op1=ALU.add).then_inc(s_gate[b], 1)

                def update_gate(t, b):
                    dve.wait_ge(s_tzr[b], t + 1)
                    v.scalar_tensor_tensor(out=zh[:, b:b + 1], in0=tzr[:, 0, b:b + 1], scalar=1.0, in1=h_half[:, b:b + 1],
                                           op0=ALU.add, op1=ALU.mult).then_inc(s_zh[b], 1)
                    v.tensor_scalar(omz[:, b:b + 1], tzr[:, 0, b:b + 1], -0.5, 0.5, ALU.mult, ALU.add).then_inc(s_zh[b], 1)

                def state(t, u, b):
                    dve.wait_ge(s_zh[b], 2 * t + 2)
                    dve.wait_ge(s_hh[b], t + 1)
                    v.scalar_tensor_tensor(out=state_of(u)[:, b:b + 1], in0=hh[:, b:b + 1], scalar=omz[:, b:b + 1], in1=zh[:, b:b + 1],
                                           op0=ALU.mult, op1=ALU.add).then_inc(s_h[b], 1)

                def step(t, u):
                    h = state_of(u - 1)
                    dve.wait_ge(s_h[1], t + 1)
                    v.tensor_scalar(h_part[:, 0, :], h, 1.0, None, ALU.mult).then_inc(s_part, 1)
                    v.tensor_scalar(h_half[:], h, 0.5, None, ALU.mult).then_inc(s_part, 1)
                    dve.wait_ge(s_part, PARTS * t + 2)
                    v.tensor_tensor(h_rest[:], h, h_part[:, 0, :], ALU.subtract).then_inc(s_part, 1)
                    dve.wait_ge(s_part, PARTS * t + 3)
                    v.tensor_copy(h_part[:, 1, :], h_rest[:]).then_inc(s_part, 1)
                    dve.wait_ge(s_part, PARTS * t + 4)
                    v.tensor_tensor(h_part[:, 2, :], h_rest[:], h_part[:, 1, :], ALU.subtract).then_inc(s_part, 1)
                    for b in range(B):
                        dve.wait_ge(s_score[b], t + 1)
                        v.tensor_reduce(negmax[:, b:b + 1], S_ps[b], AX.X, ALU.max, negate=True).then_inc(s_max[b], 1)
                    dve.wait_ge(s_exp[0], t + 1)
                    v.reciprocal(erec[:, 0:1], esum[:, 0:1]).then_inc(s_raw[0], 1)
                    weigh(t, 0, (0, 1, 2)).then_inc(s_raw[0], 1)
                    dve.wait_ge(s_uh, t + 1)
                    v.tensor_tensor(pre[:], U_ps, xg[:, t, :, :], ALU.add).then_inc(s_pre, 1)
                    dve.wait_ge(s_exp[1], t + 1)
                    weigh(t, 1, (0,))
                    dve.wait_ge(s_pre, t + 1)
                    gates_in(t, 0)
                    v.reciprocal(erec[:, 1:2], esum[:, 1:2]).then_inc(s_raw[1], 1)
                    weigh(t, 1, (1, 2)).then_inc(s_raw[1], 1)
                    update_gate(t, 0)
                    gates_in(t, 1)
                    state(t, u, 0)
                    update_gate(t, 1)
                    state(t, u, 1)

                with dve.Fori(0, T // UNROLL) as i:
                    for u in range(UNROLL):
                        if u % HALF == 0:
                            dve.wait_ge(s_kept, 2 * i + u // HALF)
                        step(i * UNROLL + u, u)


def fold_butterflies(k, block, ctx):
    nc, w = k.nc, k.w
    F = 4 * D
    STAGES = 9
    wt = k.sb(ctx, "fly_w", [P, 2, 4, F // 2])
    y = k.sb(ctx, "fly_y", [P, 2, 2, F])
    prod = k.sb(ctx, "fly_products", [P, 4, 2, F // 2])
    load_c, step_c = k.count("fly_loads"), k.count("fly_step")

    @block.gpsimd
    def _(pool):
        done = 0
        for d, (rows, src) in enumerate(((2, "l1f_w_exp"), (1, "l1f_w_conT"))):
            pool.dma_start(y[:, 0, 0, :], w[src]).then_inc(load_c.sem, 16)
            done += 16
            if rows == 2:
                pool.dma_start(y[:, 0, 1, :], w["l1f_b_exp"].to_broadcast([P, F])).then_inc(load_c.sem, 16)
                done += 16
            for n in range(STAGES):
                g = n if d == 0 else STAGES - 1 - n
                s = 2 ** g
                pool.dma_start(wt[:, n % 2, :, :].rearrange("p c i -> p (c i)"),
                               w["l1f_fly"][d, g:g + 1, :].to_broadcast([P, 2 * F])).then_inc(load_c.sem, 16)
                done += 16
                pool.wait_ge(load_c.sem, load_c.at + done)

                def pairs(buf, side):
                    v = y[:, buf, 0:rows, :].rearrange("p r (n c s) -> p r n c s", c=2, s=s)
                    return v[:, :, :, side, :]

                for r in range(rows):
                    for c in range(4):
                        o, i = c // 2, c % 2
                        wc = wt[:, n % 2, 2 * o + i if d == 0 else 2 * i + o, :].rearrange("p (n s) -> p n s", s=s)
                        nc.gpsimd.tensor_tensor(prod[:, c, r, :].rearrange("p (n s) -> p n s", s=s), pairs(n % 2, i)[:, r], wc,
                                                ALU.mult).then_inc(step_c.sem, 1)
                        step_c.at += 1
                pool.wait_ge(step_c.sem, step_c.at)
                for r in range(rows):
                    for o in range(2):
                        nc.gpsimd.tensor_tensor(pairs((n + 1) % 2, o)[:, r],
                                                prod[:, 2 * o, r, :].rearrange("p (n s) -> p n s", s=s),
                                                prod[:, 2 * o + 1, r, :].rearrange("p (n s) -> p n s", s=s),
                                                ALU.add).then_inc(step_c.sem, 1)
                        step_c.at += 1
                pool.wait_ge(step_c.sem, step_c.at)
            out = k.fly_up if d == 0 else k.fly_downT
            nc.gpsimd.tensor_copy(out[:, 0:rows, :], y[:, STAGES % 2, 0:rows, :]).then_inc(step_c.sem, 1)
            step_c.at += 1
            pool.wait_ge(step_c.sem, step_c.at)
        load_c.at += done


def fold_ends(k):
    nc = k.nc
    with ExitStack() as ctx:
        down = k.sb(ctx, "fly_down", [P, 4, D])
        ps_c, sb_c, st_c = k.count("fold_psum"), k.count("fold_sbuf"), k.count("fold_stored")
        with nc.Block() as block:
            @block.tensor
            def _(pe):
                for f in range(4):
                    nc.tensor.transpose(k.bank[0][:, f * P:(f + 1) * P], k.fly_downT[:, 0, f * P:(f + 1) * P], k.ident[:])
                for f in range(4):
                    last = nc.tensor.matmul(k.bank[1][:, f:f + 1], k.fly_up[0:1, 1, f * P:(f + 1) * P], k.ones[0:1, 0:1],
                                            start=True, stop=True)
                last.then_inc(ps_c.sem, 1)

            @block.vector
            def _(dve):
                dve.wait_ge(ps_c.sem, ps_c.at + 1)
                nc.vector.tensor_copy(down[:].rearrange("p f d -> p (f d)"), k.bank[0]).then_inc(sb_c.sem, 1)
                nc.vector.tensor_tensor(k.fly_bias[:], k.bank[1][:, 0:4], k.cols["l1f_up_bias"], ALU.add).then_inc(sb_c.sem, 1)

            @block.sync
            def _(sp):
                sp.dma_start(k.d_fly_up[0], k.fly_up[:, 0, :]).then_inc(st_c.sem, 16)
                sp.wait_ge(sb_c.sem, sb_c.at + 2)
                sp.dma_start(k.d_fly_down[0].rearrange("f p d -> p f d"), down[:]).then_inc(st_c.sem, 16)
                sp.wait_ge(st_c.sem, st_c.at + 32)
        ps_c.at += 1
        sb_c.at += 2
        st_c.at += 32


def router(k, x_T, w_r, E, top, over_all, comb, comb_T=None):
    nc = k.nc
    tri = k.tri[:].rearrange("p (e j) -> p e j", e=16)[:, 0:E, 0:E]
    link = chain(k, "router_step")
    psum_c, exp_c, comb_c, back_c, turned_c, sb_c, st_c = (k.count("router_" + x) for x in ("psum", "exp", "comb", "sub", "turned", "sbuf",
                                                                                             "stored"))
    with ExitStack() as ctx:
        lg = k.sb(ctx, "router_logits", [P, NT, E])
        d_s = k.sb(ctx, "router_shifted", [P, NT, E])
        ex = k.sb(ctx, "router_exp", [P, NT, E])
        gt = k.sb(ctx, "router_gt", [P, NT, E, E])
        ge = k.sb(ctx, "router_ge", [P, NT, E, E])
        m = k.sb(ctx, "router_max", [P, NT])
        z = k.sb(ctx, "router_sum", [P, NT])
        zr = k.sb(ctx, "router_recip", [P, NT])
        rank = k.sb(ctx, "router_rank", [P, NT, E])
        cT = comb_T if comb_T is not None else k.sb(ctx, "router_comb_T", [P, B * T])
        with nc.Block() as block:
            @block.tensor
            def _(pe):
                for j in range(NT):
                    last = nc.tensor.matmul(k.bank[0][:, j * E:(j + 1) * E], x_T[:, j * P:(j + 1) * P], w_r, start=True, stop=True)
                last.then_inc(psum_c.sem, 1)
                pe.wait_ge(comb_c.sem, comb_c.at + 1)
                for j in range(NT):
                    last = nc.tensor.transpose(k.bank[1 + j // TB][0:E, (j % TB) * P:(j % TB + 1) * P], ex[:, j, :], k.ident[:])
                last.then_inc(turned_c.sem, 1)

            @block.vector
            def _(dve):
                v = nc.vector

                def wide(a):
                    return a.unsqueeze(2).to_broadcast([P, NT, E])

                dve.wait_ge(psum_c.sem, psum_c.at + 1)
                link(dve, v.tensor_copy(lg[:].rearrange("p t e -> p (t e)"), k.bank[0][:, 0:NT * E]))
                link(dve, v.tensor_reduce(m[:], lg[:], AX.X, ALU.max))
                v.tensor_tensor(d_s[:], lg[:], wide(m[:]), ALU.subtract).then_inc(back_c.sem, 1)
                dve.wait_ge(exp_c.sem, exp_c.at + 1)
                ranked = lg
                if over_all:
                    link(dve, v.tensor_reduce(z[:], ex[:], AX.X, ALU.add))
                    link(dve, v.reciprocal(zr[:], z[:]))
                    link(dve, v.tensor_tensor(ex[:], ex[:], wide(zr[:]), ALU.mult))
                    ranked = ex
                for t in range(NT):
                    other = ranked[:, t, :].unsqueeze(1).to_broadcast([P, E, E])
                    own = ranked[:, t, :].unsqueeze(2).to_broadcast([P, E, E])
                    v.tensor_tensor(gt[:, t], other, own, ALU.is_gt)
                    last = v.tensor_tensor(ge[:, t], other, own, ALU.is_ge)
                link(dve, last)
                for t in range(NT):
                    last = v.tensor_tensor(ge[:, t], ge[:, t], tri, ALU.mult)
                link(dve, last)
                for t in range(NT):
                    last = v.tensor_tensor(gt[:, t], gt[:, t], ge[:, t], ALU.max)
                link(dve, last)
                for t in range(NT):
                    last = v.tensor_reduce(rank[:, t, :], gt[:, t], AX.X, ALU.add)
                link(dve, last)
                link(dve, v.tensor_scalar(rank[:], rank[:], float(top), None, ALU.is_lt))
                link(dve, v.tensor_tensor(ex[:], ex[:], rank[:], ALU.mult))
                link(dve, v.tensor_reduce(z[:], ex[:], AX.X, ALU.add))
                if over_all:
                    link(dve, v.tensor_scalar(z[:], z[:], 1e-12, None, ALU.max))
                link(dve, v.reciprocal(zr[:], z[:]))
                v.tensor_tensor(ex[:], ex[:], wide(zr[:]), ALU.mult).then_inc(comb_c.sem, 1)
                dve.wait_ge(turned_c.sem, turned_c.at + 1)
                for b in range(B):
                    v.tensor_copy(cT[0:E, b * T:(b + 1) * T], k.bank[1 + b][0:E, :]).then_inc(sb_c.sem, 1)

            @block.scalar
            def _(act):
                act.wait_ge(back_c.sem, back_c.at + 1)
                nc.scalar.activation(ex[:], d_s[:], ACT.Exp).then_inc(exp_c.sem, 1)

            @block.sync
            def _(sp):
                sp.wait_ge(sb_c.sem, sb_c.at + B)
                sp.dma_start(comb, cT[0:E, :]).then_inc(st_c.sem, 16)
                sp.wait_ge(st_c.sem, st_c.at + 16)
    for c, n in ((psum_c, 1), (exp_c, 1), (comb_c, 1), (back_c, 1), (turned_c, 1), (sb_c, B), (st_c, 16)):
        c.at += n


def project(k, x_T, weight, out, func=ACT.Identity, bias=0.0, scale=1.0):
    nc = k.nc
    ps_c, out_c = k.count("project_psum"), k.count("project_out")
    with nc.Block() as block:
        @block.tensor
        def _(pe):
            for b in range(B):
                nc.tensor.matmul(k.bank[b], weight, x_T[:, b, :], start=True, stop=True).then_inc(ps_c.sem, 1)

        @block.scalar
        def _(act):
            for b in range(B):
                act.wait_ge(ps_c.sem, ps_c.at + b + 1)
                nc.scalar.activation(out[:, b, :], k.bank[b], func, bias=bias, scale=scale).then_inc(out_c.sem, 1)
    ps_c.at += B
    out_c.at += B


def slots(k):
    nc, w = k.nc, k.w
    link = chain(k, "slot_step")
    ld_c, ps_c, out_c, max_c, exp_c, att_c, upd_c = (k.count("slot_" + x) for x in ("loads", "psum", "out", "max", "exp", "att", "upd"))
    cols = k.cols
    with ExitStack() as ctx:
        ws = k.sb(ctx, "slot_w", [P, 6, D])
        rows = k.sb(ctx, "slot_rows", [P, 5, D])
        cond_r = k.sb(ctx, "slot_cond", [P, B, D])
        els = k.sb(ctx, "slot_exp", [P, D])
        sl = k.sb(ctx, "slot_slots", [P, NT, D])
        cT = k.sb(ctx, "slot_ctx_T", [P, B, S])
        kT = k.sb(ctx, "slot_k", [P, B, S])
        vt = k.sb(ctx, "slot_v", [P, B, D])
        a_T = k.sb(ctx, "slot_a", [P, B, T])
        q_T = k.sb(ctx, "slot_q", [P, B, T])
        e_s = k.sb(ctx, "slot_e", [P, B, T])
        negmax = k.sb(ctx, "slot_negmax", [P, B])
        esum = k.sb(ctx, "slot_esum", [P, B])
        crec = k.sb(ctx, "slot_crec", [P, B, T])
        upd = k.sb(ctx, "slot_upd", [P, B, T])
        bq = k.sb(ctx, "slot_bq", [P, 1])
        WK, WV, WQ, WU, W1, W2 = range(6)
        BV, LS, MU, PG, PB = range(5)
        root = float(D) ** 0.5

        layernorm(k, k.ctx_tok, S, B, dst_T=lambda g: cT[:, g, :], affine=[(cols["lnkv_g"], cols["lnkv_b"])] * B, group=1)
        layernorm(k, k.x_tok, P, NT, dst=sl)
        with nc.Block() as block:
            @block.sync
            def _(sp):
                sp.dma_start(ws[:], w["l2_w"]).then_inc(ld_c.sem, 16)
                sp.dma_start(rows[:].rearrange("p n d -> p (n d)"), w["l2_rows"].to_broadcast([P, 5 * D])).then_inc(ld_c.sem, 16)
                sp.dma_start(cond_r[:].rearrange("p b d -> p (b d)"), w["cond_row"].to_broadcast([P, B * D])).then_inc(ld_c.sem, 16)

            @block.scalar
            def _(act):
                act.wait_ge(ld_c.sem, ld_c.at + 48)
                nc.scalar.activation(els[:], rows[:, LS, :], ACT.Exp).then_inc(exp_c.sem, 1)
                nc.scalar.activation(bq[:], cols["l2_bq"], ACT.Copy, scale=root).then_inc(exp_c.sem, 1)
                act.wait_ge(ps_c.sem, ps_c.at + 1)
                nc.scalar.activation(kT[:].rearrange("p b s -> p (b s)"), k.bank[0][:, 0:B * S], ACT.Identity, bias=cols["l2_bk"])

            @block.tensor
            def _(pe):
                pe.wait_ge(ld_c.sem, ld_c.at + 48)
                nc.tensor.matmul(k.bank[0][:, 0:B * S], ws[:, WK, :], cT[:].rearrange("p b s -> p (b s)"), start=True,
                                 stop=True).then_inc(ps_c.sem, 1)
                for b in range(B):
                    nc.tensor.matmul(k.bank[1 + b][0:S, 0:D], cT[:, b, :], ws[:, WV, :], start=True, stop=True).then_inc(ps_c.sem, 1)

            @block.vector
            def _(dve):
                v = nc.vector
                dve.wait_ge(ld_c.sem, ld_c.at + 48)
                for b in range(B):
                    dve.wait_ge(ps_c.sem, ps_c.at + 2 + b)
                    v.tensor_tensor(vt[0:S, b, :], k.bank[1 + b][0:S, 0:D], rows[0:S, BV, :], ALU.add)
                dve.wait_ge(exp_c.sem, exp_c.at + 1)
                link(dve, v.tensor_tensor(sl[:], sl[:], els[:].unsqueeze(1).to_broadcast([P, NT, D]), ALU.mult))
                link(dve, v.tensor_tensor(sl[:], sl[:], rows[:, MU, :].unsqueeze(1).to_broadcast([P, NT, D]), ALU.add))
        ld_c.at += 48
        ps_c.at += 3
        exp_c.at += 2
        for _ in range(3):
            layernorm(k, sl, P, NT, dst_T=lambda g: a_T[:, g, :], affine=[(cols["lnq_g"], cols["lnq_b"])] * B)
            project(k, a_T, ws[:, WQ, :], q_T, bias=bq[:, 0:1], scale=root)
            with nc.Block() as block:
                @block.tensor
                def _(pe):
                    for b in range(B):
                        nc.tensor.matmul(k.bank[b][0:S, :], kT[:, b, :], q_T[:, b, :], start=True, stop=True).then_inc(ps_c.sem, 1)
                    for b in range(B):
                        pe.wait_ge(att_c.sem, att_c.at + b + 1)
                        nc.tensor.matmul(k.bank[2 + b], k.ones[0:S, 0:P], e_s[0:S, b, :], start=True, stop=True).then_inc(ps_c.sem, 1)
                        nc.tensor.matmul(k.bank[4 + b], vt[0:S, b, :], e_s[0:S, b, :], start=True, stop=True).then_inc(ps_c.sem, 1)
                    for b in range(B):
                        pe.wait_ge(upd_c.sem, upd_c.at + b + 1)
                        nc.tensor.matmul(k.bank[6 + b], ws[:, WU, :], upd[:, b, :], start=True, stop=True)

                @block.scalar
                def _(act):
                    for b in range(B):
                        act.wait_ge(max_c.sem, max_c.at + b + 1)
                        nc.scalar.activation(e_s[0:S, b, :], k.bank[b][0:S, :], ACT.Exp, bias=negmax[0:S, b:b + 1],
                                             accum_out=esum[0:S, b:b + 1]).then_inc(exp_c.sem, 1)

                @block.vector
                def _(dve):
                    v = nc.vector
                    for b in range(B):
                        dve.wait_ge(ps_c.sem, ps_c.at + b + 1)
                        v.tensor_reduce(negmax[0:S, b:b + 1], k.bank[b][0:S, :], AX.X, ALU.max, negate=True).then_inc(max_c.sem, 1)
                    for b in range(B):
                        dve.wait_ge(exp_c.sem, exp_c.at + b + 1)
                        link(dve, v.reciprocal(esum[0:S, b:b + 1], esum[0:S, b:b + 1]))
                        v.tensor_scalar(e_s[0:S, b, :], e_s[0:S, b, :], esum[0:S, b:b + 1], 1e-8, ALU.mult, ALU.add).then_inc(att_c.sem, 1)
                    for b in range(B):
                        dve.wait_ge(ps_c.sem, ps_c.at + B + 2 * b + 2)
                        link(dve, v.reciprocal(crec[:, b, :], k.bank[2 + b]))
                        v.tensor_tensor(upd[:, b, :], k.bank[4 + b], crec[:, b, :], ALU.mult).then_inc(upd_c.sem, 1)
            ps_c.at += 3 * B
            exp_c.at += B
            max_c.at += B
            att_c.at += B
            upd_c.at += B
            turn_and_add(k, k.bank[6:8], sl, bias=cols["l2_bu"])
            layernorm(k, sl, P, NT, dst_T=lambda g: a_T[:, g, :], affine=[(cols["lnm_g"], cols["lnm_b"])] * B)
            project(k, a_T, ws[:, W1, :], q_T, func=ACT.Gelu, bias=cols["l2_b1"])
            project(k, q_T, ws[:, W2, :], upd, bias=cols["l2_b2"])
            turn_and_add(k, [upd[:, b, :] for b in range(B)], sl)
            with nc.Block() as block:
                @block.vector
                def _(dve):
                    for b in range(B):
                        nc.vector.tensor_tensor(sl[:, b * TB:(b + 1) * TB, :], sl[:, b * TB:(b + 1) * TB, :],
                                                cond_r[:, b, :].unsqueeze(1).to_broadcast([P, TB, D]), ALU.add)
            layernorm(k, sl, P, NT, dst=sl)
            with nc.Block() as block:
                @block.vector
                def _(dve):
                    v = nc.vector
                    link(dve, v.tensor_tensor(sl[:], sl[:], rows[:, PG, :].unsqueeze(1).to_broadcast([P, NT, D]), ALU.mult))
                    link(dve, v.tensor_tensor(sl[:], sl[:], rows[:, PB, :].unsqueeze(1).to_broadcast([P, NT, D]), ALU.add))
        with nc.Block() as block:
            @block.vector
            def _(dve):
                nc.vector.tensor_tensor(k.x_tok[:], k.x_tok[:], sl[:], ALU.add)


COLS = ("l1_bo1", "l1_bo2", "l1_ff_b2", "lnkv_g", "lnkv_b", "lnq_g", "lnq_b", "lnm_g", "lnm_b", "l2_bk", "l2_bq", "l2_bu", "l2_b1",
        "l2_b2", "ln1_w", "ln1_b", "ln2_w", "ln2_b", "l1f_b_con", "l1f_down_bias")


def program(nc, w, out, stages=99):
    ctx = ExitStack()
    with ctx:
        k = Core(nc, ctx, w)
        k.x_tok = k.sb(ctx, "x_tok", [P, NT, D])
        k.y_tok = k.sb(ctx, "y_tok", [P, NT, D])
        k.y_T = k.sb(ctx, "y_T", [P, B * T])
        k.hT = k.sb(ctx, "h_T", [P, T, B])
        k.ident = k.sb(ctx, "ident", [P, P])
        k.ones = k.sb(ctx, "ones", [P, T])
        k.zeros = k.sb(ctx, "zeros", [P, P])
        k.eps = k.sb(ctx, "eps", [P, 1])
        k.tri = k.sb(ctx, "tri", [P, 256])
        k.ctxT = k.sb(ctx, "ctx_T", [P, B, S])
        k.ctx_tok = k.sb(ctx, "ctx_tok", [P, B, D])
        k.condT = k.sb(ctx, "cond_T", [P, B])
        k.fly_up = k.sb(ctx, "fly_up", [P, 2, 4 * D])
        k.fly_downT = k.sb(ctx, "fly_downT", [P, 1, 4 * D])
        k.fly_bias = k.sb(ctx, "fly_bias", [P, 4])
        cols = k.sb(ctx, "cols", [P, len(COLS)])
        many = k.sb(ctx, "many", [P, 4 + 8 + 6])
        bo = k.sb(ctx, "bo_rows", [1, 2, D])
        k.cols = {n: cols[:, i:i + 1] for i, n in enumerate(COLS)}
        k.cols["l1f_up_bias"] = many[:, 0:4]
        ff_b1, norm_b = many[:, 4:12], many[:, 12:18]
        norm_w = k.sb(ctx, "norm_w", [P, 3, 2, D])
        aff = k.sb(ctx, "adaln", [P, 3, 2, B])
        aff3 = k.sb(ctx, "l3_affine", [P, 2, B])
        con_b = k.sb(ctx, "con_b", [P, 1])
        gates = k.sb(ctx, "router_w", [P, 24])
        k.d_fly_up = nc.dram_tensor("fly_up_dram", [1, D, 4 * D], F32, kind="Internal").ap()
        k.d_fly_down = nc.dram_tensor("fly_down_dram", [1, 4, P, D], F32, kind="Internal").ap()
        d_comb2 = nc.dram_tensor("comb2_dram", [8, B * T], F32, kind="Internal").ap()
        d_comb3 = nc.dram_tensor("comb3_dram", [16, B * T], F32, kind="Internal").ap()
        ld_c, ps_c, set_c = k.count("setup_loads"), k.count("setup_psum"), k.count("setup_memory")
        link = chain(k, "setup_step")
        loads = ((k.x_tok[:], w["x"]), (k.ident[:], w["ident"]), (k.tri[:], w["tri"].to_broadcast([P, 256])), (k.ctxT[:], w["ctxT"]),
                 (k.ctx_tok[0:S], w["ctx_tok"]), (k.condT[:], w["condT"]), (cols[:], w["cols"]), (many[:], w["many"]),
                 (bo[:], w["bo_rows"]), (norm_w[:], w["norm_w"]), (gates[:], w["router_w"]))
        with nc.Block() as block:
            @block.sync
            def _(sp):
                for dst, src in loads:
                    sp.dma_start(dst, src).then_inc(ld_c.sem, 16)

            @block.gpsimd
            def _(pool):
                nc.gpsimd.memset(k.ones[:], 1.0)
                nc.gpsimd.memset(k.zeros[:], 0.0)

            @block.tensor
            def _(pe):
                pe.wait_ge(ld_c.sem, 16 * len(loads))
                for n in range(3):
                    for s in range(2):
                        o = (n * 2 + s) * B
                        last = nc.tensor.matmul(k.bank[0][:, o:o + B], norm_w[:, n, s, :], k.condT[:], start=True, stop=True)
                last.then_inc(ps_c.sem, 1)

            @block.vector
            def _(dve):
                v = nc.vector
                v.memset(k.eps[:], 1e-5)
                dve.wait_ge(ps_c.sem, 1)
                dve.wait_ge(ld_c.sem, 16 * len(loads))
                link(dve, v.tensor_tensor(aff[:].rearrange("p n s b -> p (n s) b"), k.bank[0][:, 0:6 * B].rearrange("p (n b) -> p n b", b=B),
                                          norm_b.unsqueeze(2).to_broadcast([P, 6, B]), ALU.add))
                link(dve, v.tensor_scalar(aff[:, :, 0, :], aff[:, :, 0, :], 1.0, None, ALU.add))
                link(dve, v.tensor_scalar(aff3[:, 0, :], k.condT[:], 1.0, None, ALU.add))
                link(dve, v.tensor_scalar(aff3[:, 1, :], aff3[:, 0, :], k.cols["ln2_b"], None, ALU.mult))
                link(dve, v.tensor_tensor(aff3[:, 1, :], aff3[:, 1, :], k.condT[:], ALU.add))
                link(dve, v.tensor_scalar(aff3[:, 0, :], aff3[:, 0, :], k.cols["ln2_w"], None, ALU.mult))
                link(dve, v.tensor_tensor(con_b[:], k.cols["l1f_b_con"], k.cols["l1f_down_bias"], ALU.add))

        def y_of(b=None):
            return lambda g: k.y_T[:, g * T:(g + 1) * T]

        y_bt = k.y_T[:].rearrange("p (b t) -> p b t", b=B)
        ones = [k.ones[0:1, :]] * B
        zero = k.zeros[0:1, 0:P]

        if stages >= 1:
            recurrence(k)
            h = [k.hT[:, :, b] for b in range(B)]
            turn_and_add(k, h, k.x_tok)
        if stages >= 2:
            layernorm(k, k.x_tok, P, NT, dst_T=y_of())
            mlp(k, k.y_T, 8, [P] * 4, w["l0_wg"], w["l0_wu"], w["l0_wd"], ACT.Silu, last=zero, last_rhs=ones,
                aside=fold_butterflies)
            turn_and_add(k, k.bank[4:6], k.x_tok)
        if stages >= 3:
            def adaptive(n):
                return [(aff[:, n, 0, b:b + 1], aff[:, n, 1, b:b + 1]) for b in range(B)]
            layernorm(k, k.x_tok, P, NT, dst=k.y_tok)
            layernorm(k, k.y_tok, P, NT, dst_T=y_of(), affine=adaptive(0))
            attention(k, y_bt, y_bt, T, w["a1_wq"], w["a1_wk"], w["a1_wv"], w["a1_wo"], bo[0:1, 0, :])
            turn_and_add(k, k.bank[6:8], k.y_tok)
            layernorm(k, k.y_tok, P, NT, dst_T=y_of(), affine=adaptive(1))
            attention(k, y_bt, k.ctxT[:], S, w["a2_wq"], w["a2_wk"], w["a2_wv"], w["a2_wo"], bo[0:1, 1, :])
            turn_and_add(k, k.bank[6:8], k.y_tok)
            layernorm(k, k.y_tok, P, NT, dst_T=y_of(), affine=adaptive(2))
            mlp(k, k.y_T, 1, [P] * 4, w["ff_wg"], w["ff_wa"], w["ff_w2"], ACT.Gelu, gate_bias=lambda f: ff_b1[:, 4 + f:5 + f],
                up_bias=lambda f: ff_b1[:, f:f + 1], last=zero, last_rhs=ones)
            turn_and_add(k, k.bank[4:6], k.y_tok, bias=k.cols["l1_ff_b2"], dst2=k.x_tok)
        if stages >= 4:
            fold_ends(k)
            layernorm(k, k.x_tok, P, NT, dst_T=y_of())
            mlp(k, k.y_T, 1, [P] * 4, k.d_fly_up, None, k.d_fly_down, ACT.Gelu, gate_bias=lambda f: k.fly_bias[:, f:f + 1],
                last=zero, last_rhs=ones)
            turn_and_add(k, k.bank[4:6], k.x_tok, bias=con_b[:, 0:1])
        if stages >= 5:
            slots(k)
        if stages >= 6:
            layernorm(k, k.x_tok, P, NT, dst_T=y_of())
            router(k, k.y_T, gates[:, 0:8], 8, 2, False, d_comb2)
            mlp(k, k.y_T, 1, [P, 64], w["sg_gate"], w["sg_up"], w["sg_down"], ACT.Silu, last=zero, last_rhs=ones)
            turn_and_add(k, k.bank[4:6], k.x_tok)
            mlp(k, k.y_T, 8, [P, 64], w["l2_wg"], w["l2_wu"], w["l2_wd"], ACT.Silu, comb=d_comb2, last=zero, last_rhs=ones)
            turn_and_add(k, k.bank[4:6], k.x_tok)
        if stages >= 7:
            with ExitStack() as c2:
                kv = k.sb(c2, "l3_kv", [P, B, T + S])
                layernorm(k, k.x_tok, P, NT, dst=k.y_tok)
                layernorm(k, k.y_tok, P, NT, dst_T=lambda g: kv[:, g, 0:T], affine=[(aff3[:, 0, b:b + 1], aff3[:, 1, b:b + 1])
                                                                                    for b in range(B)])
                layernorm(k, k.ctx_tok, S, B, dst_T=lambda g: kv[:, g, T:T + S], affine=[(k.cols["ln1_w"], k.cols["ln1_b"])] * B,
                          group=1)
                attention(k, kv[:, :, 0:T], kv[:], T + S, w["a3_wq"], w["a3_wk"], w["a3_wv"], w["a3_wo"], zero)
                turn_and_add(k, k.bank[6:8], k.x_tok)
        if stages >= 8:
            with ExitStack() as c2:
                comb_T = k.sb(c2, "l3_comb_T", [P, B * T])
                b2 = k.sb(c2, "l3_b2", [16, D])
                layernorm(k, k.x_tok, P, NT, dst_T=y_of())
                router(k, k.y_T, gates[:, 8:24], 16, 3, True, d_comb3, comb_T)
                with nc.Block() as block:
                    @block.sync
                    def _(sp):
                        sp.dma_start(b2[:], w["l3_b2"]).then_inc(ld_c.sem, 16)
                        sp.wait_ge(ld_c.sem, 16 * len(loads) + 16)
                mlp(k, k.y_T, 16, [P] * 2, w["l3_w1"], None, w["l3_w2"], ACT.Relu,
                    gate_bias="columns", comb=d_comb3, last=b2[:], last_rhs=[comb_T[0:16, b * T:(b + 1) * T] for b in range(B)])
                turn_and_add(k, k.bank[4:6], k.x_tok)
        st_c = k.count("output_stored")
        with nc.Block() as block:
            @block.sync
            def _(sp):
                sp.dma_start(out, k.x_tok[:]).then_inc(st_c.sem, 16)
                sp.wait_ge(st_c.sem, 16)


def layouts(a):
    c = np.ascontiguousarray
    r = {
        "x": c(a["x"].reshape(NT, P, D).transpose(1, 0, 2)),
        "ident": np.eye(P, dtype=np.float32),
        "tri": np.tril(np.ones((16, 16), np.float32), -1).reshape(1, 256),
        "ctxT": c(a["ctx_1024"].transpose(2, 0, 1)),
        "ctx_tok": c(a["ctx_1024"].transpose(1, 0, 2)),
        "condT": c(a["cond_1024"].T),
        "cond_row": c(a["cond_1024"].reshape(1, B * D)),
        "l0_w_att": c(a["L0_xcond_W_att"].reshape(2, P, D).transpose(1, 0, 2)),
        "l0_v": a["L0_xcond_V_att"],
        "l0_wi": c(a["L0_xcond_Wi"].reshape(2, P, 3, D).transpose(1, 0, 2, 3)),
        "l0_uh": c(a["L0_xcond_Uh"].reshape(P, 3, D)),
        "l0_b": c(a["L0_xcond_b"].reshape(3, P).T),
        "l0_wg": a["L0_ffn_Wg"],
        "l0_wu": a["L0_ffn_Wu"],
        "l0_wd": c(a["L0_ffn_Wd"].reshape(8, 4, P, D)),
        "norm_w": c(np.stack([a[f"L1_xcond_norm{n}_w"].reshape(P, 2, D) for n in (1, 2, 3)], axis=1)),
        "bo_rows": c(np.stack([a["L1_xcond_attn1_bo"], a["L1_xcond_attn2_bo"]])[None]),
        "ff_wa": c(a["L1_xcond_ff_w1"][None, :, 0:4 * D]),
        "ff_wg": c(a["L1_xcond_ff_w1"][None, :, 4 * D:8 * D]),
        "ff_w2": c(a["L1_xcond_ff_w2"].reshape(1, 4, P, D)),
        "l1f_w_exp": a["L1_ffn_W_exp"],
        "l1f_w_conT": c(a["L1_ffn_W_con"].T),
        "l1f_b_exp": c(a["L1_ffn_b_exp"][None]),
        "l1f_fly": c(np.stack([a["L1_ffn_up_weights"], a["L1_ffn_down_weights"]]).transpose(0, 1, 3, 4, 2).reshape(2, 9, 8 * D)),
        "l2_w": c(np.stack([a["L2_xcond_w" + n] for n in "kvqu12"], axis=1)),
        "l2_rows": c(np.concatenate([a["L2_xcond_bv"], a["L2_xcond_q_logsig"][0, 0], a["L2_xcond_q_mu"][0, 0], a["L2_xcond_lnp_g"],
                                     a["L2_xcond_lnp_b"]])[None]),
        "l3_w1": c(np.concatenate([a["L3_ffn_W1"], a["L3_ffn_b1"].reshape(16, 2, P).transpose(0, 2, 1)], axis=2)),
        "l3_w2": c(a["L3_ffn_W2"].reshape(16, 2, P, D)),
        "l3_b2": a["L3_ffn_b2"],
        "router_w": c(np.concatenate([a["L2_ffn_gate_w"].T, a["L3_ffn_gate"]], axis=1)),
    }
    for n, (q, kk, v, o) in (("a1", [a[f"L1_xcond_attn1_w{x}"] for x in "qkvo"]), ("a2", [a[f"L1_xcond_attn2_w{x}"] for x in "qkvo"]),
                             ("a3", [a["L3_xcond_Wq"].T, a["L3_xcond_Wkv"][0:HEADS * DH].T, a["L3_xcond_Wkv"][HEADS * DH:].T,
                                     a["L3_xcond_Wo"].T])):
        r[n + "_wq"] = c(q.reshape(D, HP, P).transpose(1, 0, 2))
        r[n + "_wk"] = c(kk.reshape(D, HP, P).transpose(1, 0, 2))
        r[n + "_wv"] = c(v)
        r[n + "_wo"] = c(o.reshape(HP, P, D))
    up, down = a["L2_ffn_w_up"], a["L2_ffn_w_down"]
    r["l2_wg"] = c(up[:, 0:192].transpose(0, 2, 1))
    r["l2_wu"] = c(up[:, 192:].transpose(0, 2, 1))
    r["sg_gate"] = c(a["L2_ffn_sg_gate"].T[None])
    r["sg_up"] = c(a["L2_ffn_sg_up"].T[None])
    for n, x in (("l2_wd", down.transpose(0, 2, 1)), ("sg_down", a["L2_ffn_sg_down"].T[None])):
        padded = np.zeros((x.shape[0], 256, D), np.float32)
        padded[:, 0:192] = x
        r[n] = padded.reshape(-1, 2, P, D)
    src = {"l1_bo1": "L1_xcond_attn1_bo", "l1_bo2": "L1_xcond_attn2_bo", "l1_ff_b2": "L1_xcond_ff_b2", "l1f_b_con": "L1_ffn_b_con",
           "l1f_down_bias": "L1_ffn_down_bias"}
    for n in COLS:
        src.setdefault(n, ("L2_xcond_" + n[3:]) if n.startswith("l2_") else ("L3_xcond_" + n) if n[2] in "12" else "L2_xcond_" + n)
    r["cols"] = c(np.stack([a[src[n]] for n in COLS], axis=1))
    r["many"] = c(np.concatenate([a["L1_ffn_up_bias"].reshape(4, P).T, a["L1_xcond_ff_b1"].reshape(8, P).T]
                                 + [a[f"L1_xcond_norm{n}_b"].reshape(2, P).T for n in (1, 2, 3)], axis=1))
    return r


STAGES_RUN = 99


def kernel(**inputs):
    import concourse.bacc as bacc
    from concourse.bass_utils import run_bass_kernel_spmd as run
    arrays = {"in_" + n: v for n, v in layouts({n: np.asarray(v) for n, v in inputs.items()}).items()}
    nc = bacc.Bacc("TRN2", target_bir_lowering=False, num_devices=1)
    w = {n[3:]: nc.dram_tensor(n, v.shape, mybir.dt.from_np(v.dtype), kind="ExternalInput").ap() for n, v in arrays.items()}
    out = nc.dram_tensor("out", (P, NT, D), F32, kind="ExternalOutput").ap()
    program(nc, w, out, STAGES_RUN)
    r = run(nc, [arrays], core_ids=[0])
    return np.ascontiguousarray(r.results[0]["out"].transpose(1, 0, 2)).reshape(B, T, D)
```

```python
from contextlib import ExitStack

import concourse.bass as bass
import numpy as np
from concourse import mybir

P = 128
B, T, D = 2, 512, 128
NT = B * T // P
TB = T // P
S = 77
HEADS, DH = 16, 64
HP = HEADS // 2
F32 = mybir.dt.float32
BF16 = mybir.dt.bfloat16
ALU = mybir.AluOpType
ACT = mybir.ActivationFunctionType
AX = mybir.AxisListType


class Count:

    def __init__(self, sem):
        self.sem, self.at = sem, 0


class Core:

    def __init__(self, nc, ctx, w):
        self.nc, self.ctx, self.w = nc, ctx, w
        self.counts = {}
        self.pair = [ctx.enter_context(nc.psum_tensor(f"pair{i}", [P, 1024], F32)) for i in range(4)]
        self.bank = [self.pair[i // 2][:, (i % 2) * 512:(i % 2) * 512 + 512] for i in range(8)]
        self.n = 0

    def count(self, name):
        if name not in self.counts:
            self.counts[name] = Count(self.ctx.enter_context(self.nc.semaphore(name)))
        return self.counts[name]

    def sb(self, ctx, name, shape, dt=F32):
        self.n += 1
        return ctx.enter_context(self.nc.sbuf_tensor(f"{name}_{self.n}", shape, dt))


def layernorm(k, src, rows, n, dst=None, dst_T=None, affine=None, group=TB):
    nc = k.nc
    stats_c, sd_c, xn_c, turned_c, out_c = (k.count(x) for x in ("ln_stats", "ln_deviation", "ln_normal", "ln_turned", "ln_out"))
    groups = n // group
    with ExitStack() as ctx:
        stats = k.sb(ctx, "ln_stats", [P, n, 6])
        mv = k.sb(ctx, "ln_mv", [P, n, 2])
        sd = k.sb(ctx, "ln_sd", [P, n])
        rstd = k.sb(ctx, "ln_rstd", [P, n])
        xn = dst if dst is not None else k.sb(ctx, "ln_xn", [P, n, D])
        with nc.Block() as block:
            @block.vector
            def _(dve):
                for j in range(n):
                    nc.vector.bn_stats(stats[0:rows, j, :], src[0:rows, j, :]).then_inc(stats_c.sem, 1)
                for j in range(n):
                    dve.wait_ge(stats_c.sem, stats_c.at + j + 1)
                    nc.vector.bn_aggr(mv[0:rows, j, :], stats[0:rows, j, :]).then_inc(stats_c.sem, 1)
                dve.wait_ge(sd_c.sem, sd_c.at + 1)
                nc.vector.reciprocal(rstd[0:rows, :], sd[0:rows, :]).then_inc(stats_c.sem, 1)
                dve.wait_ge(stats_c.sem, stats_c.at + 2 * n + 1)
                for j in range(n):
                    nc.vector.tensor_scalar(xn[0:rows, j, :], src[0:rows, j, :], mv[0:rows, j, 0:1], rstd[0:rows, j:j + 1],
                                            ALU.subtract, ALU.mult).then_inc(xn_c.sem, 1)
                if dst_T is not None:
                    for g in range(1, groups, 2):
                        dve.wait_ge(turned_c.sem, turned_c.at + g + 1)
                        out = dst_T(g)
                        ps = k.bank[g][:, 0:group * rows]
                        if affine is None:
                            nc.vector.tensor_copy(out, ps).then_inc(out_c.sem, 1)
                        else:
                            nc.vector.tensor_scalar(out, ps, affine[g][0], affine[g][1], ALU.mult, ALU.add).then_inc(out_c.sem, 1)

            @block.scalar
            def _(act):
                act.wait_ge(stats_c.sem, stats_c.at + 2 * n)
                nc.scalar.activation(sd[0:rows, :], mv[0:rows, :, 1], ACT.Sqrt, bias=k.eps[0:rows, 0:1]).then_inc(sd_c.sem, 1)
                if dst_T is not None:
                    for g in range(0, groups, 2):
                        act.wait_ge(turned_c.sem, turned_c.at + g + 1)
                        out = dst_T(g)
                        ps = k.bank[g][:, 0:group * rows]
                        if affine is None:
                            nc.scalar.activation(out, ps, ACT.Copy).then_inc(out_c.sem, 1)
                        else:
                            nc.scalar.activation(out, ps, ACT.Identity, scale=affine[g][0], bias=affine[g][1]).then_inc(out_c.sem, 1)

            if dst_T is not None:
                @block.tensor
                def _(pe):
                    for j in range(n):
                        pe.wait_ge(xn_c.sem, xn_c.at + j + 1)
                        c = j % group
                        last = nc.tensor.transpose(k.bank[j // group][:, c * rows:(c + 1) * rows], xn[0:rows, j, :],
                                                   k.ident[0:rows, 0:rows])
                        if c == group - 1:
                            last.then_inc(turned_c.sem, 1)
    stats_c.at += 2 * n + 1
    sd_c.at += 1
    xn_c.at += n
    if dst_T is not None:
        turned_c.at += groups
        out_c.at += groups


def turn_and_add(k, src_T, dst, bias=None, dst2=None, scale=None):
    nc = k.nc
    flat_c, turned_c, out_c = (k.count(x) for x in ("add_flat", "add_turned", "add_out"))
    with ExitStack() as ctx:
        flat = k.sb(ctx, "add_flat", [P, B, T])
        with nc.Block() as block:
            @block.scalar
            def _(act):
                for b in range(B):
                    if bias is None:
                        nc.scalar.activation(flat[:, b, :], src_T[b], ACT.Copy).then_inc(flat_c.sem, 1)
                    else:
                        nc.scalar.activation(flat[:, b, :], src_T[b], ACT.Identity, bias=bias).then_inc(flat_c.sem, 1)

            @block.tensor
            def _(pe):
                for b in range(B):
                    pe.wait_ge(flat_c.sem, flat_c.at + b + 1)
                    for c in range(TB):
                        last = nc.tensor.transpose(k.bank[b][:, c * P:(c + 1) * P], flat[:, b, c * P:(c + 1) * P], k.ident[:])
                    last.then_inc(turned_c.sem, 1)

            @block.vector
            def _(dve):
                for b in range(B):
                    dve.wait_ge(turned_c.sem, turned_c.at + b + 1)
                    ps = k.bank[b].rearrange("p (c d) -> p c d", c=TB)
                    if scale is None:
                        last = nc.vector.tensor_tensor(dst[:, b * TB:(b + 1) * TB, :], dst[:, b * TB:(b + 1) * TB, :], ps, ALU.add)
                    else:
                        for c in range(TB):
                            j = b * TB + c
                            last = nc.vector.scalar_tensor_tensor(out=dst[:, j, :], in0=ps[:, c, :], scalar=scale[:, j:j + 1],
                                                                  in1=dst[:, j, :], op0=ALU.mult, op1=ALU.add)
                    last.then_inc(out_c.sem, 1)
                    if dst2 is not None:
                        dve.wait_ge(out_c.sem, out_c.at + b + 1)
                        nc.vector.tensor_tensor(dst2[:, b * TB:(b + 1) * TB, :], dst2[:, b * TB:(b + 1) * TB, :],
                                                dst[:, b * TB:(b + 1) * TB, :], ALU.add)
    flat_c.at += B
    turned_c.at += B
    out_c.at += B


def mlp(k, x_T, experts, widths, gate, up, down, func, gate_bias=None, up_bias=None, comb=None, last=None, last_rhs=None,
        aside=None):
    nc = k.nc
    F = sum(widths)
    nf = len(widths)
    per = 2 if experts > 1 else 1
    U = nf * B
    units = [(s, f, b) for s in range(per) for f in range(nf) for b in range(B)]
    nU = len(units)
    loads = (2 + (up is not None) + (comb is not None)) * 16
    names = ("mlp_gate", "mlp_up", "mlp_act", "mlp_mul", "mlp_hidden", "mlp_down", "mlp_opened")
    gate_c, up_c, act_c, mul_c, hid_c, down_c, open_c = (k.count(x) for x in names)
    if comb is None:
        hid_c = act_c if up is None else mul_c
    load_c = [k.count(f"mlp_loads{s}") for s in range(2)]
    acc = k.bank[4:6]
    rounds = experts // per
    with ExitStack() as ctx:
        G = F + (nf if gate_bias == "columns" else 0)
        wg = k.sb(ctx, "mlp_wg", [P, per, G])
        wu = k.sb(ctx, "mlp_wu", [P, per, F]) if up is not None else None
        wd = k.sb(ctx, "mlp_wd", [P, per, nf, D])
        cb = k.sb(ctx, "mlp_cb", [P, per, B, T]) if comb is not None else None
        a_s = k.sb(ctx, "mlp_act", [P, 2, T])
        m_s = k.sb(ctx, "mlp_mul", [P, 2, T]) if (up is not None and comb is not None) else None
        h_s = k.sb(ctx, "mlp_hidden", [P, 3, T])
        hid_buf = h_s if (up is not None or comb is not None) else None

        def load(q, e, s):
            q.dma_start(wg[:, s, :], gate[e]).then_inc(load_c[s].sem, 16)
            if up is not None:
                q.dma_start(wu[:, s, :], up[e]).then_inc(load_c[s].sem, 16)
            if comb is not None:
                q.dma_start(cb[:, s, :, :].rearrange("p b t -> p (b t)"), comb[e:e + 1, :].to_broadcast([P, B * T]) if isinstance(e, int)
                            else comb[bass.ds(e, 1), :].to_broadcast([P, B * T])).then_inc(load_c[s].sem, 16)
            q.dma_start(wd[:, s, :, :], down[e].rearrange("f p d -> p f d")).then_inc(load_c[s].sem, 16)

        def rounds_of(eng, body):
            if rounds == 1:
                body(0)
            else:
                with eng.Fori(0, rounds) as r:
                    body(r)

        with nc.Block() as block:
            if aside is not None:
                @block.gpsimd
                def _(pool):
                    aside(pool, ctx)

            @block.sync
            def _(sp):
                for s in range(per):
                    load(sp, s, s)
                if rounds > 1:
                    with sp.Fori(0, rounds - 1) as r:
                        for s in range(per):
                            sp.wait_ge(down_c.sem, down_c.at + r * nU + (s + 1) * U)
                            load(sp, (r + 1) * per + s, s)

            @block.tensor
            def _(pe):
                for b in range(B):
                    nc.tensor.matmul(acc[b], k.zeros[0:1, 0:P], k.ones[0:1, :], start=True, stop=False, skip_group_check=True)

                def down_product(r, q):
                    s, f, b = units[q]
                    m = widths[f]
                    pe.wait_ge(hid_c.sem, hid_c.at + r * nU + q + 1)
                    nc.tensor.matmul(acc[b], wd[0:m, s, f, :], h_s[0:m, q % 3, :], start=False, stop=False,
                                     skip_group_check=True).then_inc(down_c.sem, 1)

                def body(r):
                    for q, (s, f, b) in enumerate(units):
                        m, f0 = widths[f], sum(widths[:f])
                        if q % U == 0:
                            pe.wait_ge(load_c[s].sem, load_c[s].at + (r + 1) * loads)
                        if q >= 2:
                            pe.wait_ge(act_c.sem, act_c.at + r * nU + q - 1)
                        nc.tensor.matmul(k.bank[q % 2][0:m, :], wg[:, s, f0:f0 + m], x_T[:, b * T:(b + 1) * T], start=True,
                                         stop=True).then_inc(gate_c.sem, 1)
                        if up is not None:
                            if q >= 2:
                                pe.wait_ge(mul_c.sem, mul_c.at + r * nU + q - 1)
                            nc.tensor.matmul(k.bank[2 + q % 2][0:m, :], wu[:, s, f0:f0 + m], x_T[:, b * T:(b + 1) * T],
                                             start=True, stop=True).then_inc(up_c.sem, 1)
                        if q >= 2:
                            down_product(r, q - 2)
                    for q in range(max(nU - 2, 0), nU):
                        down_product(r, q)

                rounds_of(pe, body)
                for b in range(B):
                    nc.tensor.matmul(acc[b], last, last_rhs[b], start=False, stop=True, skip_group_check=True)

            @block.scalar
            def _(act):
                def body(r):
                    for q, (s, f, b) in enumerate(units):
                        m = widths[f]
                        act.wait_ge(gate_c.sem, gate_c.at + r * nU + q + 1)
                        if hid_buf is None:
                            if q >= 3:
                                act.wait_ge(down_c.sem, down_c.at + r * nU + q - 2)
                            out = h_s[0:m, q % 3, :]
                        else:
                            if q >= 2:
                                act.wait_ge(mul_c.sem if up is not None else hid_c.sem,
                                            (mul_c.at if up is not None else hid_c.at) + r * nU + q - 1)
                            out = a_s[0:m, q % 2, :]
                        if gate_bias == "columns":
                            bias = wg[:, s, F + f:F + f + 1]
                        else:
                            bias = gate_bias(f) if gate_bias is not None else 0.0
                        nc.scalar.activation(out, k.bank[q % 2][0:m, :], func, bias=bias).then_inc(act_c.sem, 1)

                rounds_of(act, body)

            if up is not None:
                @block.vector
                def _(dve):
                    def body(r):
                        for q, (s, f, b) in enumerate(units):
                            m = widths[f]
                            dve.wait_ge(act_c.sem, act_c.at + r * nU + q + 1)
                            dve.wait_ge(up_c.sem, up_c.at + r * nU + q + 1)
                            if comb is None:
                                if q >= 3:
                                    dve.wait_ge(down_c.sem, down_c.at + r * nU + q - 2)
                                out = h_s[0:m, q % 3, :]
                            else:
                                if q >= 2:
                                    dve.wait_ge(hid_c.sem, hid_c.at + r * nU + q - 1)
                                out = m_s[0:m, q % 2, :]
                            if up_bias is None:
                                i = nc.vector.tensor_tensor(out, k.bank[2 + q % 2][0:m, :], a_s[0:m, q % 2, :], ALU.mult)
                            else:
                                i = nc.vector.scalar_tensor_tensor(out=out, in0=k.bank[2 + q % 2][0:m, :], scalar=up_bias(f),
                                                                   in1=a_s[0:m, q % 2, :], op0=ALU.add, op1=ALU.mult)
                            i.then_inc(mul_c.sem, 1)

                    rounds_of(dve, body)

            if comb is not None:
                @block.gpsimd
                def _(pool):
                    def body(r):
                        for q, (s, f, b) in enumerate(units):
                            m = widths[f]
                            if q % U == 0:
                                pool.wait_ge(load_c[s].sem, load_c[s].at + (r + 1) * loads)
                            src = m_s if up is not None else a_s
                            c = mul_c if up is not None else act_c
                            pool.wait_ge(c.sem, c.at + r * nU + q + 1)
                            if q >= 3:
                                pool.wait_ge(down_c.sem, down_c.at + r * nU + q - 2)
                            nc.gpsimd.tensor_tensor(h_s[0:m, q % 3, :], src[0:m, q % 2, :], cb[0:m, s, b, :],
                                                    ALU.mult).then_inc(hid_c.sem, 1)

                    rounds_of(pool, body)
    n = rounds * nU
    for c in (gate_c, act_c, down_c):
        c.at += n
    if comb is not None:
        hid_c.at += n
    if up is not None:
        up_c.at += n
        mul_c.at += n
    for s in range(per):
        load_c[s].at += rounds * loads


def attention(k, q_T, kv_T, nk, wq, wk, wv, wo, warm=0):
    nc = k.nc
    tiles = [(i * P, min(P, nk - i * P)) for i in range((nk + P - 1) // P)]
    KT = len(tiles)
    parts = [(0, min(nk, 512))] + ([(512, nk - 512)] if nk > 512 else [])
    J = TB if TB * nk <= T else 1
    items = [(b, a, j) for b in range(B) for a in range(2) for j in range(0, TB, J)]
    nI = len(items)
    nG = B * 2
    GI = TB // J
    LAG = 2
    names = ("att_v_psum", "att_v_dve", "att_v_act", "att_zeros", "att_v_pair", "att_q_psum", "att_q", "att_k_psum", "att_k", "att_score", "att_max",
             "att_exp", "att_recip", "att_prob", "att_turned", "att_turned_copy", "att_sum", "att_heads", "att_wo_used", "att_out_added", "att_wv_load",
             "att_wqk_load", "att_wo_load")
    (vps_c, vd_c, va_c, zeros_c, vpair_c, qps_c, q_c, kps_c, k_c, score_c, max_c, exp_c, rec_c, prob_c, turned_c, copy_c, sum_c, heads_c, wo_used_c, out_c,
     wv_load_c, wqk_load_c, wo_load_c) = (k.count(x) for x in names)
    part = [k.bank[6], k.bank[5]]
    with ExitStack() as ctx:
        wq_s = k.sb(ctx, "att_wq", [P, P])
        wk_s = k.sb(ctx, "att_wk", [P, P])
        wo_s = k.sb(ctx, "att_wo", [P, P])
        wv_s = k.sb(ctx, "att_wv", [P, HEADS * DH])
        v_all = k.sb(ctx, "att_v", [P, B, KT, HEADS, DH])
        v_pair = k.sb(ctx, "att_v_pair", [P, B, KT, 4 * DH])
        qh = k.sb(ctx, "att_q", [P, 2, B, T])
        kh = k.sb(ctx, "att_k", [P, B, nk])
        ex = k.sb(ctx, "att_exp", [P, 2, J, nk])
        prob = k.sb(ctx, "att_prob", [P, 2, J, nk])
        prob_T = k.sb(ctx, "att_prob_T", [P, 2, KT, T])
        esum = k.sb(ctx, "att_esum", [P, 2, J])
        erec = k.sb(ctx, "att_erec", [P, 2, J])
        heads_T = k.sb(ctx, "att_heads_T", [P, B, T])
        negmax = k.sb(ctx, "att_negmax", [P, 2, J])

        def scores_of(i):
            return k.pair[i % 2][:, 0:J * nk].rearrange("p (j s) -> p j s", j=J)

        def rows(a):
            return slice(DH * a, DH * a + DH)

        v_jobs = [(b, t, c) for b in range(B) for t in range(KT) for c in range(2)]
        nV = len(v_jobs) // 2

        def pairs_of(eng, body):
            with eng.Fori(0, HP - 1) as r:
                body(r, False)
            body(HP - 1, True)

        def values_of(n):
            b, t, c = v_jobs[n]
            return v_all[0:tiles[t][1], b, t, 8 * c:8 * c + 8, :].rearrange("p h d -> p (h d)"), k.bank[n % 4][0:tiles[t][1], :]

        full = sum(tn == P for _, tn in tiles)
        spans = ([(P, 0, full)] if full else []) + ([(tiles[full][1], full, KT)] if full < KT else [])
        nS = nG * len(spans)

        with nc.Block() as block:
            @block.sync
            def _(sp):
                sp.dma_start(wv_s[:], wv).then_inc(wv_load_c.sem, 16)
                sp.dma_start(wq_s[:], wq[0]).then_inc(wqk_load_c.sem, 16)
                sp.dma_start(wk_s[:], wk[0]).then_inc(wqk_load_c.sem, 16)
                sp.dma_start(wo_s[:], wo[0]).then_inc(wo_load_c.sem, 16)
                with sp.Fori(0, HP - 1) as r:
                    sp.wait_ge(kps_c.sem, kps_c.at + r * B + B)
                    sp.dma_start(wq_s[:], wq[r + 1]).then_inc(wqk_load_c.sem, 16)
                    sp.dma_start(wk_s[:], wk[r + 1]).then_inc(wqk_load_c.sem, 16)
                    sp.wait_ge(wo_used_c.sem, wo_used_c.at + r * B + B)
                    sp.dma_start(wo_s[:], wo[r + 1]).then_inc(wo_load_c.sem, 16)

            @block.gpsimd
            def _(pool):
                nc.gpsimd.memset(k.att_out[:], 0.0).then_inc(zeros_c.sem, 1)
                nc.gpsimd.memset(qh[:], 0.0).then_inc(zeros_c.sem, 1)
                nc.gpsimd.memset(v_pair[:, :, :, DH:3 * DH], 0.0).then_inc(zeros_c.sem, 1)
                pool.wait_ge(vd_c.sem, vd_c.at + nV)
                pool.wait_ge(va_c.sem, va_c.at + nV)

                def values(r, g):
                    b, a = g // 2, g % 2
                    for m, t0, t1 in spans:
                        nc.gpsimd.tensor_copy(v_pair[0:m, b, t0:t1, 3 * a * DH:(3 * a + 1) * DH],
                                              v_all[0:m, b, t0:t1, 2 * r + a, :]).then_inc(vpair_c.sem, 1)

                with pool.Fori(0, HP) as r:
                    for i in range(nI):
                        if i >= 2:
                            pool.wait_ge(turned_c.sem, turned_c.at + r * nI + i - 1)
                        pool.wait_ge(rec_c.sem, rec_c.at + r * nI + i + 1)
                        nc.gpsimd.tensor_tensor(prob[:, i % 2], ex[:, i % 2], erec[:, i % 2, :].unsqueeze(2).to_broadcast([P, J, nk]),
                                                ALU.mult).then_inc(prob_c.sem, 1)
                        if GI == 1:
                            values(r, i)
                        elif i % 2 == 1 and i // 2 < nG:
                            values(r, i // 2)

            @block.tensor
            def _(pe):
                mm = nc.tensor.matmul
                pe.wait_ge(wv_load_c.sem, wv_load_c.at + 16)
                for n, (b, t, c) in enumerate(v_jobs):
                    t0, tn = tiles[t]
                    if n >= 4:
                        side = va_c if n % 2 else vd_c
                        pe.wait_ge(side.sem, side.at + n // 2 - 1)
                    mm(k.bank[n % 4][0:tn, :], kv_T[:, b, t0:t0 + tn], wv_s[:, c * 512:(c + 1) * 512], start=True,
                       stop=True).then_inc(vps_c.sem, 1)
                pe.wait_ge(vd_c.sem, vd_c.at + nV)
                pe.wait_ge(va_c.sem, va_c.at + nV)
                pe.wait_ge(zeros_c.sem, zeros_c.at + 3)

                def keep_warm(n):
                    for _ in range(n):
                        mm(k.bank[1], k.warm[:, 0:P], k.warm[:], start=True, stop=True)

                def project_pair(r):
                    pe.wait_ge(wqk_load_c.sem, wqk_load_c.at + r * 32 + 32)
                    for b in range(B):
                        mm(k.bank[2 * b], wq_s[:], q_T[:, b, :], start=True, stop=True).then_inc(qps_c.sem, 1)
                    for b in range(B):
                        pe.wait_ge(q_c.sem, q_c.at + r * B + b + 1)
                        for s0, sn in parts:
                            last = mm(k.pair[b][:, s0:s0 + sn], wk_s[:], kv_T[:, b, s0:s0 + sn], start=True, stop=True)
                        last.then_inc(kps_c.sem, 1)

                def scores(r, i):
                    b, a, j = items[i]
                    if i < 2:
                        pe.wait_ge(k_c.sem, k_c.at + r * B + B)
                    else:
                        pe.wait_ge(exp_c.sem, exp_c.at + r * nI + i - 1)
                    for n in range(J):
                        for s0, sn in parts:
                            last = mm(k.pair[i % 2][:, n * nk + s0:n * nk + s0 + sn], qh[:, a, b, (j + n) * P:(j + n + 1) * P],
                                      kh[:, b, s0:s0 + sn], start=True, stop=True)
                    last.then_inc(score_c.sem, 1)

                def turn(r, i):
                    if i >= 1:
                        pe.wait_ge(copy_c.sem, copy_c.at + r * nI + i)
                    pe.wait_ge(prob_c.sem, prob_c.at + r * nI + i + 1)
                    for n in range(J):
                        for t, (t0, tn) in enumerate(tiles):
                            out = k.bank[4][0:tn, (t + n) * P:(t + n + 1) * P] if t < 4 else k.bank[7][0:tn, 0:P]
                            last = nc.tensor.transpose(out, prob[:, i % 2, n, t0:t0 + tn], k.ident[:])
                    last.then_inc(turned_c.sem, 1)

                def weigh(r, g, ts):
                    b, a = g // 2, g % 2
                    if 0 in ts:
                        pe.wait_ge(copy_c.sem, copy_c.at + r * nI + (g + 1) * GI)
                        pe.wait_ge(vpair_c.sem, vpair_c.at + r * nS + (g + 1) * len(spans))
                        if g == 2:
                            pe.wait_ge(heads_c.sem, heads_c.at + r * B + 1)
                    for t in ts:
                        tn = tiles[t][1]
                        last = mm(k.bank[5], v_pair[0:tn, b, t, a * 2 * DH:(a + 1) * 2 * DH], prob_T[0:tn, g % 2, t, :],
                                  start=(a == 0 and t == 0), stop=(a == 1 and t == KT - 1))
                    if a == 1 and KT - 1 in ts:
                        last.then_inc(sum_c.sem, 1)

                def body(r, last_pair):
                    for i in range(LAG, nI + LAG):
                        if i < nI:
                            scores(r, i)
                        turn(r, i - LAG)
                        g, step = (i - GI - LAG) // GI, (i - GI - LAG) % GI
                        ts = [t for t in range(KT) if min(t, GI - 1) == step]
                        if g >= 0 and ts:
                            weigh(r, g, ts)
                        keep_warm(warm)
                    if not last_pair:
                        project_pair(r + 1)
                    weigh(r, nG - 1, list(range(KT)))
                    if not last_pair:
                        scores(r + 1, 0)
                        scores(r + 1, 1)
                    pe.wait_ge(wo_load_c.sem, wo_load_c.at + r * 16 + 16)
                    pe.wait_ge(heads_c.sem, heads_c.at + r * B + B)
                    for b in range(B):
                        mm(part[b], wo_s[:], heads_T[:, b, :], start=True, stop=True).then_inc(wo_used_c.sem, 1)

                project_pair(0)
                scores(0, 0)
                scores(0, 1)
                pairs_of(pe, body)

            @block.scalar
            def _(act):
                for n in range(1, 2 * nV, 2):
                    act.wait_ge(vps_c.sem, vps_c.at + n + 1)
                    nc.scalar.activation(*values_of(n), ACT.Copy).then_inc(va_c.sem, 1)
                act.wait_ge(zeros_c.sem, zeros_c.at + 2)

                def queries(r):
                    for b in range(B):
                        act.wait_ge(qps_c.sem, qps_c.at + r * B + b + 1)
                        for a in range(2):
                            last = nc.scalar.activation(qh[rows(a), a, b, :], k.bank[2 * b][rows(a), :], ACT.Copy, scale=DH ** -0.5)
                        last.then_inc(q_c.sem, 1)

                def heads(r, b):
                    act.wait_ge(sum_c.sem, sum_c.at + r * B + b + 1)
                    nc.scalar.activation(heads_T[:, b, :], k.bank[5], ACT.Copy).then_inc(heads_c.sem, 1)

                def body(r, last_pair):
                    for i in range(nI):
                        if i >= 2:
                            act.wait_ge(prob_c.sem, prob_c.at + r * nI + i - 1)
                        act.wait_ge(max_c.sem, max_c.at + r * nI + i + 1)
                        for n in range(J):
                            last = nc.scalar.activation(ex[:, i % 2, n, :], scores_of(i)[:, n, :], ACT.Exp, bias=negmax[:, i % 2, n:n + 1],
                                                        accum_out=esum[:, i % 2, n:n + 1])
                        last.then_inc(exp_c.sem, 1)
                        if i == min(3 * GI + 1, nI - 1):
                            heads(r, 0)
                    if not last_pair:
                        queries(r + 1)
                    heads(r, 1)

                queries(0)
                pairs_of(act, body)

            @block.vector
            def _(dve):
                v = nc.vector
                for n in range(0, 2 * nV, 2):
                    dve.wait_ge(vps_c.sem, vps_c.at + n + 1)
                    v.tensor_copy(*values_of(n)).then_inc(vd_c.sem, 1)

                def keys(r):
                    for b in range(B):
                        dve.wait_ge(kps_c.sem, kps_c.at + r * B + b + 1)
                        v.tensor_copy(kh[:, b, :], k.pair[b][:, 0:nk]).then_inc(k_c.sem, 1)

                def maximum(r, i):
                    dve.wait_ge(score_c.sem, score_c.at + r * nI + i + 1)
                    v.tensor_reduce(negmax[:, i % 2, :], scores_of(i), AX.X, ALU.max, negate=True).then_inc(max_c.sem, 1)

                def copy(r, i):
                    g, j = i // GI, i % GI
                    dve.wait_ge(turned_c.sem, turned_c.at + r * nI + i + 1)
                    if full:
                        last = v.tensor_copy(prob_T[:, g % 2, 0:full, j * P:(j + 1) * P],
                                             k.bank[4][:, 0:full * P].rearrange("p (t q) -> p t q", q=P))
                    if full < KT:
                        tn = tiles[full][1]
                        ps = k.bank[4][0:tn, 0:J * P] if full == 0 else k.bank[7][0:tn, 0:P]
                        last = v.tensor_copy(prob_T[0:tn, g % 2, full, j * P:(j + J) * P], ps)
                    last.then_inc(copy_c.sem, 1)

                def body(r, last_pair):
                    for i in range(1, nI + LAG):
                        if 2 <= i < nI:
                            maximum(r, i)
                        if i <= nI:
                            dve.wait_ge(exp_c.sem, exp_c.at + r * nI + i)
                            n = (i - 1) % 2
                            v.reciprocal(erec[:, n, :], esum[:, n, :]).then_inc(rec_c.sem, 1)
                        if i >= LAG:
                            copy(r, i - LAG)
                    if not last_pair:
                        keys(r + 1)
                        maximum(r + 1, 0)
                        maximum(r + 1, 1)
                    for b in range(B):
                        dve.wait_ge(wo_used_c.sem, wo_used_c.at + r * B + b + 1)
                        v.tensor_tensor(k.att_out[:, b, :], k.att_out[:, b, :], part[b], ALU.add).then_inc(out_c.sem, 1)
                    dve.wait_ge(out_c.sem, out_c.at + r * B + B)

                keys(0)
                maximum(0, 0)
                maximum(0, 1)
                pairs_of(dve, body)
    for c, n in ((vps_c, 2 * nV), (vd_c, nV), (va_c, nV), (zeros_c, 3), (vpair_c, HP * nS), (qps_c, HP * B), (q_c, HP * B), (kps_c, HP * B), (k_c, HP * B),
                 (sum_c, HP * B), (heads_c, HP * B), (out_c, HP * B), (wo_used_c, HP * B), (wv_load_c, 16), (wqk_load_c, 32 * HP),
                 (wo_load_c, 16 * HP)):
        c.at += n
    for c in (score_c, max_c, exp_c, rec_c, prob_c, turned_c, copy_c):
        c.at += HP * nI


UNROLL = 32
HALF = UNROLL // 2
WARM = (0, 9)
PRODUCTS = ((0, 2), (2, 0), (1, 1), (0, 1), (1, 0), (0, 0))


def chain(k, name):
    c = k.count(name)

    def link(eng, ins):
        ins.then_inc(c.sem, 1)
        c.at += 1
        eng.wait_ge(c.sem, c.at)
    return link


def recurrence(k):
    nc, w = k.nc, k.w
    with ExitStack() as ctx:
        def sb(name, shape, dt=F32):
            return k.sb(ctx, name, shape, dt)

        def sem(name):
            return k.count(name).sem

        def sems(name):
            return [sem(f"{name}{b}") for b in range(B)]

        xT = sb("gru_xT", [P, B, T])
        xg = sb("gru_xg", [P, T, 3, B])
        w_att = sb("gru_w_att", [P, 2, D])
        v_col = sb("gru_v", [P, 1])
        v_b = sb("gru_v_b", [P, P])
        wi = sb("gru_wi", [P, 2, 3, D])
        uh = sb("gru_uh", [P, 3, D])
        b_col = sb("gru_b", [P, 3])
        ep = sb("gru_ep", [P, B, S])
        uh_part = sb("gru_uh_parts", [P, 3, 3, D], BF16)
        uh_rest = sb("gru_uh_rest", [P, 3, D])
        ident_b = sb("gru_ident", [P, P], BF16)
        ep_part = sb("gru_ep_parts", [P, 3, B, S], BF16)
        ep_rest = sb("gru_ep_rest", [P, B, S])
        h_part = sb("gru_h_parts", [P, 3, B], BF16)
        h_rest = sb("gru_h_rest", [P, B])
        h_half = sb("gru_h_half", [P, B])
        tanh_s = sb("gru_tanh", [P, B, S])
        exp_s = sb("gru_exp", [P, B, S])
        junk = sb("gru_products", [P, 3, B, S])
        negmax = sb("gru_negmax", [P, B])
        esum = sb("gru_esum", [P, B])
        raw = sb("gru_raw", [P, 3, B])
        pre = sb("gru_pre", [P, 3, B])
        gate = sb("gru_gate", [P, 3, B])
        tzr = sb("gru_tzr", [P, 2, B])
        erec = sb("gru_erec", [P, B])
        cand = sb("gru_candidate", [P, B])
        free = sb("gru_free", [P, 1])
        ring = sb("gru_ring", [P, UNROLL, B])
        omz = sb("gru_1mz", [P, B])
        zh = sb("gru_zh", [P, B])
        hh = sb("gru_hh", [P, B])
        hT, ctxT, condT, ident, bank = k.hT, k.ctxT, k.condT, k.ident, k.bank

        HW_ps = [bank[4 * b][:, 0:S] for b in range(B)]
        S_ps = [bank[4 * b + 1][:, 0:S] for b in range(B)]
        U_ps = bank[2][:, 0:6].rearrange("p (g b) -> p g b", g=3)
        EW_ps = bank[3][:, 0:3 * B * S].rearrange("p (k b s) -> p k b s", k=3, b=B)

        s_ld, s_prep, s_h = sem("gru_loads"), sem("gru_prepared"), sems("gru_h")
        s_xgp, s_xg, s_epp, s_ep = sem("gru_xg_psum"), sem("gru_xg"), sem("gru_ep_psum"), sem("gru_ep")

        def state_of(u):
            return ring[:, u % UNROLL, :]

        layernorm(k, k.x_tok, P, NT, dst_T=lambda g: xT[:, g, :])

        with nc.Block() as block:
            @block.sync
            def _(sp):
                for dst, src in ((w_att[:], w["l0_w_att"]), (v_col[:], w["l0_v"]), (wi[:], w["l0_wi"]), (uh[:], w["l0_uh"]),
                                 (b_col[:], w["l0_b"])):
                    sp.dma_start(dst, src).then_inc(s_ld, 16)

            @block.vector
            def _(dve):
                dve.wait_ge(s_ld, 16 * 5)
                nc.vector.tensor_scalar(uh[:, 2, :], uh[:, 2, :], 0.5, None, ALU.mult).then_inc(s_prep, 1)
                nc.vector.tensor_scalar(v_b[:], k.ones[:, 0:P], v_col[:, 0:1], None, ALU.mult).then_inc(s_prep, 1)
                for b in range(B):
                    nc.vector.tensor_copy(state_of(-1)[:, b:b + 1], condT[:, b:b + 1]).then_inc(s_h[b], 1)
                dve.wait_ge(s_prep, 1)
                nc.vector.tensor_copy(uh_part[:, 0], uh[:]).then_inc(s_prep, 1)
                dve.wait_ge(s_prep, 3)
                nc.vector.tensor_tensor(uh_rest[:], uh[:], uh_part[:, 0], ALU.subtract).then_inc(s_prep, 1)
                dve.wait_ge(s_prep, 4)
                nc.vector.tensor_copy(uh_part[:, 1], uh_rest[:]).then_inc(s_prep, 1)
                dve.wait_ge(s_prep, 5)
                nc.vector.tensor_tensor(uh_part[:, 2], uh_rest[:], uh_part[:, 1], ALU.subtract).then_inc(s_prep, 1)
                nc.vector.tensor_copy(ident_b[:], ident[:])
                dve.wait_ge(s_epp, 1)
                nc.vector.tensor_copy(ep[:].rearrange("p b s -> p (b s)"), bank[0][:, 0:B * S]).then_inc(s_ep, 1)
                dve.wait_ge(s_ep, 1)
                nc.vector.tensor_copy(ep_part[:, 0], ep[:]).then_inc(s_ep, 1)
                dve.wait_ge(s_ep, 2)
                nc.vector.tensor_tensor(ep_rest[:], ep[:], ep_part[:, 0], ALU.subtract).then_inc(s_ep, 1)
                dve.wait_ge(s_ep, 3)
                nc.vector.tensor_copy(ep_part[:, 1], ep_rest[:]).then_inc(s_ep, 1)
                dve.wait_ge(s_ep, 4)
                nc.vector.tensor_tensor(ep_part[:, 2], ep_rest[:], ep_part[:, 1], ALU.subtract).then_inc(s_ep, 1)

            @block.scalar
            def _(act):
                for g in range(3):
                    for b in range(B):
                        act.wait_ge(s_xgp, g * B + b + 1)
                        nc.scalar.activation(xg[:, :, g, b], bank[2 + g * B + b], ACT.Identity, bias=b_col[:, g:g + 1]).then_inc(s_xg, 1)

            @block.tensor
            def _(pe):
                pe.wait_ge(s_ld, 16 * 5)
                for g in range(3):
                    for b in range(B):
                        nc.tensor.matmul(bank[2 + g * B + b], wi[:, 0, g, :], xT[:, b, :], start=True, stop=True).then_inc(s_xgp, 1)
                nc.tensor.matmul(bank[0][:, 0:B * S], w_att[:, 1, :], ctxT[:], start=True, stop=True).then_inc(s_epp, 1)
                pe.wait_ge(s_xg, 3 * B)
                for g in range(3):
                    nc.tensor.matmul(EW_ps[:, g, :, :], wi[:, 1, g, :], ctxT[:], start=True, stop=True)

        s_hw, s_tanh, s_score, s_max, s_exp = (sems("gru_" + x) for x in ("hw", "tanh", "score", "max", "exp"))
        s_raw, s_gate, s_tzr, s_zh, s_hh = (sems("gru_" + x) for x in ("raw", "gate", "tzr", "zh", "hh"))
        s_uh, s_high, s_rest, s_middle, s_part = (sem("gru_" + x) for x in ("uh", "high", "rest", "middle", "parts"))
        s_pre, s_cand, s_kept = (sem("gru_" + x) for x in ("pre", "candidate", "kept"))

        with nc.Block() as block:
            @block.tensor
            def _(pe):
                mm = nc.tensor.matmul

                def keep_warm(n):
                    for _ in range(n):
                        mm(bank[6][:, 0:3 * D], ident_b[:], uh_part[:, 0], start=True, stop=True)

                def step(t, u):
                    h = state_of(u - 1)
                    for b in range(B):
                        pe.wait_ge(s_h[b], t + 1)
                        mm(HW_ps[b], w_att[:, 0, :], h[:, b:b + 1].to_broadcast([P, S]), start=False, stop=True,
                           skip_group_check=True).then_inc(s_hw[b], 1)
                    keep_warm(WARM[0])
                    for b in range(B):
                        pe.wait_ge(s_tanh[b], t + 1)
                        mm(S_ps[b], v_b[:], tanh_s[:, b, :], start=True, stop=True).then_inc(s_score[b], 1)
                    pe.wait_ge(s_part, t + 1)
                    for g in range(3):
                        for n, (i, j) in enumerate(PRODUCTS):
                            last = mm(U_ps[:, g, :], uh_part[:, i, g, :], h_part[:, j, :], start=(n == 0), stop=(n == len(PRODUCTS) - 1))
                    last.then_inc(s_uh, 1)
                    attended_context()
                    keep_warm(WARM[1])

                def attended_context():
                    for b in range(B):
                        for j in range(3):
                            mm(HW_ps[b], ident_b[:], ep_part[:, j, b, :], start=(j == 0), stop=False, skip_group_check=True)

                attended_context()
                with pe.Fori(0, T // UNROLL) as i:
                    for u in range(UNROLL):
                        step(i * UNROLL + u, u)
                for b in range(B):
                    mm(HW_ps[b], k.zeros[:, 0:P], k.zeros[:, 0:S], start=False, stop=True, skip_group_check=True)

            @block.scalar
            def _(act):
                av = nc.scalar.activation

                def step(t, u):
                    for b in range(B):
                        act.wait_ge(s_hw[b], t + 1)
                        av(tanh_s[:, b, :], HW_ps[b], ACT.Tanh).then_inc(s_tanh[b], 1)
                    for b in range(B):
                        act.wait_ge(s_max[b], t + 1)
                        av(exp_s[:, b, :], S_ps[b], ACT.Exp, bias=negmax[:, b:b + 1], accum_out=esum[:, b:b + 1]).then_inc(s_exp[b], 1)
                    act.wait_ge(s_pre, t + 1)
                    av(cand[:], U_ps[:, 2, :], ACT.Copy).then_inc(s_cand, 1)
                    for b in range(B):
                        act.wait_ge(s_gate[b], t + 1)
                        av(tzr[:, :, b], gate[:, 0:2, b], ACT.Tanh, scale=0.5).then_inc(s_tzr[b], 1)
                        act.wait_ge(s_cand, t + 1)
                        act.wait_ge(s_tzr[b], t + 1)
                        av(hh[:, b:b + 1], tzr[:, 1, b:b + 1], ACT.Tanh, scale=cand[:, b:b + 1], bias=gate[:, 2, b:b + 1]).then_inc(s_hh[b], 1)

                with act.Fori(0, T // UNROLL) as i:
                    for u in range(UNROLL):
                        step(i * UNROLL + u, u)

            @block.gpsimd
            def _(pool):
                nc.gpsimd.memset(free[:], 0.0).then_inc(s_kept, 2)
                fold_butterfly(k, pool, ctx, 1)
                with pool.Fori(0, T // UNROLL) as i:
                    for u in range(UNROLL):
                        if (u + 1) % HALF == 0:
                            pool.wait_ge(s_h[0], i * UNROLL + u + 2)
                            pool.wait_ge(s_h[1], i * UNROLL + u + 2)
                            nc.gpsimd.tensor_copy(hT[:, bass.ds(i * UNROLL + (u + 1 - HALF), HALF), :],
                                                  ring[:, u + 1 - HALF:u + 1, :]).then_inc(s_kept, 1)

            @block.vector
            def _(dve):
                v = nc.vector

                def weigh(t, b, gates):
                    for g in gates:
                        last = v.tensor_tensor_reduce(junk[:, g, b, :], exp_s[:, b, :], EW_ps[:, g, b, :], 1.0, 0.0,
                                                      ALU.mult, ALU.add, raw[:, g, b:b + 1])
                    return last

                def gates_in(t, b):
                    dve.wait_ge(s_raw[b], t + 1)
                    v.scalar_tensor_tensor(out=gate[:, :, b], in0=raw[:, :, b], scalar=erec[:, b:b + 1], in1=pre[:, :, b],
                                           op0=ALU.mult, op1=ALU.add).then_inc(s_gate[b], 1)

                def update_gate(t, b):
                    dve.wait_ge(s_tzr[b], t + 1)
                    v.scalar_tensor_tensor(out=zh[:, b:b + 1], in0=tzr[:, 0, b:b + 1], scalar=1.0, in1=h_half[:, b:b + 1],
                                           op0=ALU.add, op1=ALU.mult)
                    v.tensor_scalar(omz[:, b:b + 1], tzr[:, 0, b:b + 1], -0.5, 0.5, ALU.mult, ALU.add).then_inc(s_zh[b], 1)

                def state(t, u, b):
                    dve.wait_ge(s_zh[b], t + 1)
                    dve.wait_ge(s_hh[b], t + 1)
                    v.scalar_tensor_tensor(out=state_of(u)[:, b:b + 1], in0=hh[:, b:b + 1], scalar=omz[:, b:b + 1], in1=zh[:, b:b + 1],
                                           op0=ALU.mult, op1=ALU.add).then_inc(s_h[b], 1)

                def step(t, u):
                    h = state_of(u - 1)
                    dve.wait_ge(s_h[1], t + 1)
                    v.tensor_scalar(h_part[:, 0, :], h, 1.0, None, ALU.mult).then_inc(s_high, 1)
                    v.tensor_scalar(h_half[:], h, 0.5, None, ALU.mult)
                    dve.wait_ge(s_high, t + 1)
                    v.tensor_tensor(h_rest[:], h, h_part[:, 0, :], ALU.subtract).then_inc(s_rest, 1)
                    dve.wait_ge(s_rest, t + 1)
                    v.tensor_copy(h_part[:, 1, :], h_rest[:]).then_inc(s_middle, 1)
                    dve.wait_ge(s_middle, t + 1)
                    v.tensor_tensor(h_part[:, 2, :], h_rest[:], h_part[:, 1, :], ALU.subtract).then_inc(s_part, 1)
                    for b in range(B):
                        dve.wait_ge(s_score[b], t + 1)
                        v.tensor_reduce(negmax[:, b:b + 1], S_ps[b], AX.X, ALU.max, negate=True).then_inc(s_max[b], 1)
                    dve.wait_ge(s_exp[0], t + 1)
                    v.reciprocal(erec[:, 0:1], esum[:, 0:1])
                    weigh(t, 0, (0, 1, 2)).then_inc(s_raw[0], 1)
                    dve.wait_ge(s_uh, t + 1)
                    v.tensor_tensor(pre[:], U_ps, xg[:, t, :, :], ALU.add).then_inc(s_pre, 1)
                    dve.wait_ge(s_exp[1], t + 1)
                    weigh(t, 1, (0,))
                    dve.wait_ge(s_pre, t + 1)
                    gates_in(t, 0)
                    v.reciprocal(erec[:, 1:2], esum[:, 1:2])
                    weigh(t, 1, (1, 2)).then_inc(s_raw[1], 1)
                    gates_in(t, 1)
                    update_gate(t, 0)
                    state(t, u, 0)
                    update_gate(t, 1)
                    state(t, u, 1)

                with dve.Fori(0, T // UNROLL) as i:
                    for u in range(UNROLL):
                        if u % HALF == 0:
                            dve.wait_ge(s_kept, 2 * i + u // HALF + 1)
                        step(i * UNROLL + u, u)


def fold_butterfly(k, pool, ctx, d):
    nc, w = k.nc, k.w
    F = 4 * D
    STAGES = 9
    wt = k.sb(ctx, "fly_w", [P, 2, 4, F // 2])
    y = k.sb(ctx, "fly_y", [P, 2, 2, F])
    prod = k.sb(ctx, "fly_products", [P, 4, 2, F // 2])
    load_c, step_c = k.count("fly_loads"), k.count("fly_step")

    done = 0
    rows, src = ((2, "l1f_w_exp"), (1, "l1f_w_conT"))[d]
    pool.dma_start(y[:, 0, 0, :], w[src]).then_inc(load_c.sem, 16)
    done += 16
    if rows == 2:
        pool.dma_start(y[:, 0, 1, :], w["l1f_b_exp"].to_broadcast([P, F])).then_inc(load_c.sem, 16)
        done += 16
    for n in range(STAGES):
        g = n if d == 0 else STAGES - 1 - n
        s = 2 ** g
        pool.dma_start(wt[:, n % 2, :, :].rearrange("p c i -> p (c i)"),
                       w["l1f_fly"][d, g:g + 1, :].to_broadcast([P, 2 * F])).then_inc(load_c.sem, 16)
        done += 16
        pool.wait_ge(load_c.sem, load_c.at + done)

        def pairs(buf, side):
            v = y[:, buf, 0:rows, :].rearrange("p r (n c s) -> p r n c s", c=2, s=s)
            return v[:, :, :, side, :]

        for r in range(rows):
            for c in range(4):
                o, i = c // 2, c % 2
                wc = wt[:, n % 2, 2 * o + i if d == 0 else 2 * i + o, :].rearrange("p (n s) -> p n s", s=s)
                nc.gpsimd.tensor_tensor(prod[:, c, r, :].rearrange("p (n s) -> p n s", s=s), pairs(n % 2, i)[:, r], wc,
                                        ALU.mult).then_inc(step_c.sem, 1)
                step_c.at += 1
        pool.wait_ge(step_c.sem, step_c.at)
        for r in range(rows):
            for o in range(2):
                nc.gpsimd.tensor_tensor(pairs((n + 1) % 2, o)[:, r],
                                        prod[:, 2 * o, r, :].rearrange("p (n s) -> p n s", s=s),
                                        prod[:, 2 * o + 1, r, :].rearrange("p (n s) -> p n s", s=s),
                                        ALU.add).then_inc(step_c.sem, 1)
                step_c.at += 1
        pool.wait_ge(step_c.sem, step_c.at)
    out = k.fly_up if d == 0 else k.fly_downT
    nc.gpsimd.tensor_copy(out[:, 0:rows, :], y[:, STAGES % 2, 0:rows, :]).then_inc(step_c.sem, 1)
    step_c.at += 1
    pool.wait_ge(step_c.sem, step_c.at)
    load_c.at += done


def fold_ends(k):
    nc = k.nc
    with ExitStack() as ctx:
        down = k.sb(ctx, "fly_down", [P, 4, D])
        ps_c, sb_c, st_c = k.count("fold_psum"), k.count("fold_sbuf"), k.count("fold_stored")
        with nc.Block() as block:
            @block.tensor
            def _(pe):
                for f in range(4):
                    nc.tensor.transpose(k.bank[0][:, f * P:(f + 1) * P], k.fly_downT[:, 0, f * P:(f + 1) * P], k.ident[:])
                for f in range(4):
                    last = nc.tensor.matmul(k.bank[1][:, f:f + 1], k.fly_up[0:1, 1, f * P:(f + 1) * P], k.ones[0:1, 0:1],
                                            start=True, stop=True)
                last.then_inc(ps_c.sem, 1)

            @block.vector
            def _(dve):
                dve.wait_ge(ps_c.sem, ps_c.at + 1)
                nc.vector.tensor_copy(down[:].rearrange("p f d -> p (f d)"), k.bank[0]).then_inc(sb_c.sem, 1)
                nc.vector.tensor_tensor(k.fly_bias[:], k.bank[1][:, 0:4], k.cols["l1f_up_bias"], ALU.add).then_inc(sb_c.sem, 1)

            @block.sync
            def _(sp):
                sp.dma_start(k.d_fly_up[0], k.fly_up[:, 0, :]).then_inc(st_c.sem, 16)
                sp.wait_ge(sb_c.sem, sb_c.at + 2)
                sp.dma_start(k.d_fly_down[0].rearrange("f p d -> p f d"), down[:]).then_inc(st_c.sem, 16)
                sp.wait_ge(st_c.sem, st_c.at + 32)
        ps_c.at += 1
        sb_c.at += 2
        st_c.at += 32


def router(k, x_T, w_r, E, top, over_all, comb, comb_T=None):
    nc = k.nc
    tri = k.tri[:].rearrange("p (e j) -> p e j", e=16)[:, 0:E, 0:E]
    link = chain(k, "router_step")
    psum_c, exp_c, comb_c, back_c, turned_c, sb_c, st_c = (k.count("router_" + x) for x in ("psum", "exp", "comb", "sub", "turned", "sbuf",
                                                                                             "stored"))
    with ExitStack() as ctx:
        lg = k.sb(ctx, "router_logits", [P, NT, E])
        d_s = k.sb(ctx, "router_shifted", [P, NT, E])
        ex = k.sb(ctx, "router_exp", [P, NT, E])
        gt = k.sb(ctx, "router_gt", [P, NT, E, E])
        ge = k.sb(ctx, "router_ge", [P, NT, E, E])
        m = k.sb(ctx, "router_max", [P, NT])
        z = k.sb(ctx, "router_sum", [P, NT])
        zr = k.sb(ctx, "router_recip", [P, NT])
        rank = k.sb(ctx, "router_rank", [P, NT, E])
        cT = comb_T if comb_T is not None else k.sb(ctx, "router_comb_T", [P, B * T])
        with nc.Block() as block:
            @block.tensor
            def _(pe):
                for j in range(NT):
                    last = nc.tensor.matmul(k.bank[0][:, j * E:(j + 1) * E], x_T[:, j * P:(j + 1) * P], w_r, start=True, stop=True)
                last.then_inc(psum_c.sem, 1)
                pe.wait_ge(comb_c.sem, comb_c.at + 1)
                for j in range(NT):
                    last = nc.tensor.transpose(k.bank[1 + j // TB][0:E, (j % TB) * P:(j % TB + 1) * P], ex[:, j, :], k.ident[:])
                last.then_inc(turned_c.sem, 1)

            @block.vector
            def _(dve):
                v = nc.vector

                def wide(a):
                    return a.unsqueeze(2).to_broadcast([P, NT, E])

                dve.wait_ge(psum_c.sem, psum_c.at + 1)
                link(dve, v.tensor_copy(lg[:].rearrange("p t e -> p (t e)"), k.bank[0][:, 0:NT * E]))
                link(dve, v.tensor_reduce(m[:], lg[:], AX.X, ALU.max))
                v.tensor_tensor(d_s[:], lg[:], wide(m[:]), ALU.subtract).then_inc(back_c.sem, 1)
                dve.wait_ge(exp_c.sem, exp_c.at + 1)
                ranked = lg
                if over_all:
                    link(dve, v.tensor_reduce(z[:], ex[:], AX.X, ALU.add))
                    link(dve, v.reciprocal(zr[:], z[:]))
                    link(dve, v.tensor_tensor(ex[:], ex[:], wide(zr[:]), ALU.mult))
                    ranked = ex
                for t in range(NT):
                    other = ranked[:, t, :].unsqueeze(1).to_broadcast([P, E, E])
                    own = ranked[:, t, :].unsqueeze(2).to_broadcast([P, E, E])
                    v.tensor_tensor(gt[:, t], other, own, ALU.is_gt)
                    last = v.tensor_tensor(ge[:, t], other, own, ALU.is_ge)
                link(dve, last)
                for t in range(NT):
                    last = v.tensor_tensor(ge[:, t], ge[:, t], tri, ALU.mult)
                link(dve, last)
                for t in range(NT):
                    last = v.tensor_tensor(gt[:, t], gt[:, t], ge[:, t], ALU.max)
                link(dve, last)
                for t in range(NT):
                    last = v.tensor_reduce(rank[:, t, :], gt[:, t], AX.X, ALU.add)
                link(dve, last)
                link(dve, v.tensor_scalar(rank[:], rank[:], float(top), None, ALU.is_lt))
                link(dve, v.tensor_tensor(ex[:], ex[:], rank[:], ALU.mult))
                link(dve, v.tensor_reduce(z[:], ex[:], AX.X, ALU.add))
                if over_all:
                    link(dve, v.tensor_scalar(z[:], z[:], 1e-12, None, ALU.max))
                link(dve, v.reciprocal(zr[:], z[:]))
                v.tensor_tensor(ex[:], ex[:], wide(zr[:]), ALU.mult).then_inc(comb_c.sem, 1)
                dve.wait_ge(turned_c.sem, turned_c.at + 1)
                for b in range(B):
                    v.tensor_copy(cT[0:E, b * T:(b + 1) * T], k.bank[1 + b][0:E, :]).then_inc(sb_c.sem, 1)

            @block.scalar
            def _(act):
                act.wait_ge(back_c.sem, back_c.at + 1)
                nc.scalar.activation(ex[:], d_s[:], ACT.Exp).then_inc(exp_c.sem, 1)

            @block.sync
            def _(sp):
                sp.wait_ge(sb_c.sem, sb_c.at + B)
                sp.dma_start(comb, cT[0:E, :]).then_inc(st_c.sem, 16)
                sp.wait_ge(st_c.sem, st_c.at + 16)
    for c, n in ((psum_c, 1), (exp_c, 1), (comb_c, 1), (back_c, 1), (turned_c, 1), (sb_c, B), (st_c, 16)):
        c.at += n


def project(k, x_T, weight, out, func=ACT.Identity, bias=0.0, scale=1.0):
    nc = k.nc
    ps_c, out_c = k.count("project_psum"), k.count("project_out")
    with nc.Block() as block:
        @block.tensor
        def _(pe):
            for b in range(B):
                nc.tensor.matmul(k.bank[b], weight, x_T[:, b, :], start=True, stop=True).then_inc(ps_c.sem, 1)

        @block.scalar
        def _(act):
            for b in range(B):
                act.wait_ge(ps_c.sem, ps_c.at + b + 1)
                nc.scalar.activation(out[:, b, :], k.bank[b], func, bias=bias, scale=scale).then_inc(out_c.sem, 1)
    ps_c.at += B
    out_c.at += B


def slots(k):
    nc, w = k.nc, k.w
    link = chain(k, "slot_step")
    ld_c, ps_c, out_c, max_c, exp_c, att_c, upd_c = (k.count("slot_" + x) for x in ("loads", "psum", "out", "max", "exp", "att", "upd"))
    cols = k.cols
    with ExitStack() as ctx:
        ws = k.sb(ctx, "slot_w", [P, 6, D])
        rows = k.sb(ctx, "slot_rows", [P, 6, D])
        cond_r = k.sb(ctx, "slot_cond", [P, B, D])
        els = k.sb(ctx, "slot_exp", [P, D])
        sl = k.sb(ctx, "slot_slots", [P, NT, D])
        cT = k.sb(ctx, "slot_ctx_T", [P, B, S])
        kT = k.sb(ctx, "slot_k", [P, B, S])
        vt = k.sb(ctx, "slot_v", [P, B, D])
        a_T = k.sb(ctx, "slot_a", [P, B, T])
        q_T = k.sb(ctx, "slot_q", [P, B, T])
        e_s = k.sb(ctx, "slot_e", [P, B, T])
        negmax = k.sb(ctx, "slot_negmax", [P, B])
        esum = k.sb(ctx, "slot_esum", [P, B])
        crec = k.sb(ctx, "slot_crec", [P, NT])
        upd = k.sb(ctx, "slot_upd", [P, B, T])
        bq = k.sb(ctx, "slot_bq", [P, 1])
        WK, WV, WQ, WU, W1, W2 = range(6)
        BV, LS, MU, PG, PB, BU = range(6)
        root = float(D) ** 0.5

        layernorm(k, k.ctx_tok, S, B, dst_T=lambda g: cT[:, g, :], affine=[(cols["lnkv_g"], cols["lnkv_b"])] * B, group=1)
        layernorm(k, k.x_tok, P, NT, dst=sl)
        with nc.Block() as block:
            @block.sync
            def _(sp):
                sp.dma_start(ws[:], w["l2_w"]).then_inc(ld_c.sem, 16)
                sp.dma_start(rows[:].rearrange("p n d -> p (n d)"), w["l2_rows"].to_broadcast([P, 6 * D])).then_inc(ld_c.sem, 16)
                sp.dma_start(cond_r[:].rearrange("p b d -> p (b d)"), w["cond_row"].to_broadcast([P, B * D])).then_inc(ld_c.sem, 16)

            @block.scalar
            def _(act):
                act.wait_ge(ld_c.sem, ld_c.at + 48)
                nc.scalar.activation(els[:], rows[:, LS, :], ACT.Exp).then_inc(exp_c.sem, 1)
                nc.scalar.activation(bq[:], cols["l2_bq"], ACT.Copy, scale=root).then_inc(exp_c.sem, 1)
                act.wait_ge(ps_c.sem, ps_c.at + 1)
                nc.scalar.activation(kT[:].rearrange("p b s -> p (b s)"), k.bank[0][:, 0:B * S], ACT.Identity, bias=cols["l2_bk"])

            @block.tensor
            def _(pe):
                pe.wait_ge(ld_c.sem, ld_c.at + 48)
                nc.tensor.matmul(k.bank[0][:, 0:B * S], ws[:, WK, :], cT[:].rearrange("p b s -> p (b s)"), start=True,
                                 stop=True).then_inc(ps_c.sem, 1)
                for b in range(B):
                    nc.tensor.matmul(k.bank[1 + b][0:S, 0:D], cT[:, b, :], ws[:, WV, :], start=True, stop=True).then_inc(ps_c.sem, 1)

            @block.vector
            def _(dve):
                v = nc.vector
                dve.wait_ge(ld_c.sem, ld_c.at + 48)
                for b in range(B):
                    dve.wait_ge(ps_c.sem, ps_c.at + 2 + b)
                    v.tensor_tensor(vt[0:S, b, :], k.bank[1 + b][0:S, 0:D], rows[0:S, BV, :], ALU.add)
                dve.wait_ge(exp_c.sem, exp_c.at + 1)
                link(dve, v.tensor_tensor(sl[:], sl[:], els[:].unsqueeze(1).to_broadcast([P, NT, D]), ALU.mult))
                link(dve, v.tensor_tensor(sl[:], sl[:], rows[:, MU, :].unsqueeze(1).to_broadcast([P, NT, D]), ALU.add))
        ld_c.at += 48
        ps_c.at += 3
        exp_c.at += 2
        for _ in range(3):
            layernorm(k, sl, P, NT, dst_T=lambda g: a_T[:, g, :], affine=[(cols["lnq_g"], cols["lnq_b"])] * B)
            project(k, a_T, ws[:, WQ, :], q_T, bias=bq[:, 0:1], scale=root)
            with nc.Block() as block:
                @block.tensor
                def _(pe):
                    for b in range(B):
                        nc.tensor.matmul(k.bank[b][0:S, :], kT[:, b, :], q_T[:, b, :], start=True, stop=True).then_inc(ps_c.sem, 1)
                    for b in range(B):
                        pe.wait_ge(att_c.sem, att_c.at + b + 1)
                        for j in range(TB):
                            nc.tensor.matmul(k.bank[2][:, b * TB + j:b * TB + j + 1], e_s[0:S, b, j * P:(j + 1) * P], k.ones[0:S, 0:1],
                                             start=True, stop=True)
                        nc.tensor.matmul(k.bank[4 + b], vt[0:S, b, :], e_s[0:S, b, :], start=True, stop=True).then_inc(ps_c.sem, 1)
                    for b in range(B):
                        pe.wait_ge(upd_c.sem, upd_c.at + b + 1)
                        nc.tensor.matmul(k.bank[6 + b], ws[:, WU, :], upd[:, b, :], start=True, stop=True)

                @block.scalar
                def _(act):
                    for b in range(B):
                        act.wait_ge(max_c.sem, max_c.at + b + 1)
                        nc.scalar.activation(e_s[0:S, b, :], k.bank[b][0:S, :], ACT.Exp, bias=negmax[0:S, b:b + 1],
                                             accum_out=esum[0:S, b:b + 1]).then_inc(exp_c.sem, 1)

                @block.vector
                def _(dve):
                    v = nc.vector
                    v.tensor_tensor(sl[:], sl[:], rows[:, BU, :].unsqueeze(1).to_broadcast([P, NT, D]), ALU.add)
                    for b in range(B):
                        dve.wait_ge(ps_c.sem, ps_c.at + b + 1)
                        v.tensor_reduce(negmax[0:S, b:b + 1], k.bank[b][0:S, :], AX.X, ALU.max, negate=True).then_inc(max_c.sem, 1)
                    for b in range(B):
                        dve.wait_ge(exp_c.sem, exp_c.at + b + 1)
                        link(dve, v.reciprocal(esum[0:S, b:b + 1], esum[0:S, b:b + 1]))
                        v.tensor_scalar(e_s[0:S, b, :], e_s[0:S, b, :], esum[0:S, b:b + 1], 1e-8, ALU.mult, ALU.add).then_inc(att_c.sem, 1)
                    for b in range(B):
                        dve.wait_ge(ps_c.sem, ps_c.at + B + b + 1)
                        v.tensor_copy(upd[:, b, :], k.bank[4 + b]).then_inc(upd_c.sem, 1)
                    v.reciprocal(crec[:], k.bank[2][:, 0:NT])
            ps_c.at += 2 * B
            exp_c.at += B
            max_c.at += B
            att_c.at += B
            upd_c.at += B
            turn_and_add(k, k.bank[6:8], sl, scale=crec)
            layernorm(k, sl, P, NT, dst_T=lambda g: a_T[:, g, :], affine=[(cols["lnm_g"], cols["lnm_b"])] * B)
            project(k, a_T, ws[:, W1, :], q_T, func=ACT.Gelu, bias=cols["l2_b1"])
            project(k, q_T, ws[:, W2, :], upd, bias=cols["l2_b2"])
            turn_and_add(k, [upd[:, b, :] for b in range(B)], sl)
            with nc.Block() as block:
                @block.vector
                def _(dve):
                    for b in range(B):
                        nc.vector.tensor_tensor(sl[:, b * TB:(b + 1) * TB, :], sl[:, b * TB:(b + 1) * TB, :],
                                                cond_r[:, b, :].unsqueeze(1).to_broadcast([P, TB, D]), ALU.add)
            layernorm(k, sl, P, NT, dst=sl)
            with nc.Block() as block:
                @block.vector
                def _(dve):
                    v = nc.vector
                    link(dve, v.tensor_tensor(sl[:], sl[:], rows[:, PG, :].unsqueeze(1).to_broadcast([P, NT, D]), ALU.mult))
                    link(dve, v.tensor_tensor(sl[:], sl[:], rows[:, PB, :].unsqueeze(1).to_broadcast([P, NT, D]), ALU.add))
        with nc.Block() as block:
            @block.vector
            def _(dve):
                nc.vector.tensor_tensor(k.x_tok[:], k.x_tok[:], sl[:], ALU.add)


COLS = ("l1_bo1", "l1_bo2", "l1_ff_b2", "lnkv_g", "lnkv_b", "lnq_g", "lnq_b", "lnm_g", "lnm_b", "l2_bk", "l2_bq", "l2_b1",
        "l2_b2", "ln1_w", "ln1_b", "ln2_w", "ln2_b", "l1f_b_con", "l1f_down_bias")


def program(nc, w, out, stages=99):
    ctx = ExitStack()
    with ctx:
        k = Core(nc, ctx, w)
        k.x_tok = k.sb(ctx, "x_tok", [P, NT, D])
        k.y_tok = k.sb(ctx, "y_tok", [P, NT, D])
        k.y_T = k.sb(ctx, "y_T", [P, B * T])
        k.hT = k.sb(ctx, "h_T", [P, T, B])
        k.ident = k.sb(ctx, "ident", [P, P])
        k.ones = k.sb(ctx, "ones", [P, T])
        k.zeros = k.sb(ctx, "zeros", [P, P])
        k.warm = k.sb(ctx, "warm", [P, T], BF16)
        k.eps = k.sb(ctx, "eps", [P, 1])
        k.tri = k.sb(ctx, "tri", [P, 256])
        k.ctxT = k.sb(ctx, "ctx_T", [P, B, S])
        k.ctx_tok = k.sb(ctx, "ctx_tok", [P, B, D])
        k.condT = k.sb(ctx, "cond_T", [P, B])
        k.fly_up = k.sb(ctx, "fly_up", [P, 2, 4 * D])
        k.fly_downT = k.sb(ctx, "fly_downT", [P, 1, 4 * D])
        k.fly_bias = k.sb(ctx, "fly_bias", [P, 4])
        cols = k.sb(ctx, "cols", [P, len(COLS)])
        many = k.sb(ctx, "many", [P, 4 + 8 + 6])
        k.att_out = k.sb(ctx, "att_out", [P, B, T])
        att_out = [k.att_out[:, b, :] for b in range(B)]
        k.cols = {n: cols[:, i:i + 1] for i, n in enumerate(COLS)}
        k.cols["l1f_up_bias"] = many[:, 0:4]
        ff_b1, norm_b = many[:, 4:12], many[:, 12:18]
        norm_w = k.sb(ctx, "norm_w", [P, 3, 2, D])
        aff = k.sb(ctx, "adaln", [P, 3, 2, B])
        aff3 = k.sb(ctx, "l3_affine", [P, 2, B])
        con_b = k.sb(ctx, "con_b", [P, 1])
        gates = k.sb(ctx, "router_w", [P, 24])
        k.d_fly_up = nc.dram_tensor("fly_up_dram", [1, D, 4 * D], F32, kind="Internal").ap()
        k.d_fly_down = nc.dram_tensor("fly_down_dram", [1, 4, P, D], F32, kind="Internal").ap()
        d_comb2 = nc.dram_tensor("comb2_dram", [8, B * T], F32, kind="Internal").ap()
        d_comb3 = nc.dram_tensor("comb3_dram", [16, B * T], F32, kind="Internal").ap()
        ld_c, ps_c, set_c = k.count("setup_loads"), k.count("setup_psum"), k.count("setup_memory")
        link = chain(k, "setup_step")
        loads = ((k.x_tok[:], w["x"]), (k.ident[:], w["ident"]), (k.tri[:], w["tri"].to_broadcast([P, 256])), (k.ctxT[:], w["ctxT"]),
                 (k.ctx_tok[0:S], w["ctx_tok"]), (k.condT[:], w["condT"]), (cols[:], w["cols"]), (many[:], w["many"]),
                 (norm_w[:], w["norm_w"]), (gates[:], w["router_w"]))
        with nc.Block() as block:
            @block.sync
            def _(sp):
                for dst, src in loads:
                    sp.dma_start(dst, src).then_inc(ld_c.sem, 16)

            @block.gpsimd
            def _(pool):
                nc.gpsimd.memset(k.ones[:], 1.0)
                nc.gpsimd.memset(k.zeros[:], 0.0)
                nc.gpsimd.memset(k.warm[:], 1.0)

            @block.tensor
            def _(pe):
                pe.wait_ge(ld_c.sem, 16 * len(loads))
                for n in range(3):
                    for s in range(2):
                        o = (n * 2 + s) * B
                        last = nc.tensor.matmul(k.bank[0][:, o:o + B], norm_w[:, n, s, :], k.condT[:], start=True, stop=True)
                last.then_inc(ps_c.sem, 1)

            @block.vector
            def _(dve):
                v = nc.vector
                v.memset(k.eps[:], 1e-5)
                dve.wait_ge(ps_c.sem, 1)
                dve.wait_ge(ld_c.sem, 16 * len(loads))
                link(dve, v.tensor_tensor(aff[:].rearrange("p n s b -> p (n s) b"), k.bank[0][:, 0:6 * B].rearrange("p (n b) -> p n b", b=B),
                                          norm_b.unsqueeze(2).to_broadcast([P, 6, B]), ALU.add))
                link(dve, v.tensor_scalar(aff[:, :, 0, :], aff[:, :, 0, :], 1.0, None, ALU.add))
                link(dve, v.tensor_scalar(aff3[:, 0, :], k.condT[:], 1.0, None, ALU.add))
                link(dve, v.tensor_scalar(aff3[:, 1, :], aff3[:, 0, :], k.cols["ln2_b"], None, ALU.mult))
                link(dve, v.tensor_tensor(aff3[:, 1, :], aff3[:, 1, :], k.condT[:], ALU.add))
                link(dve, v.tensor_scalar(aff3[:, 0, :], aff3[:, 0, :], k.cols["ln2_w"], None, ALU.mult))
                link(dve, v.tensor_tensor(con_b[:], k.cols["l1f_b_con"], k.cols["l1f_down_bias"], ALU.add))

        def y_of(b=None):
            return lambda g: k.y_T[:, g * T:(g + 1) * T]

        y_bt = k.y_T[:].rearrange("p (b t) -> p b t", b=B)
        ones = [k.ones[0:1, :]] * B
        zero = k.zeros[0:1, 0:P]

        if stages >= 1:
            recurrence(k)
            h = [k.hT[:, :, b] for b in range(B)]
            turn_and_add(k, h, k.x_tok)
        if stages >= 2:
            layernorm(k, k.x_tok, P, NT, dst_T=y_of())
            mlp(k, k.y_T, 8, [P] * 4, w["l0_wg"], w["l0_wu"], w["l0_wd"], ACT.Silu, last=zero, last_rhs=ones,
                aside=lambda pool, ctx: fold_butterfly(k, pool, ctx, 0))
            turn_and_add(k, k.bank[4:6], k.x_tok)
        if stages >= 3:
            def adaptive(n):
                return [(aff[:, n, 0, b:b + 1], aff[:, n, 1, b:b + 1]) for b in range(B)]
            layernorm(k, k.x_tok, P, NT, dst=k.y_tok)
            layernorm(k, k.y_tok, P, NT, dst_T=y_of(), affine=adaptive(0))
            attention(k, y_bt, y_bt, T, w["a1_wq"], w["a1_wk"], w["a1_wv"], w["a1_wo"])
            turn_and_add(k, att_out, k.y_tok, bias=k.cols["l1_bo1"])
            layernorm(k, k.y_tok, P, NT, dst_T=y_of(), affine=adaptive(1))
            attention(k, y_bt, k.ctxT[:], S, w["a2_wq"], w["a2_wk"], w["a2_wv"], w["a2_wo"], warm=2)
            turn_and_add(k, att_out, k.y_tok, bias=k.cols["l1_bo2"])
            layernorm(k, k.y_tok, P, NT, dst_T=y_of(), affine=adaptive(2))
            mlp(k, k.y_T, 1, [P] * 4, w["ff_wg"], w["ff_wa"], w["ff_w2"], ACT.Gelu, gate_bias=lambda f: ff_b1[:, 4 + f:5 + f],
                up_bias=lambda f: ff_b1[:, f:f + 1], last=zero, last_rhs=ones)
            turn_and_add(k, k.bank[4:6], k.y_tok, bias=k.cols["l1_ff_b2"], dst2=k.x_tok)
        if stages >= 4:
            fold_ends(k)
            layernorm(k, k.x_tok, P, NT, dst_T=y_of())
            mlp(k, k.y_T, 1, [P] * 4, k.d_fly_up, None, k.d_fly_down, ACT.Gelu, gate_bias=lambda f: k.fly_bias[:, f:f + 1],
                last=zero, last_rhs=ones)
            turn_and_add(k, k.bank[4:6], k.x_tok, bias=con_b[:, 0:1])
        if stages >= 5:
            slots(k)
        if stages >= 6:
            layernorm(k, k.x_tok, P, NT, dst_T=y_of())
            router(k, k.y_T, gates[:, 0:8], 8, 2, False, d_comb2)
            mlp(k, k.y_T, 1, [P, 64], w["sg_gate"], w["sg_up"], w["sg_down"], ACT.Silu, last=zero, last_rhs=ones)
            turn_and_add(k, k.bank[4:6], k.x_tok)
            mlp(k, k.y_T, 8, [P, 64], w["l2_wg"], w["l2_wu"], w["l2_wd"], ACT.Silu, comb=d_comb2, last=zero, last_rhs=ones)
            turn_and_add(k, k.bank[4:6], k.x_tok)
        if stages >= 7:
            with ExitStack() as c2:
                kv = k.sb(c2, "l3_kv", [P, B, T + S])
                layernorm(k, k.x_tok, P, NT, dst=k.y_tok)
                layernorm(k, k.y_tok, P, NT, dst_T=lambda g: kv[:, g, 0:T], affine=[(aff3[:, 0, b:b + 1], aff3[:, 1, b:b + 1])
                                                                                    for b in range(B)])
                layernorm(k, k.ctx_tok, S, B, dst_T=lambda g: kv[:, g, T:T + S], affine=[(k.cols["ln1_w"], k.cols["ln1_b"])] * B,
                          group=1)
                attention(k, kv[:, :, 0:T], kv[:], T + S, w["a3_wq"], w["a3_wk"], w["a3_wv"], w["a3_wo"])
                turn_and_add(k, att_out, k.x_tok)
        if stages >= 8:
            with ExitStack() as c2:
                comb_T = k.sb(c2, "l3_comb_T", [P, B * T])
                b2 = k.sb(c2, "l3_b2", [16, D])
                layernorm(k, k.x_tok, P, NT, dst_T=y_of())
                router(k, k.y_T, gates[:, 8:24], 16, 3, True, d_comb3, comb_T)
                with nc.Block() as block:
                    @block.sync
                    def _(sp):
                        sp.dma_start(b2[:], w["l3_b2"]).then_inc(ld_c.sem, 16)
                        sp.wait_ge(ld_c.sem, 16 * len(loads) + 16)
                mlp(k, k.y_T, 16, [P] * 2, w["l3_w1"], None, w["l3_w2"], ACT.Relu,
                    gate_bias="columns", comb=d_comb3, last=b2[:], last_rhs=[comb_T[0:16, b * T:(b + 1) * T] for b in range(B)])
                turn_and_add(k, k.bank[4:6], k.x_tok)
        st_c = k.count("output_stored")
        with nc.Block() as block:
            @block.sync
            def _(sp):
                sp.dma_start(out, k.x_tok[:]).then_inc(st_c.sem, 16)
                sp.wait_ge(st_c.sem, 16)


def layouts(a):
    c = np.ascontiguousarray
    r = {
        "x": c(a["x"].reshape(NT, P, D).transpose(1, 0, 2)),
        "ident": np.eye(P, dtype=np.float32),
        "tri": np.tril(np.ones((16, 16), np.float32), -1).reshape(1, 256),
        "ctxT": c(a["ctx_1024"].transpose(2, 0, 1)),
        "ctx_tok": c(a["ctx_1024"].transpose(1, 0, 2)),
        "condT": c(a["cond_1024"].T),
        "cond_row": c(a["cond_1024"].reshape(1, B * D)),
        "l0_w_att": c(a["L0_xcond_W_att"].reshape(2, P, D).transpose(1, 0, 2)),
        "l0_v": a["L0_xcond_V_att"],
        "l0_wi": c(a["L0_xcond_Wi"].reshape(2, P, 3, D).transpose(1, 0, 2, 3)),
        "l0_uh": c(a["L0_xcond_Uh"].reshape(P, 3, D)),
        "l0_b": c(a["L0_xcond_b"].reshape(3, P).T),
        "l0_wg": a["L0_ffn_Wg"],
        "l0_wu": a["L0_ffn_Wu"],
        "l0_wd": c(a["L0_ffn_Wd"].reshape(8, 4, P, D)),
        "norm_w": c(np.stack([a[f"L1_xcond_norm{n}_w"].reshape(P, 2, D) for n in (1, 2, 3)], axis=1)),
        "ff_wa": c(a["L1_xcond_ff_w1"][None, :, 0:4 * D]),
        "ff_wg": c(a["L1_xcond_ff_w1"][None, :, 4 * D:8 * D]),
        "ff_w2": c(a["L1_xcond_ff_w2"].reshape(1, 4, P, D)),
        "l1f_w_exp": a["L1_ffn_W_exp"],
        "l1f_w_conT": c(a["L1_ffn_W_con"].T),
        "l1f_b_exp": c(a["L1_ffn_b_exp"][None]),
        "l1f_fly": c(np.stack([a["L1_ffn_up_weights"], a["L1_ffn_down_weights"]]).transpose(0, 1, 3, 4, 2).reshape(2, 9, 8 * D)),
        "l2_w": c(np.stack([a["L2_xcond_w" + n] for n in "kvqu12"], axis=1)),
        "l2_rows": c(np.concatenate([a["L2_xcond_bv"], a["L2_xcond_q_logsig"][0, 0], a["L2_xcond_q_mu"][0, 0], a["L2_xcond_lnp_g"],
                                     a["L2_xcond_lnp_b"], a["L2_xcond_bu"]])[None]),
        "l3_w1": c(np.concatenate([a["L3_ffn_W1"], a["L3_ffn_b1"].reshape(16, 2, P).transpose(0, 2, 1)], axis=2)),
        "l3_w2": c(a["L3_ffn_W2"].reshape(16, 2, P, D)),
        "l3_b2": a["L3_ffn_b2"],
        "router_w": c(np.concatenate([a["L2_ffn_gate_w"].T, a["L3_ffn_gate"]], axis=1)),
    }
    for n, (q, kk, v, o) in (("a1", [a[f"L1_xcond_attn1_w{x}"] for x in "qkvo"]), ("a2", [a[f"L1_xcond_attn2_w{x}"] for x in "qkvo"]),
                             ("a3", [a["L3_xcond_Wq"].T, a["L3_xcond_Wkv"][0:HEADS * DH].T, a["L3_xcond_Wkv"][HEADS * DH:].T,
                                     a["L3_xcond_Wo"].T])):
        r[n + "_wq"] = c(q.reshape(D, HP, P).transpose(1, 0, 2))
        r[n + "_wk"] = c(kk.reshape(D, HP, P).transpose(1, 0, 2))
        r[n + "_wv"] = c(v)
        r[n + "_wo"] = c(o.reshape(HP, P, D))
    up, down = a["L2_ffn_w_up"], a["L2_ffn_w_down"]
    r["l2_wg"] = c(up[:, 0:192].transpose(0, 2, 1))
    r["l2_wu"] = c(up[:, 192:].transpose(0, 2, 1))
    r["sg_gate"] = c(a["L2_ffn_sg_gate"].T[None])
    r["sg_up"] = c(a["L2_ffn_sg_up"].T[None])
    for n, x in (("l2_wd", down.transpose(0, 2, 1)), ("sg_down", a["L2_ffn_sg_down"].T[None])):
        padded = np.zeros((x.shape[0], 256, D), np.float32)
        padded[:, 0:192] = x
        r[n] = padded.reshape(-1, 2, P, D)
    src = {"l1_bo1": "L1_xcond_attn1_bo", "l1_bo2": "L1_xcond_attn2_bo", "l1_ff_b2": "L1_xcond_ff_b2", "l1f_b_con": "L1_ffn_b_con",
           "l1f_down_bias": "L1_ffn_down_bias"}
    for n in COLS:
        src.setdefault(n, ("L2_xcond_" + n[3:]) if n.startswith("l2_") else ("L3_xcond_" + n) if n[2] in "12" else "L2_xcond_" + n)
    r["cols"] = c(np.stack([a[src[n]] for n in COLS], axis=1))
    r["many"] = c(np.concatenate([a["L1_ffn_up_bias"].reshape(4, P).T, a["L1_xcond_ff_b1"].reshape(8, P).T]
                                 + [a[f"L1_xcond_norm{n}_b"].reshape(2, P).T for n in (1, 2, 3)], axis=1))
    return r


STAGES_RUN = 99


def kernel(**inputs):
    import concourse.bacc as bacc
    from concourse.bass_utils import run_bass_kernel_spmd as run
    arrays = {"in_" + n: v for n, v in layouts({n: np.asarray(v) for n, v in inputs.items()}).items()}
    nc = bacc.Bacc("TRN2", target_bir_lowering=False, num_devices=1)
    w = {n[3:]: nc.dram_tensor(n, v.shape, mybir.dt.from_np(v.dtype), kind="ExternalInput").ap() for n, v in arrays.items()}
    out = nc.dram_tensor("out", (P, NT, D), F32, kind="ExternalOutput").ap()
    program(nc, w, out, STAGES_RUN)
    r = run(nc, [arrays], core_ids=[0])
    return np.ascontiguousarray(r.results[0]["out"].transpose(1, 0, 2)).reshape(B, T, D)
```
